# Optimizing a Trainium2 kernel written in Bass

```python
import numpy as np
import jax
import jax.numpy as jnp

def _softmax(x, axis=-1):
    return jax.nn.softmax(x, axis=axis)

def _gelu(x):
    return jax.nn.gelu(x, approximate=True)

def _silu(x):
    return jax.nn.silu(x)

def _sigmoid(x):
    return jax.nn.sigmoid(x)

def _layernorm(x, axis=-1, eps=1e-05):
    m = jnp.mean(x, axis=axis, keepdims=True)
    v = jnp.var(x, axis=axis, keepdims=True)
    return (x - m) / jnp.sqrt(v + eps)

def _scatter_add(tgt, idx, src, axis=0):
    return tgt.at[idx].add(src)

def _segment_sum(src, seg, n):
    return jax.ops.segment_sum(src, seg, n)
kernel_name = 'mk_macaron_d4_jaxref_r8_e1a2b0'

def setup_inputs(seed: int=0):
    np.random.seed(seed)
    _w = jnp.asarray

    def _L0_attn_setup():
        import jax, jax.numpy as jnp
        import numpy as np
        B, T, D, N, R = (2, 256, 128, 16, 64)
        key = jax.random.key(seed)
        ks = jax.random.split(key, 8)
        sc = 0.02
        return {'x': jax.random.normal(ks[0], (B, T, D), jnp.float32), 'W_in': jax.random.normal(ks[1], (2 * D, D), jnp.float32) * sc, 'conv_w': jax.random.normal(ks[2], (D, 3), jnp.float32) * sc, 'W_x': jax.random.normal(ks[3], (R + 2 * N, D), jnp.float32) * sc, 'W_dt': jax.random.normal(ks[4], (D, R), jnp.float32) * sc, 'b_dt': jnp.ones((D,), jnp.float32), 'A_log': jnp.full((D, N), -2.0, jnp.float32), 'D_param': jnp.ones((D,), jnp.float32), 'W_C': jax.random.normal(ks[5], (D, N), jnp.float32) * sc, 'W_out': jax.random.normal(ks[6], (D, D), jnp.float32) * sc}
    _L0_attn_in = _L0_attn_setup()

    def _L0_ffn_setup():
        import jax, jax.numpy as jnp
        import numpy as np
        B, S, D = (4, 256, 128)
        DFF = 64
        E = 16
        TOP_K = 2
        N_SHARED = 2
        FUSED_DFF = DFF * N_SHARED
        key = jax.random.key(seed)
        ks = jax.random.split(key, 16)
        sc_d = 1.0 / np.sqrt(D)
        sc_f = 1.0 / np.sqrt(DFF)
        sc_sf = 1.0 / np.sqrt(FUSED_DFF)
        inp = {'x': jax.random.normal(ks[0], (B, S, D), dtype=jnp.float32), 'gate_w': jax.random.uniform(ks[1], (E, D), dtype=jnp.float32, minval=-sc_d, maxval=sc_d), 'expert_bias': jnp.zeros((E,), dtype=jnp.float32), 'w1': jax.random.uniform(ks[2], (E, DFF, D), dtype=jnp.float32, minval=-sc_d, maxval=sc_d), 'b1': jax.random.uniform(ks[3], (E, DFF), dtype=jnp.float32, minval=-sc_d, maxval=sc_d), 'w3': jax.random.uniform(ks[4], (E, DFF, D), dtype=jnp.float32, minval=-sc_d, maxval=sc_d), 'b3': jax.random.uniform(ks[5], (E, DFF), dtype=jnp.float32, minval=-sc_d, maxval=sc_d), 'w2': jax.random.uniform(ks[6], (E, D, DFF), dtype=jnp.float32, minval=-sc_f, maxval=sc_f), 'b2': jax.random.uniform(ks[7], (E, D), dtype=jnp.float32, minval=-sc_f, maxval=sc_f), 'sw1': jax.random.uniform(ks[8], (FUSED_DFF, D), dtype=jnp.float32, minval=-sc_d, maxval=sc_d), 'sb1': jax.random.uniform(ks[9], (FUSED_DFF,), dtype=jnp.float32, minval=-sc_d, maxval=sc_d), 'sw3': jax.random.uniform(ks[10], (FUSED_DFF, D), dtype=jnp.float32, minval=-sc_d, maxval=sc_d), 'sb3': jax.random.uniform(ks[11], (FUSED_DFF,), dtype=jnp.float32, minval=-sc_d, maxval=sc_d), 'sw2': jax.random.uniform(ks[12], (D, FUSED_DFF), dtype=jnp.float32, minval=-sc_sf, maxval=sc_sf), 'sb2': jax.random.uniform(ks[13], (D,), dtype=jnp.float32, minval=-sc_sf, maxval=sc_sf)}
        return inp
    _L0_ffn_in = _L0_ffn_setup()

    def _L1_attn_setup():
        import jax, jax.numpy as jnp
        import numpy as np
        B, L, D = (2, 256, 128)
        K, M, A = (32, 4, 4)
        H = D // K
        CK = 4
        TOTAL = 2 * D + K

        def _glorot(k, shape):
            lim = np.sqrt(6.0 / (shape[0] + shape[1]))
            return jax.random.uniform(k, shape, jnp.float32, -lim, lim)
        key = jax.random.key(seed)
        ks = jax.random.split(key, 8)
        grid = np.linspace(-np.pi / 3, np.pi / 3, M, dtype=np.float32)
        theta = np.tile(grid.reshape(1, 1, 1, 1, M), (1, 1, K, H, 1)).astype(np.float32)
        dr = np.geomspace(0.001, 0.1, K - A).astype(np.float32)
        ar = np.geomspace(0.01, 0.1, A).astype(np.float32)
        return {'x': jax.random.normal(ks[0], (B, L, D), jnp.float32), 'in_proj_w': _glorot(ks[1], (D, TOTAL)), 'conv_w': jax.random.normal(ks[2], (CK, 1, TOTAL), jnp.float32) * 0.1, 'conv_b': jnp.zeros((TOTAL,), jnp.float32), 'theta': jnp.asarray(theta), 'decay_slopes': jnp.asarray(np.log(np.exp(dr) - 1.0)), 'anchor_slopes': jnp.asarray(np.log(np.exp(ar) - 1.0)), 'score_scale': jnp.ones((K,), jnp.float32), 'deriv_logits': jnp.asarray([5.0, 0.0, 0.0], jnp.float32), 'norm_scale': jnp.ones((2 * H * M,), jnp.float32), 'W_re': _glorot(ks[3], (H * M, H)), 'W_im': _glorot(ks[4], (H * M, H)), 'out_proj_w': _glorot(ks[5], (D, D))}
    _L1_attn_in = _L1_attn_setup()

    def _L1_ffn_setup():
        import jax, jax.numpy as jnp
        import numpy as np
        D = 128
        E = 12
        HS = 2 * D
        HR = 3 * D
        TAU = 1.5

        def _geglu(h):
            a, g = jnp.split(h, 2, axis=-1)
            return a * jax.nn.gelu(g, approximate=False)
        key = jax.random.key(seed)
        ks = jax.random.split(key, 12)

        def xavier(k, shape):
            fan_in, fan_out = (shape[-2], shape[-1])
            lim = jnp.sqrt(6.0 / (fan_in + fan_out))
            return jax.random.uniform(k, shape, jnp.float32, -lim, lim)
        x = jax.random.normal(ks[0], (2, 128, D), jnp.float32)
        Ws1 = xavier(ks[1], (D, 2 * HS))
        bs1 = jnp.zeros((2 * HS,), jnp.float32)
        Ws2 = xavier(ks[2], (HS, D))
        bs2 = jnp.zeros((D,), jnp.float32)
        We1 = xavier(ks[3], (E, D, 2 * HR))
        be1 = jnp.zeros((E, 2 * HR), jnp.float32)
        We2 = xavier(ks[4], (E, HR, D))
        be2 = jnp.zeros((E, D), jnp.float32)
        Wr = xavier(ks[5], (D, E))
        br = jnp.zeros((E,), jnp.float32)
        return {'x': x, 'Ws1': Ws1, 'bs1': bs1, 'Ws2': Ws2, 'bs2': bs2, 'We1': We1, 'be1': be1, 'We2': We2, 'be2': be2, 'Wr': Wr, 'br': br}
    _L1_ffn_in = _L1_ffn_setup()

    def _L2_attn_setup():
        import jax, jax.numpy as jnp
        import numpy as np
        import math
        B, N, E, D = (4, 1024, 128, 64)
        key = jax.random.key(seed)
        kx, kq, kk, kv, ko = jax.random.split(key, 5)
        x = jax.random.normal(kx, (B, N, E), dtype=jnp.float32)
        wq = jnp.sign(jax.random.normal(kq, (D, E), dtype=jnp.float32)) / math.sqrt(E)
        wk = jnp.sign(jax.random.normal(kk, (D, E), dtype=jnp.float32)) / math.sqrt(E)
        wv = jnp.sign(jax.random.normal(kv, (D, E), dtype=jnp.float32)) / math.sqrt(E)
        wo = jnp.sign(jax.random.normal(ko, (E, D), dtype=jnp.float32)) / math.sqrt(D)
        return {'x': x, 'wq': wq, 'wk': wk, 'wv': wv, 'wo': wo}
    _L2_attn_in = _L2_attn_setup()

    def _L2_ffn_setup():
        import jax, jax.numpy as jnp
        import numpy as np
        B, S = (4, 64)
        H = 128
        I = 352
        E = 8
        K = 2
        IS = 176
        key = jax.random.key(seed)
        ks = jax.random.split(key, 8)

        def init(k, shape, fan_in):
            return (jax.random.normal(k, shape, jnp.float32) / np.sqrt(fan_in)).astype(jnp.float32)
        return {'hidden_states': jax.random.normal(ks[0], (B, S, H), jnp.float32), 'gate_w': init(ks[1], (H, E), H), 'Wg': init(ks[2], (E, H, I), H), 'Wu': init(ks[3], (E, H, I), H), 'Wd': init(ks[4], (E, I, H), I), 'Sg': init(ks[5], (H, IS), H), 'Su': init(ks[6], (H, IS), H), 'Sd': init(ks[7], (IS, H), IS)}
    _L2_ffn_in = _L2_ffn_setup()

    def _L3_attn_setup():
        import jax, jax.numpy as jnp
        import numpy as np
        B, T, C = (8, 256, 128)
        EPS_LN = 1e-05
        EPS_WKV = 1e-08

        def layer_norm(x, g, b):
            mu = jnp.mean(x, axis=-1, keepdims=True)
            var = jnp.var(x, axis=-1, keepdims=True)
            return (x - mu) * jax.lax.rsqrt(var + EPS_LN) * g + b

        def time_shift(x, ratio):
            x_prev = jnp.pad(x[:, :-1, :], ((0, 0), (1, 0), (0, 0)))
            return x * ratio + x_prev * (1.0 - ratio)

        def wkv(w, u, k, v):
            kT = jnp.swapaxes(k, 0, 1)
            vT = jnp.swapaxes(v, 0, 1)
            aa0 = jnp.zeros((k.shape[0], k.shape[2]), k.dtype)
            ninf = jnp.full_like(aa0, -jnp.inf)

            def step(carry, kv):
                aa, bb, pp = carry
                kk, vv = kv
                ww = u + kk
                p = jnp.maximum(pp, ww)
                e1 = jnp.exp(pp - p)
                e2 = jnp.exp(ww - p)
                out = (e1 * aa + e2 * vv) / (e1 + e2 + EPS_WKV)
                bb_new = w + pp
                p2 = jnp.maximum(pp, kk)
                e1b = jnp.exp(pp - p2)
                e2b = jnp.exp(kk - p2)
                aa_new = e1b * aa + e2b * vv
                pp_new = p2 + jnp.log(e1b + e2b + EPS_WKV)
                return ((aa_new, bb_new, pp_new), out)
            (aa, bb, pp), outT = jax.lax.scan(step, (aa0, ninf, ninf), (kT, vT))
            output = jnp.swapaxes(outT, 0, 1)
            final_state = jnp.stack([aa, bb, pp], axis=2)
            return (output, final_state)

        def _reference_tuple_inner(x, time_decay, time_first, Wk_t, Wv_t, Wr_t, Wk_c, Wv_c, Wr_c, ln1_g, ln1_b, ln2_g, ln2_b, mix_k, mix_v, mix_r, cmix_k, cmix_r):
            h = layer_norm(x, ln1_g, ln1_b)
            k = time_shift(h, mix_k) @ Wk_t.T
            v = time_shift(h, mix_v) @ Wv_t.T
            r = jax.nn.sigmoid(time_shift(h, mix_r) @ Wr_t.T)
            w = -jnp.exp(time_decay)
            wkv_out, new_state = wkv(w, time_first, k, v)
            x = x + r * wkv_out
            h2 = layer_norm(x, ln2_g, ln2_b)
            kc = time_shift(h2, cmix_k) @ Wk_c.T
            rc = jax.nn.sigmoid(time_shift(h2, cmix_r) @ Wr_c.T)
            vv = jnp.square(jax.nn.relu(kc)) @ Wv_c.T
            x = x + rc * vv
            return (x, new_state)
        key = jax.random.key(seed)
        ks = jax.random.split(key, 16)
        s = 1.0 / np.sqrt(C)
        inp = {'x': jax.random.normal(ks[0], (B, T, C), jnp.float32), 'time_decay': jax.random.normal(ks[1], (C,), jnp.float32), 'time_first': jax.random.normal(ks[2], (C,), jnp.float32), 'Wk_t': jax.random.normal(ks[3], (C, C), jnp.float32) * s, 'Wv_t': jax.random.normal(ks[4], (C, C), jnp.float32) * s, 'Wr_t': jax.random.normal(ks[5], (C, C), jnp.float32) * s, 'Wk_c': jax.random.normal(ks[6], (4 * C, C), jnp.float32) * s, 'Wv_c': jax.random.normal(ks[7], (C, 4 * C), jnp.float32) * (0.5 * s), 'Wr_c': jax.random.normal(ks[8], (C, C), jnp.float32) * s, 'ln1_g': jnp.ones((C,), jnp.float32), 'ln1_b': jnp.zeros((C,), jnp.float32), 'ln2_g': jnp.ones((C,), jnp.float32), 'ln2_b': jnp.zeros((C,), jnp.float32), 'mix_k': jnp.ones((C,), jnp.float32), 'mix_v': jnp.ones((C,), jnp.float32), 'mix_r': jnp.ones((C,), jnp.float32), 'cmix_k': jnp.ones((C,), jnp.float32), 'cmix_r': jnp.ones((C,), jnp.float32)}
        return inp
    _L3_attn_in = _L3_attn_setup()

    def _L3_ffn_setup():
        import jax, jax.numpy as jnp
        import numpy as np
        D_MODEL, D_FF, NUM_EXPERTS, RANK, TOP_K = (128, 512, 8, 16, 2)
        B, S = (8, 256)

        def _expert_ffn(h, wi_w, wo_w, A, Bm):
            inter = jnp.einsum('bsd,fd->bsf', h, wi_w)
            lora = jnp.einsum('bsr,fr->bsf', jnp.einsum('bsd,rd->bsr', h, A), Bm)
            inter = jax.nn.relu(inter + lora)
            return jnp.einsum('bsf,df->bsd', inter, wo_w)
        key = jax.random.key(seed)
        ks = jax.random.split(key, 8)
        hidden_states = jax.random.normal(ks[0], (B, S, D_MODEL), dtype=jnp.float32)
        wi_w = jax.random.normal(ks[1], (D_FF, D_MODEL), dtype=jnp.float32) * (1.0 / np.sqrt(D_MODEL))
        wo_w = jax.random.normal(ks[2], (D_MODEL, D_FF), dtype=jnp.float32) * (1.0 / np.sqrt(D_FF))
        lora_As = jax.random.uniform(ks[3], (NUM_EXPERTS, RANK, D_MODEL), dtype=jnp.float32, minval=-1.0, maxval=1.0) / np.sqrt(D_MODEL)
        lora_Bs = jax.random.normal(ks[4], (NUM_EXPERTS, D_FF, RANK), dtype=jnp.float32) * 0.02
        top_k_indices = jnp.arange(TOP_K, dtype=jnp.int32)
        top_k_values = jax.random.uniform(ks[5], (TOP_K,), dtype=jnp.float32)
        return {'hidden_states': hidden_states, 'wi_w': wi_w, 'wo_w': wo_w, 'lora_As': lora_As, 'lora_Bs': lora_Bs, 'top_k_indices': top_k_indices, 'top_k_values': top_k_values}
    _L3_ffn_in = _L3_ffn_setup()
    _d = {'L0_attn_x': _L0_attn_in['x'], 'L0_attn_W_in': _L0_attn_in['W_in'], 'L0_attn_conv_w': _L0_attn_in['conv_w'], 'L0_attn_W_x': _L0_attn_in['W_x'], 'L0_attn_W_dt': _L0_attn_in['W_dt'], 'L0_attn_b_dt': _L0_attn_in['b_dt'], 'L0_attn_A_log': _L0_attn_in['A_log'], 'L0_attn_D_param': _L0_attn_in['D_param'], 'L0_attn_W_C': _L0_attn_in['W_C'], 'L0_attn_W_out': _L0_attn_in['W_out'], 'L0_ffn_gate_w': _L0_ffn_in['gate_w'], 'L0_ffn_expert_bias': _L0_ffn_in['expert_bias'], 'L0_ffn_w1': _L0_ffn_in['w1'], 'L0_ffn_b1': _L0_ffn_in['b1'], 'L0_ffn_w2': _L0_ffn_in['w2'], 'L0_ffn_b2': _L0_ffn_in['b2'], 'L0_ffn_w3': _L0_ffn_in['w3'], 'L0_ffn_b3': _L0_ffn_in['b3'], 'L0_ffn_sw1': _L0_ffn_in['sw1'], 'L0_ffn_sb1': _L0_ffn_in['sb1'], 'L0_ffn_sw2': _L0_ffn_in['sw2'], 'L0_ffn_sb2': _L0_ffn_in['sb2'], 'L0_ffn_sw3': _L0_ffn_in['sw3'], 'L0_ffn_sb3': _L0_ffn_in['sb3'], 'L1_attn_in_proj_w': _L1_attn_in['in_proj_w'], 'L1_attn_conv_w': _L1_attn_in['conv_w'], 'L1_attn_conv_b': _L1_attn_in['conv_b'], 'L1_attn_theta': _L1_attn_in['theta'], 'L1_attn_decay_slopes': _L1_attn_in['decay_slopes'], 'L1_attn_anchor_slopes': _L1_attn_in['anchor_slopes'], 'L1_attn_score_scale': _L1_attn_in['score_scale'], 'L1_attn_deriv_logits': _L1_attn_in['deriv_logits'], 'L1_attn_norm_scale': _L1_attn_in['norm_scale'], 'L1_attn_W_re': _L1_attn_in['W_re'], 'L1_attn_W_im': _L1_attn_in['W_im'], 'L1_attn_out_proj_w': _L1_attn_in['out_proj_w'], 'L1_ffn_Ws1': _L1_ffn_in['Ws1'], 'L1_ffn_bs1': _L1_ffn_in['bs1'], 'L1_ffn_Ws2': _L1_ffn_in['Ws2'], 'L1_ffn_bs2': _L1_ffn_in['bs2'], 'L1_ffn_We1': _L1_ffn_in['We1'], 'L1_ffn_be1': _L1_ffn_in['be1'], 'L1_ffn_We2': _L1_ffn_in['We2'], 'L1_ffn_be2': _L1_ffn_in['be2'], 'L1_ffn_Wr': _L1_ffn_in['Wr'], 'L1_ffn_br': _L1_ffn_in['br'], 'L2_attn_wq': _L2_attn_in['wq'], 'L2_attn_wk': _L2_attn_in['wk'], 'L2_attn_wv': _L2_attn_in['wv'], 'L2_attn_wo': _L2_attn_in['wo'], 'L2_ffn_gate_w': _L2_ffn_in['gate_w'], 'L2_ffn_Wg': _L2_ffn_in['Wg'], 'L2_ffn_Wu': _L2_ffn_in['Wu'], 'L2_ffn_Wd': _L2_ffn_in['Wd'], 'L2_ffn_Sg': _L2_ffn_in['Sg'], 'L2_ffn_Su': _L2_ffn_in['Su'], 'L2_ffn_Sd': _L2_ffn_in['Sd'], 'L3_attn_time_decay': _L3_attn_in['time_decay'], 'L3_attn_time_first': _L3_attn_in['time_first'], 'L3_attn_Wk_t': _L3_attn_in['Wk_t'], 'L3_attn_Wv_t': _L3_attn_in['Wv_t'], 'L3_attn_Wr_t': _L3_attn_in['Wr_t'], 'L3_attn_Wk_c': _L3_attn_in['Wk_c'], 'L3_attn_Wv_c': _L3_attn_in['Wv_c'], 'L3_attn_Wr_c': _L3_attn_in['Wr_c'], 'L3_attn_ln1_g': _L3_attn_in['ln1_g'], 'L3_attn_ln1_b': _L3_attn_in['ln1_b'], 'L3_attn_ln2_g': _L3_attn_in['ln2_g'], 'L3_attn_ln2_b': _L3_attn_in['ln2_b'], 'L3_attn_mix_k': _L3_attn_in['mix_k'], 'L3_attn_mix_v': _L3_attn_in['mix_v'], 'L3_attn_mix_r': _L3_attn_in['mix_r'], 'L3_attn_cmix_k': _L3_attn_in['cmix_k'], 'L3_attn_cmix_r': _L3_attn_in['cmix_r'], 'L3_ffn_wi_w': _L3_ffn_in['wi_w'], 'L3_ffn_wo_w': _L3_ffn_in['wo_w'], 'L3_ffn_lora_As': _L3_ffn_in['lora_As'], 'L3_ffn_lora_Bs': _L3_ffn_in['lora_Bs'], 'L3_ffn_top_k_indices': _L3_ffn_in['top_k_indices'], 'L3_ffn_top_k_values': _L3_ffn_in['top_k_values']}
    _x0 = _d['L0_attn_x']
    _d['L0_attn_x'] = jax.random.normal(jax.random.fold_in(jax.random.key(seed), 1), (8, 512, 128), dtype=_x0.dtype)
    del _x0
    return _d

def reference(L0_attn_x, L0_attn_W_in, L0_attn_conv_w, L0_attn_W_x, L0_attn_W_dt, L0_attn_b_dt, L0_attn_A_log, L0_attn_D_param, L0_attn_W_C, L0_attn_W_out, L0_ffn_gate_w, L0_ffn_expert_bias, L0_ffn_w1, L0_ffn_b1, L0_ffn_w2, L0_ffn_b2, L0_ffn_w3, L0_ffn_b3, L0_ffn_sw1, L0_ffn_sb1, L0_ffn_sw2, L0_ffn_sb2, L0_ffn_sw3, L0_ffn_sb3, L1_attn_in_proj_w, L1_attn_conv_w, L1_attn_conv_b, L1_attn_theta, L1_attn_decay_slopes, L1_attn_anchor_slopes, L1_attn_score_scale, L1_attn_deriv_logits, L1_attn_norm_scale, L1_attn_W_re, L1_attn_W_im, L1_attn_out_proj_w, L1_ffn_Ws1, L1_ffn_bs1, L1_ffn_Ws2, L1_ffn_bs2, L1_ffn_We1, L1_ffn_be1, L1_ffn_We2, L1_ffn_be2, L1_ffn_Wr, L1_ffn_br, L2_attn_wq, L2_attn_wk, L2_attn_wv, L2_attn_wo, L2_ffn_gate_w, L2_ffn_Wg, L2_ffn_Wu, L2_ffn_Wd, L2_ffn_Sg, L2_ffn_Su, L2_ffn_Sd, L3_attn_time_decay, L3_attn_time_first, L3_attn_Wk_t, L3_attn_Wv_t, L3_attn_Wr_t, L3_attn_Wk_c, L3_attn_Wv_c, L3_attn_Wr_c, L3_attn_ln1_g, L3_attn_ln1_b, L3_attn_ln2_g, L3_attn_ln2_b, L3_attn_mix_k, L3_attn_mix_v, L3_attn_mix_r, L3_attn_cmix_k, L3_attn_cmix_r, L3_ffn_wi_w, L3_ffn_wo_w, L3_ffn_lora_As, L3_ffn_lora_Bs, L3_ffn_top_k_indices, L3_ffn_top_k_values):

    def _L0_attn_ref(x, W_in, conv_w, W_x, W_dt, b_dt, A_log, D_param, W_C, W_out):
        import jax, jax.numpy as jnp
        import numpy as np
        B, T, D, N, R = (2, 256, 128, 16, 64)
        xz = jnp.einsum('btd,ed->bte', x, W_in)
        xc, z = jnp.split(xz, 2, axis=-1)
        xp = jnp.pad(xc, ((0, 0), (1, 1), (0, 0)))
        xconv = xp[:, :-2] * conv_w[:, 0] + xp[:, 1:-1] * conv_w[:, 1] + xp[:, 2:] * conv_w[:, 2]
        xs = jax.nn.silu(xconv)
        x_dbl = jnp.einsum('btd,ed->bte', xs, W_x)
        dt_param = x_dbl[..., :R]
        Bp = x_dbl[..., R:R + N]
        Cp = x_dbl[..., R + N:]
        dt = jax.nn.softplus(dt_param @ W_dt.T + b_dt) + 1e-05
        A_disc = jnp.exp(-jnp.exp(A_log)[None, None] * dt[..., None])
        Bx = Bp[:, :, None, :] * dt[..., None] * xs[..., None]
        C = Cp @ W_C.T

        def step(s, inp):
            A_t, Bx_t = inp
            s = A_t * s + Bx_t
            return (s, s.sum(-1))
        s0 = jnp.zeros((x.shape[0], D, N), x.dtype)
        _, ssum = jax.lax.scan(step, s0, (A_disc.transpose(1, 0, 2, 3), Bx.transpose(1, 0, 2, 3)))
        ssum = ssum.transpose(1, 0, 2)
        y = C * ssum + D_param * xs
        return jnp.einsum('btd,ed->bte', y, W_out) * jax.nn.silu(z)

    def _L0_ffn_ref(x, gate_w, expert_bias, w1, b1, w2, b2, w3, b3, sw1, sb1, sw2, sb2, sw3, sb3):
        import jax, jax.numpy as jnp
        import numpy as np
        B, S, D = (4, 256, 128)
        DFF = 64
        E = 16
        TOP_K = 2
        N_SHARED = 2
        FUSED_DFF = DFF * N_SHARED
        Bv, Sv, Dv = x.shape
        xf = x.reshape(-1, Dv)
        logits = xf @ gate_w.T
        scores = jax.nn.sigmoid(logits)
        biased = logits + expert_bias.astype(logits.dtype)[None, :]
        _, topk_idx = jax.lax.top_k(biased, TOP_K)
        topk_w = jnp.take_along_axis(scores, topk_idx, axis=-1)
        topk_w = topk_w / (topk_w.sum(-1, keepdims=True) + 1e-10)
        gatew = (jax.nn.one_hot(topk_idx, E, dtype=xf.dtype) * topk_w[..., None]).sum(1)
        y = jnp.zeros_like(xf)
        for e in range(E):
            h = jax.nn.silu(xf @ w1[e].T + b1[e]) * (xf @ w3[e].T + b3[e])
            y = y + gatew[:, e:e + 1] * (h @ w2[e].T + b2[e])
        hs = jax.nn.silu(xf @ sw1.T + sb1) * (xf @ sw3.T + sb3)
        y = y + hs @ sw2.T + sb2
        return y.reshape(Bv, Sv, Dv)

    def _L1_attn_ref(x, in_proj_w, conv_w, conv_b, theta, decay_slopes, anchor_slopes, score_scale, deriv_logits, norm_scale, W_re, W_im, out_proj_w):
        import jax, jax.numpy as jnp
        import numpy as np
        B, L, D = (2, 256, 128)
        K, M, A = (32, 4, 4)
        H = D // K
        CK = 4
        TOTAL = 2 * D + K

        def _glorot(k, shape):
            lim = np.sqrt(6.0 / (shape[0] + shape[1]))
            return jax.random.uniform(k, shape, jnp.float32, -lim, lim)
        b, l, d = x.shape
        z = x @ in_proj_w
        zp = jnp.pad(z, ((0, 0), (CK - 1, 0), (0, 0)))
        z = jax.lax.conv_general_dilated(zp, conv_w, (1,), 'VALID', dimension_numbers=('NWC', 'WIO', 'NWC'), feature_group_count=TOTAL) + conv_b
        x_val = z[..., :D].reshape(b, l, K, H)
        x_gate = jax.nn.silu(z[..., D:2 * D])
        s_raw = z[..., -K:].reshape(b, l, K, 1)
        pos = jnp.arange(l, dtype=jnp.float32)
        d_slopes = jax.nn.softplus(decay_slopes).reshape(1, 1, K - A, 1)
        dist_d = jnp.maximum(jnp.float32(l - 1) - pos, 0.0)[None, :, None, None]
        w_decay = jnp.exp(-d_slopes * dist_d)
        a_slopes = jax.nn.softplus(anchor_slopes).reshape(1, 1, A, 1)
        w_anchor = jnp.exp(-a_slopes * pos[None, :, None, None])
        time_weight = jnp.concatenate([w_decay, w_anchor], axis=2)
        p = jnp.exp(jnp.clip(score_scale[None, None, :, None] * s_raw, -20.0, 20.0))
        x5 = x_val[..., None]
        phi = x5 * theta
        cos_b, sin_b = (jnp.cos(phi), jnp.sin(phi))
        w = jax.nn.softmax(deriv_logits)
        poly = w[0] + w[1] * x5 - w[2] * jnp.square(x5)
        re_m = poly * cos_b
        im_m = poly * sin_b
        p_w = (p * time_weight)[..., None]
        flat = (b, l, K * H * M)
        merged = jnp.concatenate([(p_w * re_m).reshape(flat), (p_w * im_m).reshape(flat), jnp.broadcast_to(p_w, (b, l, K, H, M)).reshape(flat)], axis=-1)
        num_re, num_im, den = jnp.split(jnp.cumsum(merged, axis=1), 3, axis=-1)
        inv_den = 1.0 / jnp.maximum(den, jnp.float32(0.0001))
        re = (num_re * inv_den).reshape(b, l, K, H * M)
        im = (num_im * inv_den).reshape(b, l, K, H * M)
        mean_sq = (jnp.sum(jnp.square(re), -1) + jnp.sum(jnp.square(im), -1)) / (2.0 * H * M)
        rs = jax.lax.rsqrt(mean_sq[..., None] + 1e-05)
        y = re * rs * norm_scale[:H * M] @ W_re + im * rs * norm_scale[H * M:] @ W_im
        y = y.reshape(b, l, D)
        return y * x_gate @ out_proj_w

    def _L1_ffn_ref(x, Ws1, bs1, Ws2, bs2, We1, be1, We2, be2, Wr, br):
        import jax, jax.numpy as jnp
        import numpy as np
        D = 128
        E = 12
        HS = 2 * D
        HR = 3 * D
        TAU = 1.5

        def _geglu(h):
            a, g = jnp.split(h, 2, axis=-1)
            return a * jax.nn.gelu(g, approximate=False)
        B, T, Dm = x.shape
        xf = x.reshape(-1, Dm)
        ys = _geglu(xf @ Ws1 + bs1) @ Ws2 + bs2
        logits = (xf @ Wr + br) / TAU
        top_val, top_idx = jax.lax.top_k(logits, 2)
        top_w = jax.nn.softmax(top_val, axis=-1)
        onehot = jax.nn.one_hot(top_idx, E, dtype=x.dtype)
        w = jnp.einsum('nke,nk->ne', onehot, top_w)
        h = jnp.einsum('nd,edh->enh', xf, We1) + be1[:, None, :]
        act = _geglu(h)
        yE = jnp.einsum('enh,ehd->end', act, We2) + be2[:, None, :]
        yr = jnp.einsum('end,ne->nd', yE, w)
        return (ys + yr).reshape(B, T, Dm)

    def _L2_attn_ref(x, wq, wk, wv, wo):
        import jax, jax.numpy as jnp
        import numpy as np
        import math
        B, N, E, D = (4, 1024, 128, 64)
        Q = jnp.einsum('bne,de->bnd', x, wq)
        K = jnp.einsum('bne,de->bnd', x, wk)
        V = jnp.einsum('bne,de->bnd', x, wv)
        energy = jnp.einsum('bnd,bne->bde', K, V)
        context = jnp.einsum('bnd,bde->bne', Q, energy)
        context = context * jnp.asarray(math.sqrt(3.0 / D), dtype=context.dtype)
        out = jnp.einsum('bnd,ed->bne', context, wo)
        return out

    def _L2_ffn_ref(hidden_states, gate_w, Wg, Wu, Wd, Sg, Su, Sd):
        import jax, jax.numpy as jnp
        import numpy as np
        B, S = (4, 64)
        H = 128
        I = 352
        E = 8
        K = 2
        IS = 176
        b, s, h = hidden_states.shape
        x = hidden_states.reshape(-1, h)
        T = x.shape[0]
        logits = x @ gate_w
        top_v, top_i = jax.lax.top_k(logits, K)
        top_p = jax.nn.softmax(top_v, axis=-1)
        combine = jnp.zeros((T, E), x.dtype).at[jnp.arange(T)[:, None], top_i].add(top_p)
        g = jnp.einsum('th,ehi->tei', x, Wg)
        u = jnp.einsum('th,ehi->tei', x, Wu)
        d = jnp.einsum('tei,eih->teh', jax.nn.silu(g) * u, Wd)
        expert_out = jnp.einsum('te,teh->th', combine, d)
        shared = jax.nn.silu(x @ Sg) * (x @ Su) @ Sd
        return (expert_out + shared).reshape(b, s, h)

    def _L3_attn_ref(x, time_decay, time_first, Wk_t, Wv_t, Wr_t, Wk_c, Wv_c, Wr_c, ln1_g, ln1_b, ln2_g, ln2_b, mix_k, mix_v, mix_r, cmix_k, cmix_r):
        import jax, jax.numpy as jnp
        import numpy as np
        B, T, C = (8, 256, 128)
        EPS_LN = 1e-05
        EPS_WKV = 1e-08

        def layer_norm(x, g, b):
            mu = jnp.mean(x, axis=-1, keepdims=True)
            var = jnp.var(x, axis=-1, keepdims=True)
            return (x - mu) * jax.lax.rsqrt(var + EPS_LN) * g + b

        def time_shift(x, ratio):
            x_prev = jnp.pad(x[:, :-1, :], ((0, 0), (1, 0), (0, 0)))
            return x * ratio + x_prev * (1.0 - ratio)

        def wkv(w, u, k, v):
            kT = jnp.swapaxes(k, 0, 1)
            vT = jnp.swapaxes(v, 0, 1)
            aa0 = jnp.zeros((k.shape[0], k.shape[2]), k.dtype)
            ninf = jnp.full_like(aa0, -jnp.inf)

            def step(carry, kv):
                aa, bb, pp = carry
                kk, vv = kv
                ww = u + kk
                p = jnp.maximum(pp, ww)
                e1 = jnp.exp(pp - p)
                e2 = jnp.exp(ww - p)
                out = (e1 * aa + e2 * vv) / (e1 + e2 + EPS_WKV)
                bb_new = w + pp
                p2 = jnp.maximum(pp, kk)
                e1b = jnp.exp(pp - p2)
                e2b = jnp.exp(kk - p2)
                aa_new = e1b * aa + e2b * vv
                pp_new = p2 + jnp.log(e1b + e2b + EPS_WKV)
                return ((aa_new, bb_new, pp_new), out)
            (aa, bb, pp), outT = jax.lax.scan(step, (aa0, ninf, ninf), (kT, vT))
            output = jnp.swapaxes(outT, 0, 1)
            final_state = jnp.stack([aa, bb, pp], axis=2)
            return (output, final_state)

        def _reference_tuple_inner(x, time_decay, time_first, Wk_t, Wv_t, Wr_t, Wk_c, Wv_c, Wr_c, ln1_g, ln1_b, ln2_g, ln2_b, mix_k, mix_v, mix_r, cmix_k, cmix_r):
            h = layer_norm(x, ln1_g, ln1_b)
            k = time_shift(h, mix_k) @ Wk_t.T
            v = time_shift(h, mix_v) @ Wv_t.T
            r = jax.nn.sigmoid(time_shift(h, mix_r) @ Wr_t.T)
            w = -jnp.exp(time_decay)
            wkv_out, new_state = wkv(w, time_first, k, v)
            x = x + r * wkv_out
            h2 = layer_norm(x, ln2_g, ln2_b)
            kc = time_shift(h2, cmix_k) @ Wk_c.T
            rc = jax.nn.sigmoid(time_shift(h2, cmix_r) @ Wr_c.T)
            vv = jnp.square(jax.nn.relu(kc)) @ Wv_c.T
            x = x + rc * vv
            return (x, new_state)
        return _reference_tuple_inner(x, time_decay, time_first, Wk_t, Wv_t, Wr_t, Wk_c, Wv_c, Wr_c, ln1_g, ln1_b, ln2_g, ln2_b, mix_k, mix_v, mix_r, cmix_k, cmix_r)[0]

    def _L3_ffn_ref(hidden_states, wi_w, wo_w, lora_As, lora_Bs, top_k_indices, top_k_values):
        import jax, jax.numpy as jnp
        import numpy as np
        D_MODEL, D_FF, NUM_EXPERTS, RANK, TOP_K = (128, 512, 8, 16, 2)
        B, S = (8, 256)

        def _expert_ffn(h, wi_w, wo_w, A, Bm):
            inter = jnp.einsum('bsd,fd->bsf', h, wi_w)
            lora = jnp.einsum('bsr,fr->bsf', jnp.einsum('bsd,rd->bsr', h, A), Bm)
            inter = jax.nn.relu(inter + lora)
            return jnp.einsum('bsf,df->bsd', inter, wo_w)
        out = jnp.zeros_like(hidden_states)
        for k in range(top_k_values.shape[0]):
            A = jnp.take(lora_As, top_k_indices[k], axis=0)
            Bm = jnp.take(lora_Bs, top_k_indices[k], axis=0)
            out = out + top_k_values[k] * _expert_ffn(hidden_states, wi_w, wo_w, A, Bm)
        return out
    x = L0_attn_x
    x = x + 0.5 * _L0_ffn_ref(_layernorm(x, axis=-1), L0_ffn_gate_w, L0_ffn_expert_bias, L0_ffn_w1, L0_ffn_b1, L0_ffn_w2, L0_ffn_b2, L0_ffn_w3, L0_ffn_b3, L0_ffn_sw1, L0_ffn_sb1, L0_ffn_sw2, L0_ffn_sb2, L0_ffn_sw3, L0_ffn_sb3)
    x = x + _L0_attn_ref(_layernorm(x, axis=-1), L0_attn_W_in, L0_attn_conv_w, L0_attn_W_x, L0_attn_W_dt, L0_attn_b_dt, L0_attn_A_log, L0_attn_D_param, L0_attn_W_C, L0_attn_W_out)
    x = x + 0.5 * _L0_ffn_ref(_layernorm(x, axis=-1), L0_ffn_gate_w, L0_ffn_expert_bias, L0_ffn_w1, L0_ffn_b1, L0_ffn_w2, L0_ffn_b2, L0_ffn_w3, L0_ffn_b3, L0_ffn_sw1, L0_ffn_sb1, L0_ffn_sw2, L0_ffn_sb2, L0_ffn_sw3, L0_ffn_sb3)
    x = x + 0.5 * _L1_ffn_ref(_layernorm(x, axis=-1), L1_ffn_Ws1, L1_ffn_bs1, L1_ffn_Ws2, L1_ffn_bs2, L1_ffn_We1, L1_ffn_be1, L1_ffn_We2, L1_ffn_be2, L1_ffn_Wr, L1_ffn_br)
    x = x + _L1_attn_ref(_layernorm(x, axis=-1), L1_attn_in_proj_w, L1_attn_conv_w, L1_attn_conv_b, L1_attn_theta, L1_attn_decay_slopes, L1_attn_anchor_slopes, L1_attn_score_scale, L1_attn_deriv_logits, L1_attn_norm_scale, L1_attn_W_re, L1_attn_W_im, L1_attn_out_proj_w)
    x = x + 0.5 * _L1_ffn_ref(_layernorm(x, axis=-1), L1_ffn_Ws1, L1_ffn_bs1, L1_ffn_Ws2, L1_ffn_bs2, L1_ffn_We1, L1_ffn_be1, L1_ffn_We2, L1_ffn_be2, L1_ffn_Wr, L1_ffn_br)
    x = x + 0.5 * _L2_ffn_ref(_layernorm(x, axis=-1), L2_ffn_gate_w, L2_ffn_Wg, L2_ffn_Wu, L2_ffn_Wd, L2_ffn_Sg, L2_ffn_Su, L2_ffn_Sd)
    x = x + _L2_attn_ref(_layernorm(x, axis=-1), L2_attn_wq, L2_attn_wk, L2_attn_wv, L2_attn_wo)
    x = x + 0.5 * _L2_ffn_ref(_layernorm(x, axis=-1), L2_ffn_gate_w, L2_ffn_Wg, L2_ffn_Wu, L2_ffn_Wd, L2_ffn_Sg, L2_ffn_Su, L2_ffn_Sd)
    x = x + 0.5 * _L3_ffn_ref(_layernorm(x, axis=-1), L3_ffn_wi_w, L3_ffn_wo_w, L3_ffn_lora_As, L3_ffn_lora_Bs, L3_ffn_top_k_indices, L3_ffn_top_k_values)
    x = x + _L3_attn_ref(_layernorm(x, axis=-1), L3_attn_time_decay, L3_attn_time_first, L3_attn_Wk_t, L3_attn_Wv_t, L3_attn_Wr_t, L3_attn_Wk_c, L3_attn_Wv_c, L3_attn_Wr_c, L3_attn_ln1_g, L3_attn_ln1_b, L3_attn_ln2_g, L3_attn_ln2_b, L3_attn_mix_k, L3_attn_mix_v, L3_attn_mix_r, L3_attn_cmix_k, L3_attn_cmix_r)
    x = x + 0.5 * _L3_ffn_ref(_layernorm(x, axis=-1), L3_ffn_wi_w, L3_ffn_wo_w, L3_ffn_lora_As, L3_ffn_lora_Bs, L3_ffn_top_k_indices, L3_ffn_top_k_values)
    return x

_drawn_inputs = setup_inputs


def setup_inputs(seed=0):
    import zlib

    import numpy as np

    out = dict(_drawn_inputs(seed))
    spreads = {'L0_attn_b_dt': (1.0, 0.6),
     'L0_attn_A_log': (-2.0, 0.6),
     'L0_attn_D_param': (1.0, 0.6),
     'L0_ffn_expert_bias': (0.0, 0.1),
     'L1_attn_conv_b': (0.0, 0.1),
     'L1_attn_score_scale': (1.0, 0.6),
     'L1_attn_norm_scale': (1.0, 0.2),
     'L1_ffn_bs1': (0.0, 0.1),
     'L1_ffn_bs2': (0.0, 0.1),
     'L1_ffn_be1': (0.0, 0.1),
     'L1_ffn_be2': (0.0, 0.1),
     'L1_ffn_br': (0.0, 0.1),
     'L3_attn_ln1_g': (1.0, 0.6),
     'L3_attn_ln1_b': (0.0, 0.8),
     'L3_attn_ln2_g': (1.0, 0.6),
     'L3_attn_ln2_b': (0.0, 0.8),
     'L3_attn_mix_k': (1.0, 0.6),
     'L3_attn_mix_v': (1.0, 0.6),
     'L3_attn_mix_r': (1.0, 0.6),
     'L3_attn_cmix_k': (1.0, 0.6),
     'L3_attn_cmix_r': (1.0, 0.6)}
    factors = {'L0_attn_W_in': 8.0,
     'L0_attn_conv_w': 8.0,
     'L0_attn_W_x': 8.0,
     'L0_attn_W_dt': 8.0,
     'L0_attn_W_C': 8.0,
     'L0_attn_W_out': 8.0,
     'L0_ffn_b1': 3.028,
     'L0_ffn_b3': 2.847,
     'L1_attn_anchor_slopes': 64.0,
     'L3_attn_time_first': 8.0,
     'L3_attn_Wk_t': 5.24,
     'L3_attn_Wv_t': 3.971,
     'L3_attn_Wr_t': 8.0,
     'L3_attn_Wk_c': 8.0,
     'L3_attn_Wv_c': 7.304,
     'L3_attn_Wr_c': 8.0,
     'L3_ffn_wi_w': 6.725,
     'L3_ffn_wo_w': 5.537,
     'L3_ffn_lora_As': 8.0,
     'L3_ffn_lora_Bs': 8.0,
     'L3_ffn_top_k_values': 8.0}
    for name, (base, spread) in spreads.items():
        noise = np.random.default_rng([zlib.crc32(name.encode()), seed]).standard_normal(out[name].shape)
        drawn = base * np.exp(spread * noise) if base else spread * noise
        out[name] = jnp.asarray(drawn.astype(out[name].dtype))
    for name, factor in factors.items():
        out[name] = (out[name] * factor).astype(out[name].dtype)
    return out
```

```python
from contextlib import ExitStack

import concourse.bass as bass
from concourse import mybir

F32 = mybir.dt.float32
BF16 = mybir.dt.bfloat16
I32 = mybir.dt.int32
ALU = mybir.AluOpType
ACT = mybir.ActivationFunctionType
AX = mybir.AxisListType.X

P = 128
B, T, D = 8, 512, 128
N = B * T
TILES = T // P
LN_EPS = 1e-5
NEG_HUGE = -3.0e38

E0, F0, SH0 = 16, 64, 128
E1, F1, SH1, TAU = 12, 384, 256, 1.5
E2, F2, SH2 = 8, 352, 176
E3, F3, R3, K3 = 8, 512, 16, 2
NS, R0 = 16, 64
K1, H1, M1, A1 = 32, 4, 4, 4
D2 = 64

JOBS = {0: E0 * F0 // P + SH0 // P, 1: (E1 * F1 + SH1) // P, 2: E2 * F2 // P + 2, 3: F3 // P}
GATED = {0: E0 * F0 // P, 1: E1 * F1 // P, 2: E2 * F2 // P, 3: 0}
GATE_EVERY = {0: 1, 1: F1 // P, 2: 1}
EXPERTS = {0: E0, 1: E1, 2: E2}
LAG = 2
HID = 3
CREDIT = 3
NORM_SET = "natural_log_exp_and_others"
SILU_SET = "silu_and_others"

SMALL = [
    ("center", P), ("avg", P), ("ident", P),
    ("a0_xc", P), ("a0_z", P), ("a0_dtp", R0), ("a0_cp", NS), ("a0_dt", P),
    ("a0_c", P), ("a0_out", P),
    ("a1_v", P), ("a1_g", P), ("a1_s", P), ("a1_re", M1 * P), ("a1_im", M1 * P), ("a1_sum", P),
    ("a1_out", P), ("time", T),
    ("a2_kv", P), ("a2_q", P), ("a2_o", P),
    ("gate0", 2 * E0), ("gate1", E1), ("gate2", E2), ("b2_0", P), ("b2_1", P),
    ("rank", E0),
    ("bg0", JOBS[0]), ("bu0", JOBS[0]), ("bg1", JOBS[1]), ("bu1", JOBS[1]),
    ("by0", 1), ("by1", 1), ("gb0", 1), ("gb1", 1),
    ("a0_cw", 3), ("a0_bdt", 1), ("a0_alog", NS), ("a0_d", 1),
    ("a1_cwv", 4), ("a1_cwg", 4), ("a1_cws", 4), ("a1_cbv", 1), ("a1_cbg", 1), ("a1_cbs", 1),
    ("a1_theta", M1), ("a1_slope", 1), ("a1_score", 1), ("a1_deriv", 3), ("a1_nre", M1), ("a1_nim", M1),
    ("a3_first", 1), ("a3_g1", 1), ("a3_b1", 1), ("a3_g2", 1), ("a3_b2", 1),
    ("a3_mk", 1), ("a3_mv", 1), ("a3_mr", 1), ("a3_cmk", 1), ("a3_cmr", 1),
    ("f3_val", K3), ("f3_expert", 1),
]


def offsets():
    at, out = 0, {}
    for name, n in SMALL:
        out[name] = (at, n)
        at += n
    return out, at


OFF, SMALL_COLS = offsets()

B_AT = 3 * JOBS[0] * P
W0_COLS = B_AT + NS * P
L3_AT = {"wi": 0, "wo": F3, "A": 2 * F3, "B": 3 * F3, "k": 4 * F3, "v": 4 * F3 + P, "r": 4 * F3 + 2 * P,
         "rc": 4 * F3 + 3 * P, "kc": 5 * F3, "vc": 6 * F3, "weff0": 7 * F3, "weff1": 8 * F3}
W3_COLS = L3_AT["weff0"]

INV_2PI = 0.15915494309189535
TWO_PI_HI = 6.28125
TWO_PI_LO = 0.0019353071795864769
ROUND = 12582912.0
PI_IN = 3.1415925
HALF_PI = 1.5707963267948966


class Steps:

    def __init__(self, sem, names, base):
        self.sem, self.names, self.base, self.n, self.at = sem, names, base, len(names), 0

    def value(self, c, name):
        return c * self.n + (self.base + self.names.index(name) + 1)

    def before(self, c):
        return c * self.n + self.base

    def mark(self, name):
        assert self.names[self.at % self.n] == name, (self.names[self.at % self.n], name)
        self.at += 1
        return self.sem


def behind(j, jobs, buffers):
    for k in range(1, 2 * jobs + buffers):
        if (j - k) % jobs % buffers == j % buffers if j - k < 0 else (j - k) % buffers == j % buffers:
            return k
    raise ValueError


def pro_names(kind):
    pe, act, dve = ["center", "var"], ["sq", "lnv", "rstd"], ["h"]
    if kind in EXPERTS:
        pe += ["logits", "tok", "back"]
        act += ["gexp"]
        dve += ["lg", "ltok", "m1", "eq1", "rk1", "t1", "oh1", "l2", "m2", "eq2", "rk2", "t2", "oh2", "mask"]
        dve += ["s1p", "srec"] if kind == 0 else ["arg"]
        dve += ["ms", "sum", "sume", "rec", "w", "wh", "whf", "wr", "wm", "wmf", "wl", "gf", "gb"]
    return pe, act, dve


STAGES = [(k, l) for l in range(4) for k in ("ffn", "mix", "ffn")]
SLOTS = {0: [0, 1, 2, 3, 5, 7], 1: [2, 5, 10, 14, 24, 30], 2: [2, 4, 8, 10, 18, 21], 3: [0, 1, 2, 2, 3, 3]}


def a0_names():
    pe = ["xc", "z", "dtp", "cp", "dtpre", "C"]
    for n in range(NS):
        pe += [f"bp{n}"] + ([f"ss{n - 1}"] if n else [])
    pe += [f"ss{NS - 1}", "out"]
    act = ["xcp", "sz", "xs", "dtps", "cps", "v", "av", "ev", "lv", "Cs"] + [f"Ad{n}" for n in range(NS)]
    dve = ["c0", "c1", "c2", "dt0", "dt", "dx"]
    for n in range(NS):
        dve += [f"bx{n}", f"s{n}"]
    dve += ["cs", "y", "o"]
    return pe, act, dve


def a1_names():
    pe = ["zv", "zg", "zs"]
    for m in range(M1):
        pe += [f"yre{m}", f"yim{m}", f"qre{m}", f"qim{m}"]
    pe += ["out"]
    act = ["zvp", "zgp", "zsp", "sg", "p"]
    for m in range(M1):
        act += [f"abs{m}", f"sin{m}", f"cos{m}", f"sqre{m}", f"sqim{m}"]
    act += ["lnq", "rs"]
    dve = [f"v{i}" for i in range(4)] + [f"g{i}" for i in range(4)] + [f"s{i}" for i in range(4)]
    dve += ["cl0", "cl1", "pw", "a", "m", "pwp", "den"]
    for m in range(M1):
        dve += [f"{x}{m}" for x in ("phi", "q", "k", "r1_", "r2_", "r", "re", "nre", "im", "nim")]
    dve += ["dmax", "inv", "i2", "t", "f", "f2", "yy"]
    return pe, act, dve


def a2_names():
    return (["kv", "et", "ew", "m", "out"], ["kvs", "ets", "ews", "ms"], ["none"])


def a3_names():
    pe = ["center1", "var1", "k", "v", "r", "center2", "var2", "kc0", "kc1", "kc2", "kc3", "rc", "vc"]
    act = ["sq1", "lnv1", "rstd1", "ks", "vs", "ab", "lnS", "ea", "eb", "e1", "e2", "sr",
           "sq2", "lnv2", "rstd2", "r0", "q0", "r1", "q1", "r2", "q2", "r3", "q3", "src"]
    dve = ["n1", "h1", "d1", "xk", "xv", "xr", "cm", "da", "db", "S", "pp", "dl", "al", "nb", "bv", "aa",
           "dw", "aw", "nw", "n0", "n1b", "num", "den", "deni", "rden", "o", "ro", "x1",
           "n2", "h2", "d2", "xkc", "xrc", "res", "acc"]
    return pe, act, dve


PREP = (["weff0", "weff1"], ["ealog", "sl_a", "sl_e", "sl_l", "tw", "de"],
        ["naexp", "sl_n", "sl_s", "sl_neg", "dm", "dd", "dsum", "drec", "dw", "ndw2", "blk",
         "idxf", "oh0", "oh1", "ba0", "ba1", "wi0", "wi1"])


def build(nc, x_in, small_in, w0_in, w1_in, w2_in, w3_in, sel_in, idx_in, out, stop_after=len(STAGES)):
    ctx = ExitStack()
    with ctx:
        def sb(name, shape, dt=F32):
            return ctx.enter_context(nc.sbuf_tensor(name, shape, dt))

        def sem(name):
            return ctx.enter_context(nc.semaphore(name))

        X = sb("X", [P, N])
        H = sb("H", [P, N])
        GF = sb("GF", [P, N])
        GB = sb("GB", [P, N], BF16)
        WA = sb("WA", [P, 3 * JOBS[1] * P])
        WB = sb("WB", [P, 3 * JOBS[2] * P])
        SM = sb("SM", [P, SMALL_COLS])
        SEL = sb("SEL", [P, (GATED[0] + E1 + GATED[2]) * P], BF16)
        PS = ctx.enter_context(nc.psum_tensor("PS", [P, 8, T], F32))

        sq = sb("sq", [P, T])
        rstd = sb("rstd", [P, T])
        lnvar = sb("lnvar", [P, T])
        actb = sb("actb", [P, 2, T])
        vb2 = sb("vb2", [P, 2, T])
        vb = vb2[:, 0, :]
        hid = sb("hid", [P, HID, T])
        fin = sb("fin", [P, T])
        AA = sb("AA", [P, T + 4])
        lgs = AA[:, 0:T]
        tk = sb("tk", [P, 16, TILES, E0])
        LT = sb("LT", [P, TILES, 2 * E0])
        tcol = sb("tcol", [P, 8, TILES])
        ws = sb("ws", [P, TILES, P])
        wbf = sb("wbf", [P, 2, TILES, E0], BF16)
        epsc = sb("epsc", [P, 4])
        sv = sb("sv", [P, 64])
        idxi = sb("idxi", [P, K3], I32)
        ones = sb("ones", [P, T])
        hs = sb("hs", [P, T])

        def small(name, rows=P):
            at, n = OFF[name]
            return SM[0:rows, at:at + n]

        def smallc(name, i=0, rows=P):
            at, _ = OFF[name]
            return SM[0:rows, at + i:at + i + 1]

        def ltok_view(layer):
            return LT[:, :, 0:EXPERTS[layer] * (2 if layer == 0 else 1)]

        def tile(i):
            return H[:, i * T:(i + 1) * T] if i < 8 else GF[:, (i - 8) * T:(i - 7) * T]

        def padded(i):
            return H[:, i * T:(i + 2) * T] if i < 8 else GF[:, (i - 8) * T:(i - 6) * T]

        NUM = {"re": [tile(6), tile(7)], "im": [tile(8), tile(9)]}
        SQ = {"re": tile(10), "im": tile(11)}
        DEN = sq[:, :]
        M3 = {"h": padded(0), "k": tile(2), "v": tile(3), "r": tile(4), "x1": tile(5), "kc": tile(2), "rc": tile(3),
              "q0": tile(6), "q1": tile(7), "q2": tile(8), "q3": tile(9)}
        K_, V_, MX, PP = tile(10), tile(11), padded(12), padded(14)
        AB = hid[:, 0:2, :].rearrange("p a t -> p (a t)")
        S_, LS, AL, BE, BV = hid[:, 2, :], vb[:, :], actb[:, 0, :], actb[:, 1, :], sq[:, :]
        AW, NW, R_, RC = tile(2), tile(3), tile(4), vb[:, :]

        def w3(name, n=P):
            return WA[:, L3_AT[name]:L3_AT[name] + n]

        s_x, s_small, s_w0, s_w1, s_w2, s_w3 = (sem(n) for n in ("s_x", "s_small", "s_w0", "s_w1", "s_w2", "s_w3"))
        s_out = sem("s_out")
        x_ready = sem("x_ready")
        consts = sem("consts")
        g_ready = sem("g_ready")
        u_ready = sem("u_ready")
        gate_ready = sem("gate_ready")
        act_done = sem("act_done")
        v_ready = sem("v_ready")
        hid_ready = sem("hid_ready")
        y_added = sem("y_added")
        y_final = sem("y_final")
        fin_ready = sem("fin_ready")
        sems = {k: (sem(f"{k}_pe"), sem(f"{k}_act"), sem(f"{k}_dve")) for k in ("pro", "a0", "a1", "a2", "a3", "prep")}

        MIX_NAMES = {0: a0_names(), 1: a1_names(), 2: a2_names(), 3: a3_names()}
        prep = [Steps(s, n, 0) for s, n in zip(sems["prep"], PREP)]
        prologues, base = [], [0, 0, 0]
        for kind, layer in STAGES:
            names = pro_names(layer if kind == "ffn" else None)
            prologues.append([Steps(s, n, b) for s, n, b in zip(sems["pro"], names, base)])
            base = [b + B * len(n) for b, n in zip(base, names)]
        mixes = {l: [Steps(s, n, 0) for s, n in zip(sems[f"a{l}"], MIX_NAMES[l])] for l in range(4)}
        job0, gate0, ffn_i, jb, gb = {}, {}, {}, 0, 0
        vjob0, vb0, fi = {}, 0, 0
        for s, (kind, layer) in enumerate(STAGES):
            if kind == "ffn":
                job0[s], gate0[s], vjob0[s], ffn_i[s] = jb, gb, vb0, fi
                jb += B * JOBS[layer]
                vb0 += B * (GATED[layer] if layer < 3 else JOBS[layer])
                if layer < 3:
                    gb += B * (GATED[layer] // GATE_EVERY[layer])
                fi += 1

        def chunk(c):
            return bass.ds(c * T, T)

        def x_of(s, c):
            return c + ((s - 1) * B + 1)

        def ffn_weights(layer):
            if layer == 3:
                return w3("weff0", F3), w3("weff1", F3), w3("wo", F3)
            w, j = (WB, JOBS[layer]) if layer in (0, 2) else (WA, JOBS[layer])
            return w[:, 0:j * P], w[:, j * P:2 * j * P], w[:, 2 * j * P:3 * j * P]

        sel_at = {0: 0, 1: GATED[0], 2: GATED[0] + E1}

        def loop(eng, body, last):
            with eng.Fori(0, B - 1) as c:
                body(c, False)
            if last:
                body(B - 1, True)

        block = ctx.enter_context(nc.Block())

        @block.sync
        def _(sp):
            sp.dma_start(SM[:, :], small_in).then_inc(s_small, 16)
            sp.dma_start(idxi[:, :], idx_in).then_inc(s_small, 16)
            sp.dma_start(SEL[:, :], sel_in).then_inc(s_small, 16)
            for c in range(B):
                sp.dma_start(X[:, c * T:(c + 1) * T], x_in[:, c * T:(c + 1) * T]).then_inc(s_x, 16)
            sp.dma_start(WB[:, 0:W0_COLS], w0_in).then_inc(s_w0, 16)
            sp.dma_start(WA[:, :], w1_in).then_inc(s_w1, 16)
            if stop_after > 6:
                sp.wait_ge(x_ready, 3 * B)
                sp.dma_start(WB[:, :], w2_in).then_inc(s_w2, 16)
            if stop_after > 6:
                sp.wait_ge(x_ready, 6 * B)
                sp.dma_start(WA[:, 0:W3_COLS], w3_in).then_inc(s_w3, 16)
            for c in range(B):
                sp.wait_ge(x_ready, (stop_after - 1) * B + c + 1)
                sp.dma_start(out[:, c * T:(c + 1) * T], X[:, c * T:(c + 1) * T]).then_inc(s_out, 16)
            sp.wait_ge(s_out, 16 * B)

        @block.tensor
        def _(pe):
            mm = nc.tensor.matmul

            def norm_part(s, c, part, steps, src, hdst):
                p, a, d = steps
                if part == 0:
                    if s > 0:
                        pe.wait_ge(x_ready, x_of(s, c))
                    if not (s == 0 and isinstance(c, int) and c == 0):
                        pe.wait_ge(d.sem, d.before(c))
                    mm(PS[:, 6, :], small("center"), src, start=True, stop=True).then_inc(p.mark("center"), 1)
                if part == 1:
                    pe.wait_ge(a.sem, a.value(c, "sq"))
                    mm(PS[:, 7, :], small("avg"), sq[:, :], start=True, stop=True).then_inc(p.mark("var"), 1)

            def route_part(s, c, layer, part, steps):
                p, a, d = steps
                e = EXPERTS[layer]
                nl = 2 * e if layer == 0 else e
                if part == 2:
                    pe.wait_ge(d.sem, d.value(c, "h"))
                    mm(PS[0:nl, 7, :], small(f"gate{layer}"), H[:, chunk(c)], start=True, stop=True)\
                        .then_inc(p.mark("logits"), 1)
                if part == 3:
                    pe.wait_ge(d.sem, d.value(c, "lg"))
                    for t in range(TILES):
                        last = nc.tensor.transpose(PS[:, 7, t * P:(t + 1) * P], lgs[:, t * P:(t + 1) * P],
                                                   small("ident"))
                    last.then_inc(p.mark("tok"), 1)
                if part == 5:
                    pe.wait_ge(d.sem, d.value(c, "wl"))
                    for t in range(TILES):
                        last = nc.tensor.transpose(PS[:, 7, t * P:(t + 1) * P], ws[:, t, :], small("ident"))
                    last.then_inc(p.mark("back"), 1)

            def prologue(s, c, part):
                kind, layer = STAGES[s]
                steps = prologues[s]
                if part < 2:
                    norm_part(s, c, part, steps, X[:, chunk(c)], None)
                elif kind == "ffn" and layer in EXPERTS:
                    route_part(s, c, layer, part, steps)

            def ffn(s, layer):
                J = JOBS[layer]
                wg, wu, wd = ffn_weights(layer)
                hd = lambda n: n + (1 + CREDIT)
                nxt_ffn = s + 1 < stop_after and STAGES[s + 1][0] == "ffn"
                if s == 0 or STAGES[s - 1][0] == "mix":
                    for part in range(6):
                        prologue(s, 0, part)
                if s > 0:
                    pe.wait_ge(x_ready, s * B)
                pe.wait_ge({0: s_w0, 1: s_w1, 2: s_w2, 3: s_w3}[layer], 16)

                def body(c, last):
                    n0 = c * J + job0[s]
                    h = H[:, chunk(c)]
                    p, a, d = prologues[s]
                    pe.wait_ge(d.sem, d.value(c, d.names[-1]))
                    gi = 0
                    for j in range(J + LAG):
                        if j < J:
                            pe.wait_ge(act_done, hd(n0 + (j - behind(j, J, 2))))
                            mm(PS[:, j % 2, :], wg[:, j * P:(j + 1) * P], h, start=True, stop=True).then_inc(g_ready, 1)
                            pe.wait_ge(hid_ready, hd(n0 + (j - behind(j, J, 2))))
                            mm(PS[:, 2 + j % 2, :], wu[:, j * P:(j + 1) * P], h, start=True, stop=True)\
                                .then_inc(u_ready, 1)
                        if j >= LAG:
                            jj = j - LAG
                            if jj == 0:
                                pe.wait_ge(fin_ready, c + (ffn_i[s] * B + 1))
                            pe.wait_ge(hid_ready, hd(n0 + jj))
                            mm(PS[:, 5, :], wd[:, jj * P:(jj + 1) * P], hid[:, jj % HID, :], start=jj == 0,
                               stop=jj == J - 1 and layer > 1).then_inc(y_added, 1)
                        if j < J and j < GATED[layer] and j % GATE_EVERY[layer] == 0:
                            pe.wait_ge(hid_ready, hd(n0 + (j - 1)))
                            at = (sel_at[layer] + gi) * P
                            mm(PS[:, 4, :], SEL[:, at:at + P], GB[:, chunk(c)], start=True, stop=True)\
                                .then_inc(gate_ready, 1)
                            gi += 1
                        for part in range(6):
                            if SLOTS[layer][part] == j:
                                if not last:
                                    prologue(s, c + 1, part)
                                elif nxt_ffn:
                                    prologue(s + 1, 0, part)
                    if layer in (0, 1):
                        k = 3 * EXPERTS[layer]
                        mm(PS[:, 5, :], small(f"b2_{layer}", k), GF[0:k, chunk(c)], start=False, stop=True)\
                            .then_inc(y_final, 1)

                loop(pe, body, True)

            def norm_pe(steps, c, n, src):
                p, a, d = steps
                mm(PS[:, 6, :], small("center"), src, start=True, stop=True).then_inc(p.mark(f"center{n}"), 1)
                pe.wait_ge(a.sem, a.value(c, f"sq{n}"))
                mm(PS[:, 7, :], small("avg"), sq[:, :], start=True, stop=True).then_inc(p.mark(f"var{n}"), 1)

            def mix0(c, s):
                p, a, d = mixes[0]
                prologue(s, c, 0)
                prologue(s, c, 1)
                pd = prologues[s][2]
                pe.wait_ge(pd.sem, pd.value(c, "h"))
                mm(PS[:, 0, :], small("a0_xc"), hs[:, :], start=True, stop=True).then_inc(p.mark("xc"), 1)
                mm(PS[:, 1, :], small("a0_z"), hs[:, :], start=True, stop=True).then_inc(p.mark("z"), 1)
                pe.wait_ge(a.sem, a.value(c, "xs"))
                mm(PS[0:R0, 2, :], small("a0_dtp"), tile(3), start=True, stop=True).then_inc(p.mark("dtp"), 1)
                mm(PS[0:NS, 3, :], small("a0_cp"), tile(3), start=True, stop=True).then_inc(p.mark("cp"), 1)
                pe.wait_ge(a.sem, a.value(c, "dtps"))
                mm(PS[:, 4, :], small("a0_dt", R0), tile(4)[0:R0, :], start=True, stop=True)\
                    .then_inc(p.mark("dtpre"), 1)
                pe.wait_ge(a.sem, a.value(c, "cps"))
                mm(PS[:, 5, :], small("a0_c", NS), tile(5)[0:NS, :], start=True, stop=True).then_inc(p.mark("C"), 1)

                def sum_state(n):
                    pe.wait_ge(d.sem, d.value(c, f"s{n}"))
                    mm(PS[:, 0, :], small("ident"), tile(12 + n % 2), start=n == 0, stop=n == NS - 1)\
                        .then_inc(p.mark(f"ss{n}"), 1)

                for n in range(NS):
                    if n >= 2:
                        pe.wait_ge(d.sem, d.value(c, f"bx{n - 2}"))
                    mm(PS[:, 2 + n % 2, :], WB[:, B_AT + n * P:B_AT + (n + 1) * P], tile(3), start=True, stop=True)\
                        .then_inc(p.mark(f"bp{n}"), 1)
                    if n:
                        sum_state(n - 1)
                sum_state(NS - 1)
                pe.wait_ge(d.sem, d.value(c, "y"))
                mm(PS[:, 1, :], small("a0_out"), tile(6), start=True, stop=True).then_inc(p.mark("out"), 1)

            def mix1(c, s):
                p, a, d = mixes[1]
                prologue(s, c, 0)
                prologue(s, c, 1)
                pd = prologues[s][2]
                pe.wait_ge(pd.sem, pd.value(c, "h"))
                for b, z in enumerate("vgs"):
                    mm(PS[:, b, :], small(f"a1_{z}"), hs[:, :], start=True, stop=True).then_inc(p.mark(f"z{z}"), 1)
                for m in range(M1):
                    for part in ("re", "im"):
                        pe.wait_ge(d.sem, d.value(c, f"n{part}{m}"))
                        mm(PS[:, 3, :], small(f"a1_{part}")[:, m * P:(m + 1) * P], NUM[part][m % 2],
                           start=m == 0 and part == "re", stop=m == M1 - 1 and part == "im")\
                            .then_inc(p.mark(f"y{part}{m}"), 1)
                    for part in ("re", "im"):
                        pe.wait_ge(a.sem, a.value(c, f"sq{part}{m}"))
                        mm(PS[:, 4, :], small("a1_sum"), SQ[part], start=m == 0 and part == "re",
                           stop=m == M1 - 1 and part == "im").then_inc(p.mark(f"q{part}{m}"), 1)
                pe.wait_ge(d.sem, d.value(c, "yy"))
                mm(PS[:, 5, :], small("a1_out"), fin[:, :], start=True, stop=True).then_inc(p.mark("out"), 1)

            def mix2(c, s):
                p, a, d = mixes[2]
                prologue(s, c, 0)
                prologue(s, c, 1)
                pd = prologues[s][2]
                pe.wait_ge(pd.sem, pd.value(c, "h"))
                for t in range(TILES):
                    last = mm(PS[:, 0, t * P:(t + 1) * P], hs[:, t * P:(t + 1) * P], small("a2_kv"),
                              start=True, stop=True)
                last.then_inc(p.mark("kv"), 1)
                pe.wait_ge(a.sem, a.value(c, "kvs"))
                kv = tile(0).rearrange("p (t n) -> p t n", t=TILES)
                for t in range(TILES):
                    last = mm(PS[0:D2, 1, 0:P], kv[:, t, 0:D2], kv[:, t, :], start=t == 0, stop=t == TILES - 1)
                last.then_inc(p.mark("et"), 1)
                pe.wait_ge(a.sem, a.value(c, "ets"))
                mm(PS[:, 2, 0:P], tile(1)[0:D2, 0:P], small("a2_o", D2), start=True, stop=True)\
                    .then_inc(p.mark("ew"), 1)
                pe.wait_ge(a.sem, a.value(c, "ews"))
                mm(PS[:, 3, 0:P], small("a2_q"), tile(2)[:, 0:P], start=True, stop=True)\
                    .then_inc(p.mark("m"), 1)
                pe.wait_ge(a.sem, a.value(c, "ms"))
                mm(PS[:, 4, :], tile(3)[:, 0:P], hs[:, :], start=True, stop=True).then_inc(p.mark("out"), 1)

            def mix3(c, s):
                p, a, d = mixes[3]
                prologue(s, c, 0)
                prologue(s, c, 1)
                pd = prologues[s][2]
                pe.wait_ge(pd.sem, pd.value(c, "h"))
                norm_pe(mixes[3], c, 1, hs[:, :])
                for b, z in enumerate("kvr"):
                    pe.wait_ge(d.sem, d.value(c, f"x{z}"))
                    mm(PS[:, b, :], w3(z), M3[z], start=True, stop=True).then_inc(p.mark(z), 1)
                pe.wait_ge(d.sem, d.value(c, "x1"))
                norm_pe(mixes[3], c, 2, M3["x1"])
                pe.wait_ge(d.sem, d.value(c, "xkc"))
                for f in range(4):
                    if f == 2:
                        pe.wait_ge(a.sem, a.value(c, "sr"))
                    mm(PS[:, f, :], w3("kc", F3)[:, f * P:(f + 1) * P], M3["kc"], start=True, stop=True)\
                        .then_inc(p.mark(f"kc{f}"), 1)
                pe.wait_ge(d.sem, d.value(c, "xrc"))
                mm(PS[:, 4, :], w3("rc"), M3["rc"], start=True, stop=True).then_inc(p.mark("rc"), 1)
                for f in range(4):
                    pe.wait_ge(a.sem, a.value(c, f"q{f}"))
                    last = mm(PS[:, 5, :], w3("vc", F3)[:, f * P:(f + 1) * P], M3[f"q{f}"], start=f == 0, stop=f == 3)
                last.then_inc(p.mark("vc"), 1)

            pe.wait_ge(s_small, 48)
            pe.wait_ge(s_x, 16 * B)
            pe.wait_ge(consts, 6)

            def prep_pe():
                p, a, d = prep
                pe.wait_ge(s_w3, 16)
                for k in range(K3):
                    pe.wait_ge(d.sem, d.value(0, f"ba{k}"))
                    mm(PS[:, 6 + k, :], w3("A"), w3(f"weff{k}", F3),
                       start=True, stop=True).then_inc(p.mark(f"weff{k}"), 1)

            for s, (kind, layer) in enumerate(STAGES[:stop_after]):
                if s == 9:
                    pe.wait_ge(x_ready, 9 * B)
                    prep_pe()
                    pe.wait_ge(prep[2].sem, prep[2].value(0, "wi1"))
                if kind == "ffn":
                    ffn(s, layer)
                else:
                    pe.wait_ge(x_ready, s * B)
                    if layer == 1 or layer == 0:
                        pe.wait_ge(prep[2].sem, prep[2].value(0, "blk"))
                    with pe.Fori(0, B) as c:
                        (mix0, mix1, mix2, mix3)[layer](c, s)

        @block.scalar
        def _(act):
            run = nc.scalar.activation
            eps = epsc[:, 0:1]

            def norm_act(steps, c, sq_n, ln_n, rs_n, ce, va):
                p, a, d = steps
                act.wait_ge(p.sem, p.value(c, ce))
                run(sq[:, :], PS[:, 6, :], ACT.Square).then_inc(a.mark(sq_n), 1)

            def norm_act2(steps, c, sq_n, ln_n, rs_n, ce, va):
                p, a, d = steps
                nc.scalar.preload_act_table_set(NORM_SET)
                act.wait_ge(p.sem, p.value(c, va))
                run(lnvar[:, :], PS[:, 7, :], ACT.Ln, bias=eps).then_inc(a.mark(ln_n), 1)
                act.wait_ge(a.sem, a.value(c, ln_n))
                run(rstd[:, :], lnvar[:, :], ACT.Exp, scale=-0.5).then_inc(a.mark(rs_n), 1)

            NRM = ("sq", "lnv", "rstd", "center", "var")

            def prologue(s, c, part):
                kind, layer = STAGES[s]
                steps = prologues[s]
                p, a, d = steps
                if part == 0:
                    norm_act(steps, c, *NRM)
                if part == 1:
                    norm_act2(steps, c, *NRM)
                if part == 3 and kind == "ffn" and layer in EXPERTS:
                    nc.scalar.preload_act_table_set(NORM_SET)
                    e = EXPERTS[layer]
                    if layer == 0:
                        act.wait_ge(d.sem, d.value(c, "ltok"))
                        run(tk[:, 12, :, 0:e], ltok_view(layer)[:, :, e:2 * e], ACT.Exp, scale=-1.0)\
                            .then_inc(a.mark("gexp"), 1)
                    else:
                        act.wait_ge(d.sem, d.value(c, "arg"))
                        run(tk[:, 12, :, 0:e], tk[:, 11, :, 0:e], ACT.Exp).then_inc(a.mark("gexp"), 1)

            def ffn(s, layer):
                J = JOBS[layer]
                func = {0: ACT.Silu, 1: ACT.Gelu, 2: ACT.Silu, 3: ACT.Relu}[layer]
                nxt_ffn = s + 1 < stop_after and STAGES[s + 1][0] == "ffn"
                if s == 0 or STAGES[s - 1][0] == "mix":
                    for part in range(6):
                        prologue(s, 0, part)

                def body(c, last):
                    n0 = c * J + job0[s]
                    for j in range(J):
                        act.wait_ge(hid_ready, n0 + (j - behind(j, J, 2) + 1 + CREDIT))
                        act.wait_ge(g_ready, n0 + (j + 1))
                        kw = {"bias": smallc(f"bg{layer}", j)} if layer < 2 else {}
                        run(actb[:, j % 2, :], PS[:, j % 2, :], func, **kw).then_inc(act_done, 1)
                        for part in range(6):
                            if SLOTS[layer][part] == j:
                                if not last:
                                    prologue(s, c + 1, part)
                                elif nxt_ffn:
                                    prologue(s + 1, 0, part)

                loop(act, body, True)

            def mix0(c, s):
                p, a, d = mixes[0]
                prologue(s, c, 0)
                prologue(s, c, 1)
                xcp, v, av, lv, dt, cs, sz, xs = (padded(0), tile(8), tile(9), tile(9), tile(10), tile(7), tile(2), tile(3))
                act.wait_ge(p.sem, p.value(c, "xc"))
                run(xcp[:, 1:T + 1], PS[:, 0, :], ACT.Copy).then_inc(a.mark("xcp"), 1)
                nc.scalar.preload_act_table_set(SILU_SET)
                act.wait_ge(p.sem, p.value(c, "z"))
                run(sz, PS[:, 1, :], ACT.Silu).then_inc(a.mark("sz"), 1)
                act.wait_ge(d.sem, d.value(c, "c2"))
                run(xs, fin[:, :], ACT.Silu).then_inc(a.mark("xs"), 1)
                act.wait_ge(p.sem, p.value(c, "dtp"))
                run(tile(4)[0:R0, :], PS[0:R0, 2, :], ACT.Copy).then_inc(a.mark("dtps"), 1)
                act.wait_ge(p.sem, p.value(c, "cp"))
                run(tile(5)[0:NS, :], PS[0:NS, 3, :], ACT.Copy).then_inc(a.mark("cps"), 1)
                nc.scalar.preload_act_table_set(NORM_SET)
                act.wait_ge(p.sem, p.value(c, "dtpre"))
                run(v, PS[:, 4, :], ACT.Identity, bias=smallc("a0_bdt")).then_inc(a.mark("v"), 1)
                act.wait_ge(a.sem, a.value(c, "v"))
                run(av, v, ACT.Abs).then_inc(a.mark("av"), 1)
                act.wait_ge(a.sem, a.value(c, "av"))
                run(tile(11), av, ACT.Exp, scale=-1.0).then_inc(a.mark("ev"), 1)
                act.wait_ge(a.sem, a.value(c, "ev"))
                run(lv, tile(11), ACT.Ln, bias=epsc[:, 3:4]).then_inc(a.mark("lv"), 1)
                act.wait_ge(p.sem, p.value(c, "C"))
                run(cs, PS[:, 5, :], ACT.Copy).then_inc(a.mark("Cs"), 1)
                act.wait_ge(d.sem, d.value(c, "dt"))
                for n in range(NS):
                    if n >= 2:
                        act.wait_ge(d.sem, d.value(c, f"s{n - 2}"))
                    run(tile(14 + n % 2), dt, ACT.Exp, scale=sv[:, n:n + 1]).then_inc(a.mark(f"Ad{n}"), 1)

            def mix1(c, s):
                p, a, d = mixes[1]
                prologue(s, c, 0)
                prologue(s, c, 1)
                for b, z in enumerate("vgs"):
                    act.wait_ge(p.sem, p.value(c, f"z{z}"))
                    run(padded(2 * b)[:, 3:T + 3], PS[:, b, :], ACT.Copy).then_inc(a.mark(f"z{z}p"), 1)
                nc.scalar.preload_act_table_set(SILU_SET)
                act.wait_ge(d.sem, d.value(c, "g3"))
                run(tile(13), tile(13), ACT.Silu).then_inc(a.mark("sg"), 1)
                nc.scalar.preload_act_table_set(NORM_SET)
                act.wait_ge(d.sem, d.value(c, "cl1"))
                run(tile(14), tile(14), ACT.Exp).then_inc(a.mark("p"), 1)
                nc.scalar.preload_act_table_set(SILU_SET)
                for m in range(M1):
                    act.wait_ge(d.sem, d.value(c, f"r{m}"))
                    run(actb[:, 0, :], vb[:, :], ACT.Abs).then_inc(a.mark(f"abs{m}"), 1)
                    if m:
                        act.wait_ge(d.sem, d.value(c, f"im{m - 1}"))
                    run(hid[:, 0, :], vb[:, :], ACT.Sin).then_inc(a.mark(f"sin{m}"), 1)
                    act.wait_ge(a.sem, a.value(c, f"abs{m}"))
                    run(hid[:, 1, :], actb[:, 0, :], ACT.Sin, scale=-1.0, bias=epsc[:, 2:3]).then_inc(a.mark(f"cos{m}"), 1)
                    for part in ("re", "im"):
                        act.wait_ge(d.sem, d.value(c, f"n{part}{m}"))
                        if m:
                            act.wait_ge(p.sem, p.value(c, f"q{part}{m - 1}"))
                        run(SQ[part], NUM[part][m % 2], ACT.Square).then_inc(a.mark(f"sq{part}{m}"), 1)
                nc.scalar.preload_act_table_set(NORM_SET)
                act.wait_ge(d.sem, d.value(c, "t"))
                run(vb[:, :], vb[:, :], ACT.Ln, scale=1.0 / (2 * H1 * M1), bias=eps).then_inc(a.mark("lnq"), 1)
                act.wait_ge(a.sem, a.value(c, "lnq"))
                run(vb[:, :], vb[:, :], ACT.Exp, scale=-0.5).then_inc(a.mark("rs"), 1)

            def mix2(c, s):
                p, a, d = mixes[2]
                prologue(s, c, 0)
                prologue(s, c, 1)
                act.wait_ge(p.sem, p.value(c, "kv"))
                run(tile(0), PS[:, 0, :], ACT.Copy).then_inc(a.mark("kvs"), 1)
                act.wait_ge(p.sem, p.value(c, "et"))
                run(tile(1)[0:D2, 0:P], PS[0:D2, 1, 0:P], ACT.Copy, scale=(3.0 / D2) ** 0.5).then_inc(a.mark("ets"), 1)
                act.wait_ge(p.sem, p.value(c, "ew"))
                run(tile(2)[:, 0:P], PS[:, 2, 0:P], ACT.Copy).then_inc(a.mark("ews"), 1)
                act.wait_ge(p.sem, p.value(c, "m"))
                run(tile(3)[:, 0:P], PS[:, 3, 0:P], ACT.Copy).then_inc(a.mark("ms"), 1)

            def mix3(c, s):
                p, a, d = mixes[3]
                prologue(s, c, 0)
                prologue(s, c, 1)
                n1 = ("sq1", "lnv1", "rstd1", "center1", "var1")
                n2 = ("sq2", "lnv2", "rstd2", "center2", "var2")
                norm_act(mixes[3], c, *n1)
                norm_act2(mixes[3], c, *n1)
                act.wait_ge(p.sem, p.value(c, "k"))
                run(K_, PS[:, 0, :], ACT.Copy).then_inc(a.mark("ks"), 1)
                act.wait_ge(p.sem, p.value(c, "v"))
                run(V_, PS[:, 1, :], ACT.Copy).then_inc(a.mark("vs"), 1)
                act.wait_ge(d.sem, d.value(c, "db"))
                run(AB, AB, ACT.Exp).then_inc(a.mark("ab"), 1)
                act.wait_ge(d.sem, d.value(c, "S"))
                run(LS, S_, ACT.Ln, bias=epsc[:, 1:2]).then_inc(a.mark("lnS"), 1)
                for n, w, t in (("ea", "al", AL), ("eb", "nb", BE), ("e1", "aw", AW), ("e2", "nw", NW)):
                    act.wait_ge(d.sem, d.value(c, w))
                    run(t, t, ACT.Exp).then_inc(a.mark(n), 1)
                act.wait_ge(p.sem, p.value(c, "r"))
                run(R_, PS[:, 2, :], ACT.Sigmoid).then_inc(a.mark("sr"), 1)
                norm_act(mixes[3], c, *n2)
                norm_act2(mixes[3], c, *n2)
                for f in range(4):
                    act.wait_ge(p.sem, p.value(c, f"kc{f}"))
                    run(actb[:, f % 2, :], PS[:, f, :], ACT.Relu).then_inc(a.mark(f"r{f}"), 1)
                    act.wait_ge(a.sem, a.value(c, f"r{f}"))
                    run(M3[f"q{f}"], actb[:, f % 2, :], ACT.Square).then_inc(a.mark(f"q{f}"), 1)
                act.wait_ge(p.sem, p.value(c, "rc"))
                run(RC, PS[:, 4, :], ACT.Sigmoid).then_inc(a.mark("src"), 1)

            act.wait_ge(s_small, 48)
            act.wait_ge(consts, 6)
            act.sem_inc(act_done, CREDIT)
            p, a, d = prep
            nc.scalar.preload_act_table_set(NORM_SET)
            run(sv[:, 0:NS], small("a0_alog"), ACT.Exp).then_inc(a.mark("ealog"), 1)
            run(sv[:, 20:21], smallc("a1_slope"), ACT.Abs).then_inc(a.mark("sl_a"), 1)
            act.wait_ge(a.sem, a.value(0, "sl_a"))
            run(sv[:, 21:22], sv[:, 20:21], ACT.Exp, scale=-1.0).then_inc(a.mark("sl_e"), 1)
            act.wait_ge(a.sem, a.value(0, "sl_e"))
            run(sv[:, 22:23], sv[:, 21:22], ACT.Ln, bias=epsc[:, 3:4]).then_inc(a.mark("sl_l"), 1)
            act.wait_ge(d.sem, d.value(0, "sl_neg"))
            run(small("time"), small("time"), ACT.Exp, scale=sv[:, 24:25]).then_inc(a.mark("tw"), 1)
            act.wait_ge(d.sem, d.value(0, "dd"))
            run(sv[:, 31:34], sv[:, 28:31], ACT.Exp).then_inc(a.mark("de"), 1)
            for s, (kind, layer) in enumerate(STAGES[:stop_after]):
                if kind == "ffn":
                    ffn(s, layer)
                else:
                    act.wait_ge(x_ready, s * B)
                    with act.Fori(0, B) as c:
                        (mix0, mix1, mix2, mix3)[layer](c, s)

        @block.vector
        def _(dve):
            v = nc.vector

            def normed(s, c, hdst):
                p, a, d = prologues[s]
                dve.wait_ge(a.sem, a.value(c, "rstd"))
                v.tensor_tensor(hdst, PS[:, 6, :], rstd[:, :], ALU.mult).then_inc(d.mark("h"), 1)

            def prologue(s, c, part):
                kind, layer = STAGES[s]
                p, a, d = prologues[s]
                if part == 1:
                    normed(s, c, H[:, chunk(c)] if kind == "ffn" else hs[:, :])
                if kind != "ffn" or layer not in EXPERTS:
                    return
                e = EXPERTS[layer]
                nl = 2 * e if layer == 0 else e

                def need(name):
                    dve.wait_ge(d.sem, d.value(c, name))

                def K(i):
                    return tk[:, i, :, 0:e]

                def col(i):
                    return tcol[:, i, :]

                def wide(i):
                    return tcol[:, i, :].unsqueeze(2).to_broadcast([P, TILES, e])

                rank = small("rank")[:, E0 - e:E0].unsqueeze(1).to_broadcast([P, TILES, e])
                tt, red = v.tensor_tensor, v.tensor_reduce
                if part == 2:
                    dve.wait_ge(p.sem, p.value(c, "logits"))
                    gb = {0: smallc("gb0", 0, nl), 1: smallc("gb1", 0, nl), 2: 0.0}[layer]
                    v.tensor_scalar(lgs[0:nl, :], PS[0:nl, 7, :], gb, 1.0 / TAU if layer == 1 else 1.0,
                                    ALU.add, ALU.mult).then_inc(d.mark("lg"), 1)
                if part == 3:
                    dve.wait_ge(p.sem, p.value(c, "tok"))
                    lt = ltok_view(layer)
                    v.tensor_copy(lt, PS[:, 7, :].rearrange("p (t e) -> p t e", t=TILES)[:, :, 0:nl])\
                        .then_inc(d.mark("ltok"), 1)
                    need("ltok")
                    lb = lt[:, :, 0:e]
                    red(col(0), lb, AX, ALU.max).then_inc(d.mark("m1"), 1)
                    need("m1")
                    tt(K(2), lb, wide(0), ALU.is_equal).then_inc(d.mark("eq1"), 1)
                    need("eq1")
                    tt(K(3), K(2), rank, ALU.mult).then_inc(d.mark("rk1"), 1)
                    need("rk1")
                    red(col(1), K(3), AX, ALU.max).then_inc(d.mark("t1"), 1)
                    need("t1")
                    tt(K(4), K(3), wide(1), ALU.is_equal).then_inc(d.mark("oh1"), 1)
                    need("oh1")
                    v.scalar_tensor_tensor(out=K(5), in0=K(4), scalar=NEG_HUGE, in1=lb, op0=ALU.mult, op1=ALU.add)\
                        .then_inc(d.mark("l2"), 1)
                    need("l2")
                    red(col(2), K(5), AX, ALU.max).then_inc(d.mark("m2"), 1)
                    need("m2")
                    tt(K(6), K(5), wide(2), ALU.is_equal).then_inc(d.mark("eq2"), 1)
                    need("eq2")
                    tt(K(7), K(6), rank, ALU.mult).then_inc(d.mark("rk2"), 1)
                    need("rk2")
                    red(col(3), K(7), AX, ALU.max).then_inc(d.mark("t2"), 1)
                    need("t2")
                    tt(K(8), K(7), wide(3), ALU.is_equal).then_inc(d.mark("oh2"), 1)
                    need("oh2")
                    tt(K(9), K(4), K(8), ALU.add).then_inc(d.mark("mask"), 1)
                    if layer == 0:
                        dve.wait_ge(a.sem, a.value(c, "gexp"))
                        v.tensor_scalar(K(11), K(12), 1.0, None, ALU.add).then_inc(d.mark("s1p"), 1)
                        need("s1p")
                        v.reciprocal(K(10), K(11)).then_inc(d.mark("srec"), 1)
                    else:
                        tt(K(11), lb, wide(0), ALU.subtract).then_inc(d.mark("arg"), 1)
                if part == 4:
                    if layer == 0:
                        need("srec")
                        score = K(10)
                    else:
                        need("arg")
                        dve.wait_ge(a.sem, a.value(c, "gexp"))
                        score = K(12)
                    tt(K(13), score, K(9), ALU.mult).then_inc(d.mark("ms"), 1)
                    need("ms")
                    red(col(4), K(13), AX, ALU.add).then_inc(d.mark("sum"), 1)
                    need("sum")
                    v.tensor_scalar(col(5), col(4), 1e-10 if layer == 0 else 0.0, None, ALU.add)\
                        .then_inc(d.mark("sume"), 1)
                    need("sume")
                    v.reciprocal(col(6), col(5)).then_inc(d.mark("rec"), 1)
                    need("rec")
                    tt(K(14), K(13), wide(6), ALU.mult).then_inc(d.mark("w"), 1)
                    need("w")
                    v.tensor_copy(wbf[:, 0, :, 0:e], K(14)).then_inc(d.mark("wh"), 1)
                    need("wh")
                    v.tensor_copy(ws[:, :, 0:e], wbf[:, 0, :, 0:e]).then_inc(d.mark("whf"), 1)
                    need("whf")
                    tt(K(15), K(14), ws[:, :, 0:e], ALU.subtract).then_inc(d.mark("wr"), 1)
                    need("wr")
                    v.tensor_copy(wbf[:, 1, :, 0:e], K(15)).then_inc(d.mark("wm"), 1)
                    need("wm")
                    v.tensor_copy(ws[:, :, e:2 * e], wbf[:, 1, :, 0:e]).then_inc(d.mark("wmf"), 1)
                    need("wmf")
                    tt(ws[:, :, 2 * e:3 * e], K(15), ws[:, :, e:2 * e], ALU.subtract).then_inc(d.mark("wl"), 1)
                if part == 5:
                    dve.wait_ge(p.sem, p.value(c, "back"))
                    v.tensor_copy(GF[0:3 * e, chunk(c)], PS[0:3 * e, 7, :]).then_inc(d.mark("gf"), 1)
                    v.tensor_copy(GB[0:3 * e, chunk(c)], PS[0:3 * e, 7, :]).then_inc(d.mark("gb"), 1)

            def ffn(s, layer):
                J, NG = JOBS[layer], GATED[layer]
                NV = NG if layer < 3 else J
                nxt_ffn = s + 1 < stop_after and STAGES[s + 1][0] == "ffn"
                if s == 0 or STAGES[s - 1][0] == "mix":
                    for part in range(6):
                        prologue(s, 0, part)

                def body(c, last):
                    n0 = c * J + job0[s]
                    v0 = c * NV + vjob0[s]
                    ge = GATE_EVERY.get(layer, 1)
                    gate_n = c * (NG // ge) + gate0[s]
                    for j in range(J):
                        dst = hid[:, j % HID, :]
                        hid_free = n0 + (j - behind(j, J, HID) + 1 + CREDIT)
                        u, g = PS[:, 2 + j % 2, :], actb[:, j % 2, :]
                        dve.wait_ge(act_done, n0 + (j + 1 + CREDIT))
                        dve.wait_ge(u_ready, n0 + (j + 1))
                        vj = vb2[:, j % 2, :]
                        dve.wait_ge(hid_ready, n0 + (j - behind(j, J, 2) + 1 + CREDIT))
                        if layer == 3:
                            v.tensor_scalar(vj, u, 0.0, smallc("f3_val", 1), ALU.max, ALU.mult).then_inc(v_ready, 1)
                            dve.wait_ge(v_ready, v0 + (j + 1))
                            dve.wait_ge(y_added, hid_free)
                            v.scalar_tensor_tensor(out=dst, in0=g, scalar=smallc("f3_val", 0), in1=vj,
                                                   op0=ALU.mult, op1=ALU.add).then_inc(hid_ready, 1)
                        else:
                            gated = j < NG
                            if not gated:
                                dve.wait_ge(y_added, hid_free)
                            res = vj if gated else dst
                            if layer < 2:
                                ins = v.scalar_tensor_tensor(out=res, in0=u, scalar=smallc(f"bu{layer}", j), in1=g,
                                                             op0=ALU.add, op1=ALU.mult)
                            else:
                                ins = v.tensor_tensor(res, u, g, ALU.mult)
                            ins.then_inc(v_ready if gated else hid_ready, 1)
                            if gated:
                                dve.wait_ge(v_ready, v0 + (j + 1))
                                dve.wait_ge(gate_ready, gate_n + (j // ge + 1))
                                dve.wait_ge(y_added, hid_free)
                                v.tensor_tensor(dst, PS[:, 4, :], vj, ALU.mult).then_inc(hid_ready, 1)
                        for part in range(6):
                            if SLOTS[layer][part] == j:
                                if not last:
                                    prologue(s, c + 1, part)
                                elif nxt_ffn:
                                    prologue(s + 1, 0, part)
                    if layer < 2:
                        dve.wait_ge(y_final, c + (ffn_i[s] * B + 1))
                    else:
                        dve.wait_ge(y_added, n0 + (J + CREDIT))
                    bias = sv[:, 50 + layer:51 + layer] if layer < 2 else 0.0
                    v.tensor_scalar(fin[:, :], PS[:, 5, :], 0.5, bias, ALU.mult, ALU.add).then_inc(fin_ready, 1)
                    dve.wait_ge(fin_ready, c + (ffn_i[s] * B + 2))
                    v.tensor_tensor(X[:, chunk(c)], X[:, chunk(c)], fin[:, :], ALU.add).then_inc(x_ready, 1)

                loop(dve, body, True)

            def mix0(c, s):
                p, a, d = mixes[0]

                def need(name):
                    dve.wait_ge(d.sem, d.value(c, name))

                prologue(s, c, 1)
                xcp, vv, lv, dt, dx, cs, sz, xs = (padded(0), tile(8), tile(9), tile(10), vb[:, :], tile(7), tile(2), tile(3))
                cw = [smallc("a0_cw", i) for i in range(3)]
                dve.wait_ge(a.sem, a.value(c, "xcp"))
                v.tensor_scalar(fin[:, :], xcp[:, 0:T], cw[0], None, ALU.mult).then_inc(d.mark("c0"), 1)
                for i in (1, 2):
                    need(f"c{i - 1}")
                    v.scalar_tensor_tensor(out=fin[:, :], in0=xcp[:, i:T + i], scalar=cw[i], in1=fin[:, :],
                                           op0=ALU.mult, op1=ALU.add).then_inc(d.mark(f"c{i}"), 1)
                dve.wait_ge(a.sem, a.value(c, "lv"))
                v.scalar_tensor_tensor(out=fin[:, :], in0=vv, scalar=0.0, in1=lv, op0=ALU.max, op1=ALU.add)\
                    .then_inc(d.mark("dt0"), 1)
                need("dt0")
                v.tensor_scalar(dt, fin[:, :], 1e-5, None, ALU.add).then_inc(d.mark("dt"), 1)
                need("dt")
                v.tensor_tensor(dx, dt, xs, ALU.mult).then_inc(d.mark("dx"), 1)
                need("dx")
                for n in range(NS):
                    dve.wait_ge(p.sem, p.value(c, f"bp{n}"))
                    v.tensor_tensor(hid[:, n % 2, :], PS[:, 2 + n % 2, :], dx, ALU.mult).then_inc(d.mark(f"bx{n}"), 1)
                    dve.wait_ge(a.sem, a.value(c, f"Ad{n}"))
                    need(f"bx{n}")
                    if n >= 2:
                        dve.wait_ge(p.sem, p.value(c, f"ss{n - 2}"))
                    v.tensor_tensor_scan(tile(12 + n % 2), tile(14 + n % 2), hid[:, n % 2, :], 0.0, ALU.mult, ALU.add)\
                        .then_inc(d.mark(f"s{n}"), 1)
                dve.wait_ge(p.sem, p.value(c, f"ss{NS - 1}"))
                v.tensor_tensor(fin[:, :], PS[:, 0, :], cs, ALU.mult).then_inc(d.mark("cs"), 1)
                need("cs")
                v.scalar_tensor_tensor(out=tile(6), in0=xs, scalar=smallc("a0_d"), in1=fin[:, :],
                                       op0=ALU.mult, op1=ALU.add).then_inc(d.mark("y"), 1)
                dve.wait_ge(p.sem, p.value(c, "out"))
                v.tensor_tensor(fin[:, :], PS[:, 1, :], sz, ALU.mult).then_inc(d.mark("o"), 1)
                need("o")
                v.tensor_tensor(X[:, chunk(c)], X[:, chunk(c)], fin[:, :], ALU.add).then_inc(x_ready, 1)

            def mix1(c, s):
                p, a, d = mixes[1]

                def need(name):
                    dve.wait_ge(d.sem, d.value(c, name))

                prologue(s, c, 1)
                xv, sg, pt, pw = tile(12), tile(13), tile(14), tile(14)
                for b, (z, dst) in enumerate((("v", xv), ("g", sg), ("s", pt))):
                    zp = padded(2 * b)
                    dve.wait_ge(a.sem, a.value(c, f"z{z}p"))
                    v.tensor_scalar(dst, zp[:, 0:T], smallc(f"a1_cw{z}", 0), smallc(f"a1_cb{z}"), ALU.mult, ALU.add)\
                        .then_inc(d.mark(f"{z}0"), 1)
                    for i in range(1, 4):
                        need(f"{z}{i - 1}")
                        v.scalar_tensor_tensor(out=dst, in0=zp[:, i:T + i], scalar=smallc(f"a1_cw{z}", i), in1=dst,
                                               op0=ALU.mult, op1=ALU.add).then_inc(d.mark(f"{z}{i}"), 1)
                need("s3")
                v.tensor_scalar(pt, pt, smallc("a1_score"), 20.0, ALU.mult, ALU.min).then_inc(d.mark("cl0"), 1)
                need("cl0")
                v.tensor_scalar(pt, pt, -20.0, None, ALU.max).then_inc(d.mark("cl1"), 1)
                dve.wait_ge(a.sem, a.value(c, "p"))
                v.tensor_tensor(pw, pt, small("time"), ALU.mult).then_inc(d.mark("pw"), 1)
                v.tensor_scalar(fin[:, :], xv, sv[:, 40:41], sv[:, 37:38], ALU.mult, ALU.add).then_inc(d.mark("a"), 1)
                need("a")
                v.tensor_tensor(fin[:, :], fin[:, :], xv, ALU.mult).then_inc(d.mark("m"), 1)
                need("m")
                v.scalar_tensor_tensor(out=tile(15), in0=fin[:, :], scalar=sv[:, 36:37], in1=pw, op0=ALU.add,
                                       op1=ALU.mult).then_inc(d.mark("pwp"), 1)
                v.tensor_tensor_scan(DEN, ones[:, :], pw, 0.0, ALU.mult, ALU.add).then_inc(d.mark("den"), 1)
                pwp = tile(15)
                phi, k = actb[:, 1, :], hid[:, 2, :]
                need("pwp")
                for m in range(M1):
                    v.tensor_scalar(phi, xv, smallc("a1_theta", m), None, ALU.mult).then_inc(d.mark(f"phi{m}"), 1)
                    need(f"phi{m}")
                    v.tensor_scalar(k, phi, INV_2PI, ROUND, ALU.mult, ALU.add).then_inc(d.mark(f"q{m}"), 1)
                    need(f"q{m}")
                    v.tensor_scalar(k, k, ROUND, None, ALU.subtract).then_inc(d.mark(f"k{m}"), 1)
                    need(f"k{m}")
                    v.scalar_tensor_tensor(out=phi, in0=k, scalar=-TWO_PI_HI, in1=phi, op0=ALU.mult, op1=ALU.add)\
                        .then_inc(d.mark(f"r1_{m}"), 1)
                    need(f"r1_{m}")
                    v.scalar_tensor_tensor(out=phi, in0=k, scalar=-TWO_PI_LO, in1=phi, op0=ALU.mult, op1=ALU.add)\
                        .then_inc(d.mark(f"r2_{m}"), 1)
                    need(f"r2_{m}")
                    if m:
                        dve.wait_ge(a.sem, a.value(c, f"sin{m - 1}"))
                    v.tensor_scalar(vb[:, :], phi, PI_IN, -PI_IN, ALU.min, ALU.max).then_inc(d.mark(f"r{m}"), 1)
                    for part, src, dst in (("re", hid[:, 1, :], fin[:, :]), ("im", hid[:, 0, :], vb2[:, 1, :])):
                        dve.wait_ge(a.sem, a.value(c, f"cos{m}"))
                        v.tensor_tensor(dst, pwp, src, ALU.mult).then_inc(d.mark(f"{part}{m}"), 1)
                        need(f"{part}{m}")
                        if m >= 2:
                            dve.wait_ge(a.sem, a.value(c, f"sq{part}{m - 2}"))
                            dve.wait_ge(p.sem, p.value(c, f"y{part}{m - 2}"))
                        v.tensor_tensor_scan(NUM[part][m % 2], ones[:, :], dst, 0.0, ALU.mult, ALU.add)\
                            .then_inc(d.mark(f"n{part}{m}"), 1)
                v.tensor_scalar(actb[:, 0, :], DEN, 1e-4, None, ALU.max).then_inc(d.mark("dmax"), 1)
                need("dmax")
                v.reciprocal(actb[:, 1, :], actb[:, 0, :]).then_inc(d.mark("inv"), 1)
                need("inv")
                v.tensor_tensor(actb[:, 0, :], actb[:, 1, :], actb[:, 1, :], ALU.mult).then_inc(d.mark("i2"), 1)
                need("i2")
                dve.wait_ge(p.sem, p.value(c, f"qim{M1 - 1}"))
                v.tensor_tensor(vb[:, :], PS[:, 4, :], actb[:, 0, :], ALU.mult).then_inc(d.mark("t"), 1)
                dve.wait_ge(a.sem, a.value(c, "rs"))
                v.tensor_tensor(vb[:, :], vb[:, :], actb[:, 1, :], ALU.mult).then_inc(d.mark("f"), 1)
                need("f")
                v.tensor_tensor(vb[:, :], vb[:, :], sg, ALU.mult).then_inc(d.mark("f2"), 1)
                need("f2")
                v.tensor_tensor(fin[:, :], PS[:, 3, :], vb[:, :], ALU.mult).then_inc(d.mark("yy"), 1)
                dve.wait_ge(p.sem, p.value(c, "out"))
                v.tensor_tensor(X[:, chunk(c)], PS[:, 5, :], X[:, chunk(c)], ALU.add).then_inc(x_ready, 1)

            def mix2(c, s):
                p, a, d = mixes[2]
                prologue(s, c, 1)
                dve.wait_ge(p.sem, p.value(c, "out"))
                v.tensor_tensor(X[:, chunk(c)], PS[:, 4, :], X[:, chunk(c)], ALU.add).then_inc(x_ready, 1)

            def mix3(c, s):
                p, a, d = mixes[3]

                def need(name):
                    dve.wait_ge(d.sem, d.value(c, name))

                def tt(name, out, i0, i1, op):
                    v.tensor_tensor(out, i0, i1, op).then_inc(d.mark(name), 1)

                def ts(name, out, i0, s1, s2, o0, o1=None):
                    if o1 is None:
                        v.tensor_scalar(out, i0, s1, None, o0).then_inc(d.mark(name), 1)
                    else:
                        v.tensor_scalar(out, i0, s1, s2, o0, o1).then_inc(d.mark(name), 1)

                def stt(name, out, i0, sc, i1, o0, o1):
                    v.scalar_tensor_tensor(out=out, in0=i0, scalar=sc, in1=i1, op0=o0, op1=o1).then_inc(d.mark(name), 1)

                prologue(s, c, 1)
                hp = M3["h"]
                dve.wait_ge(a.sem, a.value(c, "rstd1"))
                tt("n1", fin[:, :], PS[:, 6, :], rstd[:, :], ALU.mult)
                need("n1")
                ts("h1", hp[:, 1:T + 1], fin[:, :], smallc("a3_g1"), smallc("a3_b1"), ALU.mult, ALU.add)
                need("h1")
                tt("d1", fin[:, :], hp[:, 1:T + 1], hp[:, 0:T], ALU.subtract)
                need("d1")
                for z in "kvr":
                    stt(f"x{z}", M3[z], fin[:, :], smallc(f"a3_m{z}"), hp[:, 0:T], ALU.mult, ALU.add)
                dve.wait_ge(a.sem, a.value(c, "ks"))
                v.tensor_tensor_scan(MX[:, 1:T + 1], ones[:, :], K_, NEG_HUGE, ALU.mult, ALU.max).then_inc(d.mark("cm"), 1)
                need("cm")
                tt("da", AB[:, 0:T], MX[:, 0:T], MX[:, 1:T + 1], ALU.subtract)
                tt("db", AB[:, T:2 * T], K_, MX[:, 1:T + 1], ALU.subtract)
                dve.wait_ge(a.sem, a.value(c, "ab"))
                v.tensor_tensor_scan(S_, AB[:, 0:T], AB[:, T:2 * T], 0.0, ALU.mult, ALU.add).then_inc(d.mark("S"), 1)
                dve.wait_ge(a.sem, a.value(c, "lnS"))
                tt("pp", PP[:, 1:T + 1], MX[:, 1:T + 1], LS, ALU.add)
                need("pp")
                tt("dl", fin[:, :], PP[:, 0:T], K_, ALU.subtract)
                need("dl")
                ts("al", AL, fin[:, :], 0.0, None, ALU.min)
                ts("nb", BE, fin[:, :], -1.0, 0.0, ALU.mult, ALU.min)
                dve.wait_ge(a.sem, a.value(c, "eb"))
                tt("bv", BV, BE, V_, ALU.mult)
                need("bv")
                v.tensor_tensor_scan(AA[:, 1:T + 1], AL, BV, 0.0, ALU.mult, ALU.add).then_inc(d.mark("aa"), 1)
                stt("dw", fin[:, :], K_, smallc("a3_first"), PP[:, 0:T], ALU.add, ALU.subtract)
                need("dw")
                ts("aw", AW, fin[:, :], -1.0, 0.0, ALU.mult, ALU.min)
                ts("nw", NW, fin[:, :], 0.0, None, ALU.min)
                dve.wait_ge(a.sem, a.value(c, "e2"))
                need("aa")
                tt("n0", BV, AW, AA[:, 0:T], ALU.mult)
                tt("n1b", BE, NW, V_, ALU.mult)
                need("n1b")
                tt("num", BV, BV, BE, ALU.add)
                tt("den", AW, AW, NW, ALU.add)
                need("den")
                ts("deni", AW, AW, 1e-8, None, ALU.add)
                need("deni")
                v.reciprocal(NW, AW).then_inc(d.mark("rden"), 1)
                need("rden")
                tt("o", BV, BV, NW, ALU.mult)
                need("o")
                dve.wait_ge(a.sem, a.value(c, "sr"))
                tt("ro", BV, BV, R_, ALU.mult)
                need("ro")
                tt("x1", M3["x1"], BV, hs[:, :], ALU.add)
                dve.wait_ge(a.sem, a.value(c, "rstd2"))
                tt("n2", fin[:, :], PS[:, 6, :], rstd[:, :], ALU.mult)
                need("n2")
                ts("h2", hp[:, 1:T + 1], fin[:, :], smallc("a3_g2"), smallc("a3_b2"), ALU.mult, ALU.add)
                need("h2")
                tt("d2", fin[:, :], hp[:, 1:T + 1], hp[:, 0:T], ALU.subtract)
                need("d2")
                stt("xkc", M3["kc"], fin[:, :], smallc("a3_cmk"), hp[:, 0:T], ALU.mult, ALU.add)
                stt("xrc", M3["rc"], fin[:, :], smallc("a3_cmr"), hp[:, 0:T], ALU.mult, ALU.add)
                dve.wait_ge(p.sem, p.value(c, "vc"))
                dve.wait_ge(a.sem, a.value(c, "src"))
                tt("res", fin[:, :], PS[:, 5, :], RC, ALU.mult)
                need("res")
                tt("acc", fin[:, :], fin[:, :], M3["x1"], ALU.add)
                need("acc")
                v.tensor_tensor(X[:, chunk(c)], X[:, chunk(c)], fin[:, :], ALU.add).then_inc(x_ready, 1)

            for i, val in enumerate((LN_EPS, 1e-8, HALF_PI, 1.0)):
                v.memset(epsc[:, i:i + 1], val).then_inc(consts, 1)
            v.memset(ones[:, :], 1.0).then_inc(consts, 1)
            v.memset(AA[:, :], 0.0)
            v.memset(GB[:, :], 0.0)
            v.memset(ws[:, :, :], 0.0).then_inc(consts, 1)
            dve.sem_inc(hid_ready, CREDIT)
            dve.sem_inc(y_added, CREDIT)
            dve.sem_inc(fin_ready, 1)
            dve.wait_ge(consts, 6)
            dve.wait_ge(s_small, 48)
            p, a, d = prep

            def need(name):
                dve.wait_ge(d.sem, d.value(0, name))

            dve.wait_ge(a.sem, a.value(0, "sl_l"))
            v.tensor_scalar(sv[:, 0:NS], sv[:, 0:NS], -1.0, None, ALU.mult).then_inc(d.mark("naexp"), 1)
            v.tensor_scalar(sv[:, 23:24], smallc("a1_slope"), 0.0, None, ALU.max).then_inc(d.mark("sl_n"), 1)
            need("sl_n")
            v.tensor_tensor(sv[:, 25:26], sv[:, 23:24], sv[:, 22:23], ALU.add).then_inc(d.mark("sl_s"), 1)
            need("sl_s")
            v.tensor_scalar(sv[:, 24:25], sv[:, 25:26], -1.0, None, ALU.mult).then_inc(d.mark("sl_neg"), 1)
            v.tensor_reduce(sv[:, 26:27], small("a1_deriv"), AX, ALU.max).then_inc(d.mark("dm"), 1)
            need("dm")
            v.tensor_scalar(sv[:, 28:31], small("a1_deriv"), sv[:, 26:27], None, ALU.subtract).then_inc(d.mark("dd"), 1)
            dve.wait_ge(a.sem, a.value(0, "de"))
            v.tensor_reduce(sv[:, 34:35], sv[:, 31:34], AX, ALU.add).then_inc(d.mark("dsum"), 1)
            need("dsum")
            v.reciprocal(sv[:, 35:36], sv[:, 34:35]).then_inc(d.mark("drec"), 1)
            need("drec")
            v.tensor_scalar(sv[:, 36:39], sv[:, 31:34], sv[:, 35:36], None, ALU.mult).then_inc(d.mark("dw"), 1)
            need("dw")
            v.tensor_scalar(sv[:, 40:41], sv[:, 38:39], -1.0, None, ALU.mult).then_inc(d.mark("ndw2"), 1)
            for part, gain in (("re", "a1_nre"), ("im", "a1_nim")):
                for m in range(M1):
                    w = small(f"a1_{part}")[:, m * P:(m + 1) * P]
                    last = v.tensor_scalar(w, w, smallc(gain, m), None, ALU.mult)
            last.then_inc(d.mark("blk"), 1)
            v.tensor_copy(sv[:, 42:44], idxi[:, :]).then_inc(d.mark("idxf"), 1)
            need("idxf")
            for k in range(K3):
                v.tensor_tensor(sv[:, 44 + k:45 + k], sv[:, 42 + k:43 + k], smallc("f3_expert"), ALU.is_equal)\
                    .then_inc(d.mark(f"oh{k}"), 1)

            def prep_l3():
                dve.wait_ge(s_w3, 16)
                need("oh1")
                for k in range(K3):
                    v.tensor_scalar(w3(f"weff{k}", F3), w3("B", F3), sv[:, 44 + k:45 + k], None, ALU.mult)\
                        .then_inc(d.mark(f"ba{k}"), 1)
                for k in range(K3):
                    dve.wait_ge(prep[0].sem, prep[0].value(0, f"weff{k}"))
                    v.tensor_tensor(w3(f"weff{k}", F3), PS[:, 6 + k, :], w3("wi", F3), ALU.add)\
                        .then_inc(d.mark(f"wi{k}"), 1)

            for i in range(2):
                v.tensor_scalar(sv[:, 50 + i:51 + i], smallc(f"by{i}"), 0.5, None, ALU.mult).then_inc(consts, 1)
            dve.wait_ge(consts, 8)
            for s, (kind, layer) in enumerate(STAGES[:stop_after]):
                if s == 9:
                    prep_l3()
                if kind == "ffn":
                    ffn(s, layer)
                    continue
                if layer == 0:
                    v.memset(padded(0)[:, 0:1], 0.0)
                    v.memset(padded(0)[:, T + 1:T + 2], 0.0).then_inc(consts, 1)
                    dve.wait_ge(consts, 9)
                if layer == 1:
                    for b in range(3):
                        last = v.memset(padded(2 * b)[:, 0:3], 0.0)
                    last.then_inc(consts, 1)
                    dve.wait_ge(consts, 10)
                if layer == 3:
                    v.memset(M3["h"][:, 0:1], 0.0)
                    v.memset(MX[:, 0:1], NEG_HUGE)
                    v.memset(PP[:, 0:1], NEG_HUGE)
                    v.memset(AA[:, 0:1], 0.0).then_inc(consts, 1)
                    dve.wait_ge(consts, 11)
                with dve.Fori(0, B) as c:
                    (mix0, mix1, mix2, mix3)[layer](c, s)


_OUTS = [((8, 512, 128), "float32")]


def kernel(**inputs):
    import numpy as np
    import concourse.bacc as _bacc
    from concourse import mybir as _mybir
    from concourse.bass_utils import run_bass_kernel_spmd as _run

    f32 = np.float32
    get = {k: np.asarray(v) for k, v in inputs.items()}

    def T_(a):
        return np.ascontiguousarray(a.T)

    def wide(a, cols=P):
        out = np.zeros((P, cols), f32)
        out[:a.shape[0], :a.shape[1]] = a
        return out

    sm = {}
    eye = np.eye(P, dtype=f32)
    sm["center"] = eye - f32(1.0 / P)
    sm["avg"] = np.full((P, P), 1.0 / P, f32)
    sm["ident"] = eye
    w_in, w_x = get["L0_attn_W_in"], get["L0_attn_W_x"]
    sm["a0_xc"], sm["a0_z"] = w_in[:P].T, w_in[P:].T
    sm["a0_dtp"], sm["a0_cp"] = w_x[:R0].T, w_x[R0 + NS:].T
    sm["a0_dt"] = wide(get["L0_attn_W_dt"].T)
    sm["a0_c"] = wide(get["L0_attn_W_C"].T)
    sm["a0_out"] = get["L0_attn_W_out"].T
    w_p = get["L1_attn_in_proj_w"]
    sm["a1_v"], sm["a1_g"] = w_p[:, :P], w_p[:, P:2 * P]
    sm["a1_s"] = np.repeat(w_p[:, 2 * P:], H1, axis=1)
    for name, src in (("a1_re", "L1_attn_W_re"), ("a1_im", "L1_attn_W_im")):
        w = get[src].reshape(H1, M1, H1)
        blocks = np.zeros((M1, P, P), f32)
        for m in range(M1):
            for k in range(K1):
                blocks[m, H1 * k:H1 * k + H1, H1 * k:H1 * k + H1] = w[:, m, :]
        sm[name] = blocks.transpose(1, 0, 2).reshape(P, M1 * P)
    sm["a1_sum"] = np.kron(np.eye(K1, dtype=f32), np.ones((H1, H1), f32))
    sm["a1_out"] = get["L1_attn_out_proj_w"]
    t = np.arange(T, dtype=f32)
    sm["time"] = np.where(np.arange(P)[:, None] < (K1 - A1) * H1, (T - 1 - t)[None, :], t[None, :]).astype(f32)
    sm["a2_kv"] = np.concatenate([get["L2_attn_wv"].T, get["L2_attn_wk"].T], axis=1)
    sm["a2_q"] = np.concatenate([np.zeros((P - D2, P), f32), get["L2_attn_wq"]])
    sm["a2_o"] = wide(get["L2_attn_wo"].T)
    g0 = get["L0_ffn_gate_w"].T
    sm["gate0"] = np.concatenate([g0, g0], axis=1)
    sm["gate1"], sm["gate2"] = get["L1_ffn_Wr"], get["L2_ffn_gate_w"]
    sm["b2_0"] = wide(np.concatenate([get["L0_ffn_b2"]] * 3))
    sm["b2_1"] = wide(np.concatenate([get["L1_ffn_be2"]] * 3))
    sm["rank"] = np.broadcast_to(np.arange(E0, 0, -1, dtype=f32), (P, E0))

    def col(a):
        a = a.reshape(-1, 1)
        return wide(a, 1)

    be1, bs1 = get["L1_ffn_be1"], get["L1_ffn_bs1"]
    sm["bg0"] = np.concatenate([get["L0_ffn_b1"].reshape(-1), get["L0_ffn_sb1"]]).reshape(-1, P).T
    sm["bu0"] = np.concatenate([get["L0_ffn_b3"].reshape(-1), get["L0_ffn_sb3"]]).reshape(-1, P).T
    sm["bg1"] = np.concatenate([be1[:, F1:].reshape(-1), bs1[SH1:]]).reshape(-1, P).T
    sm["bu1"] = np.concatenate([be1[:, :F1].reshape(-1), bs1[:SH1]]).reshape(-1, P).T
    sm["by0"], sm["by1"] = col(get["L0_ffn_sb2"]), col(get["L1_ffn_bs2"])
    sm["gb0"] = col(np.concatenate([get["L0_ffn_expert_bias"], np.zeros(E0, f32)]))
    sm["gb1"] = col(get["L1_ffn_br"])
    sm["a0_cw"] = get["L0_attn_conv_w"]
    sm["a0_bdt"], sm["a0_alog"], sm["a0_d"] = col(get["L0_attn_b_dt"]), get["L0_attn_A_log"], col(get["L0_attn_D_param"])
    cw, cb = get["L1_attn_conv_w"][:, 0, :].T, get["L1_attn_conv_b"]
    sm["a1_cwv"], sm["a1_cwg"], sm["a1_cws"] = cw[:P], cw[P:2 * P], np.repeat(cw[2 * P:], H1, axis=0)
    sm["a1_cbv"], sm["a1_cbg"], sm["a1_cbs"] = col(cb[:P]), col(cb[P:2 * P]), col(np.repeat(cb[2 * P:], H1))
    sm["a1_theta"] = get["L1_attn_theta"].reshape(P, M1)
    sm["a1_slope"] = col(np.repeat(np.concatenate([get["L1_attn_decay_slopes"], get["L1_attn_anchor_slopes"]]), H1))
    sm["a1_score"] = col(np.repeat(get["L1_attn_score_scale"], H1))
    sm["a1_deriv"] = np.broadcast_to(get["L1_attn_deriv_logits"], (P, 3))
    ns = get["L1_attn_norm_scale"].reshape(2, H1, M1)
    sm["a1_nre"], sm["a1_nim"] = np.tile(ns[0], (K1, 1)), np.tile(ns[1], (K1, 1))
    for name, src in (("first", "time_first"), ("g1", "ln1_g"), ("b1", "ln1_b"), ("g2", "ln2_g"), ("b2", "ln2_b"),
                      ("mk", "mix_k"), ("mv", "mix_v"), ("mr", "mix_r"), ("cmk", "cmix_k"), ("cmr", "cmix_r")):
        sm[f"a3_{name}"] = col(get[f"L3_attn_{src}"])
    sm["f3_val"] = np.broadcast_to(get["L3_ffn_top_k_values"], (P, K3))
    sm["f3_expert"] = col(np.repeat(np.arange(E3, dtype=f32), R3))
    small = np.concatenate([sm[name].reshape(P, n) for name, n in SMALL], axis=1)

    def rows(a):
        return a.reshape(-1, P, D).transpose(1, 0, 2).reshape(P, -1)

    def pad(a, n):
        return np.concatenate([a, np.zeros((n - a.shape[0],) + a.shape[1:], f32)])

    w0 = np.concatenate([
        np.concatenate([get["L0_ffn_w1"].reshape(-1, D), get["L0_ffn_sw1"]]).T,
        np.concatenate([get["L0_ffn_w3"].reshape(-1, D), get["L0_ffn_sw3"]]).T,
        rows(np.concatenate([get["L0_ffn_w2"].transpose(0, 2, 1).reshape(-1, D), get["L0_ffn_sw2"].T])),
        np.repeat(w_x[R0:R0 + NS].T, P, axis=1)], axis=1)
    we1, ws1 = get["L1_ffn_We1"], get["L1_ffn_Ws1"]
    w1 = np.concatenate([
        we1[:, :, F1:].transpose(1, 0, 2).reshape(D, -1), ws1[:, SH1:],
        we1[:, :, :F1].transpose(1, 0, 2).reshape(D, -1), ws1[:, :SH1],
        rows(np.concatenate([get["L1_ffn_We2"].reshape(-1, D), get["L1_ffn_Ws2"]]))], axis=1)
    w2 = np.concatenate([
        get["L2_ffn_Wg"].transpose(1, 0, 2).reshape(D, -1), wide(get["L2_ffn_Sg"], 2 * P),
        get["L2_ffn_Wu"].transpose(1, 0, 2).reshape(D, -1), wide(get["L2_ffn_Su"], 2 * P),
        rows(np.concatenate([get["L2_ffn_Wd"].reshape(-1, D), pad(get["L2_ffn_Sd"], 2 * P)]))], axis=1)
    w3 = np.concatenate([
        get["L3_ffn_wi_w"].T, rows(get["L3_ffn_wo_w"].T), wide(get["L3_ffn_lora_As"].reshape(-1, D), F3),
        get["L3_ffn_lora_Bs"].transpose(0, 2, 1).reshape(P, F3),
        get["L3_attn_Wk_t"].T, get["L3_attn_Wv_t"].T, get["L3_attn_Wr_t"].T, get["L3_attn_Wr_c"].T,
        get["L3_attn_Wk_c"].T, rows(get["L3_attn_Wv_c"].T)], axis=1)

    def spread(experts, owner):
        one = (np.arange(experts)[:, None] == owner[None, :]).astype(f32)
        return np.concatenate([one, one, one, np.zeros((P - 3 * experts, owner.size), f32)])

    sel = np.concatenate([
        spread(E0, np.arange(E0 * F0) // F0),
        spread(E1, np.repeat(np.arange(E1), P)),
        spread(E2, np.arange(E2 * F2) // F2)], axis=1).astype(np.dtype("bfloat16"))
    idx = np.ascontiguousarray(np.broadcast_to(get["L3_ffn_top_k_indices"], (P, K3)))
    x = np.ascontiguousarray(get["L0_attn_x"].reshape(N, D).T)

    arrays = {"in_x": x, "in_small": small, "in_w0": w0, "in_w1": w1, "in_w2": w2, "in_w3": w3, "in_sel": sel,
              "in_idx": idx}
    arrays = {k: np.ascontiguousarray(v) for k, v in arrays.items()}
    nc = _bacc.Bacc("TRN2", target_bir_lowering=False, num_devices=1, dynamic_dma_scratch_size=1024)
    args = [nc.dram_tensor(k, a.shape, _mybir.dt.from_np(a.dtype), kind="ExternalInput").ap()
            for k, a in arrays.items()]
    res = nc.dram_tensor("out_0_dram", (P, N), _mybir.dt.float32, kind="ExternalOutput").ap()
    build(nc, *args, res)
    r = _run(nc, [arrays], core_ids=[0])
    return np.ascontiguousarray(r.results[0]["out_0_dram"].T).reshape(B, T, D)
```

```python
from contextlib import ExitStack

import concourse.bass as bass
from concourse import mybir

F32 = mybir.dt.float32
BF16 = mybir.dt.bfloat16
F32R = mybir.dt.float32r
I32 = mybir.dt.int32
ALU = mybir.AluOpType
ACT = mybir.ActivationFunctionType
AX = mybir.AxisListType.X

P = 128
B, T, D = 8, 512, 128
N = B * T
TILES = T // P
LN_EPS = 1e-5
NEG_HUGE = -3.0e38

E0, F0, SH0 = 16, 64, 128
E1, F1, SH1, TAU = 12, 384, 256, 1.5
E2, F2, SH2 = 8, 352, 176
E3, F3, R3, K3 = 8, 512, 16, 2
NS, R0 = 16, 64
K1, H1, M1, A1 = 32, 4, 4, 4
D2 = 64

JOBS = {0: E0 * F0 // P + SH0 // P, 1: (E1 * F1 + SH1) // P, 2: E2 * F2 // P + 2, 3: F3 // P}
GATED = {0: E0 * F0 // P, 1: E1 * F1 // P, 2: E2 * F2 // P, 3: 0}
GATE_EVERY = {0: 1, 1: F1 // P, 2: 1}
EXPERTS = {0: E0, 1: E1, 2: E2}
LAG = 2
HID = 3
CREDIT = 3
X0 = 1
NORM_SET = "natural_log_exp_and_others"
SILU_SET = "silu_and_others"

SMALL = [
    ("center", P), ("avg", P), ("ident", P),
    ("a0_xc", P), ("a0_z", P), ("a0_xd", P), ("a0_dt", P),
    ("a0_c", P), ("a0_out", P),
    ("a1_v", P), ("a1_g", P), ("a1_s", P), ("a1_re", M1 * P), ("a1_im", M1 * P), ("a1_sum", P),
    ("a1_out", P), ("time", T),
    ("a2_kv", P), ("a2_q", P), ("a2_o", P),
    ("gate0", 2 * E0), ("gate1", E1), ("gate2", E2), ("b2_0", P), ("b2_1", P),
    ("rank", E0),
    ("bg0", JOBS[0]), ("bu0", JOBS[0]), ("bg1", JOBS[1]), ("bu1", JOBS[1]),
    ("by0", 1), ("by1", 1), ("gb0", 1), ("gb1", 1),
    ("a0_cw", 3), ("a0_bdt", 1), ("a0_alog", NS), ("a0_d", 1),
    ("a1_cwv", 4), ("a1_cwg", 4), ("a1_cws", 4), ("a1_cbv", 1), ("a1_cbg", 1), ("a1_cbs", 1),
    ("a1_theta", M1), ("a1_slope", 1), ("a1_score", 1), ("a1_deriv", 3), ("a1_nre", M1), ("a1_nim", M1),
    ("a3_first", 1), ("a3_g1", 1), ("a3_b1", 1), ("a3_g2", 1), ("a3_b2", 1),
    ("a3_mk", 1), ("a3_mv", 1), ("a3_mr", 1), ("a3_cmk", 1), ("a3_cmr", 1),
    ("f3_val", K3), ("f3_expert", 1),
]


def offsets():
    at, out = 0, {}
    for name, n in SMALL:
        out[name] = (at, n)
        at += n
    return out, at


OFF, SMALL_COLS = offsets()

W0_COLS = 3 * JOBS[0] * P
W2_COLS = 2 * JOBS[2] * P
W2_PIECES = W2_COLS // T
L3_AT = {"wi": 0, "wo": F3, "A": 2 * F3, "B": 3 * F3, "k": 4 * F3, "v": 4 * F3 + P, "r": 4 * F3 + 2 * P,
         "rc": 4 * F3 + 3 * P, "kc": 5 * F3, "vc": 6 * F3, "weff0": 7 * F3, "weff1": 8 * F3}
W3_COLS = L3_AT["weff0"]

INV_2PI = 0.15915494309189535
TWO_PI_HI = 6.28125
TWO_PI_LO = 0.0019353071795864769
ROUND = 12582912.0
PI_IN = 3.1415925
HALF_PI = 1.5707963267948966


class Steps:

    def __init__(self, sem, names, base):
        self.sem, self.names, self.base, self.n, self.at = sem, names, base, len(names), 0

    def value(self, c, name):
        return c * self.n + (self.base + self.names.index(name) + 1)

    def before(self, c):
        return c * self.n + self.base

    def mark(self, name):
        assert self.names[self.at % self.n] == name, (self.names[self.at % self.n], name)
        self.at += 1
        return self.sem


def behind(j, jobs, buffers):
    for k in range(1, 2 * jobs + buffers):
        if (j - k) % jobs % buffers == j % buffers if j - k < 0 else (j - k) % buffers == j % buffers:
            return k
    raise ValueError


def pro_names(kind):
    pe, act, dve = ["center", "var"], ["sq", "lnv", "rstd"], ["h"] + (["hh", "hl"] if kind == 2 else [])
    if kind in EXPERTS:
        pe += ["logits", "tok", "back"]
        act += ["gexp"]
        dve += ["lg", "ltok", "m1", "eq1", "rk1", "t1", "oh1", "l2", "m2", "eq2", "rk2", "t2", "oh2", "mask"]
        dve += ["s1p", "srec"] if kind == 0 else ["arg"]
        dve += ["ms", "sum", "sume", "rec", "w", "wh", "whf", "wr", "wm", "wmf", "wl", "gf", "gb"]
    return pe, act, dve


SPARE = {0: 3, 1: 3, 2: 6, 3: 0}
STAGES = [(k, l) for l in range(4) for k in ("ffn", "mix", "ffn")]


def a0_names():
    front = (["center0", "var0", "xc", "z", "xd", "dtpre", "C"],
             ["sq0", "lnv0", "rstd0", "xcp", "sz", "xs", "xds", "v", "av", "ev", "lv", "Cs"],
             ["h0", "c0", "c1", "c2", "bh", "br", "bm", "bt", "bl", "dt0", "dt", "dx"])
    back = ([f"bp{n}" for n in range(NS)] + ["out"],
            [f"Ad{n}" for n in range(NS)],
            [f"{x}{n}" for n in range(NS) for x in ("bx", "s")] + ["cs", "y", "o"])
    return front, back


def a1_names():
    pe = ["center0", "var0", "zv", "zg", "zs"]
    for m in range(M1):
        pe += [f"yre{m}", f"yim{m}", f"qre{m}", f"qim{m}"]
    pe += ["out"]
    act = ["sq0", "lnv0", "rstd0", "zvp", "zgp", "zsp", "sg", "p"]
    for m in range(M1):
        act += [f"abs{m}", f"sin{m}", f"cos{m}", f"sqre{m}", f"sqim{m}"]
    act += ["lnq", "rs"]
    dve = ["h0"] + [f"{z}{i}" for z in "vgs" for i in range(4)]
    dve += ["cl0", "cl1", "pw", "a", "m", "pwp", "den"]
    for m in range(M1):
        dve += [f"{x}{m}" for x in ("phi", "q", "k", "r1_", "r2_", "r", "re", "nre", "im", "nim")]
    dve += ["dmax", "inv", "i2", "t", "f", "f2", "yy"]
    return pe, act, dve


def a2_names():
    return (["center0", "var0", "kv", "et", "ew", "m", "out"], ["sq0", "lnv0", "rstd0", "kvs", "ets", "ews", "ms"],
            ["h0"])


def a3_names():
    front = (["center0", "var0", "center1", "var1", "k", "v", "r"],
             ["sq0", "lnv0", "rstd0", "sq1", "lnv1", "rstd1", "ks", "vs", "sr"],
             ["h0", "n1", "h1", "d1", "xk", "xv", "xr"])
    middle = ([], ["ab", "lnS", "ea", "eb", "e1", "e2"],
              ["cm", "da", "db", "S", "pp", "dl", "al", "nb", "bv", "aa",
               "dw", "aw", "nw", "n0", "n1b", "num", "den", "deni", "rden", "o", "ro", "x1"])
    back = (["center2", "var2", "kc0", "kc1", "kc2", "kc3", "rc", "vc"],
            ["sq2", "lnv2", "rstd2", "r0", "q0", "r1", "q1", "r2", "q2", "r3", "q3", "src"],
            ["n2", "h2", "d2", "xkc", "xrc", "res", "acc"])
    return front, middle, back


NORM_PARTS = "center square - var rstd norm".split()
ROUTE_PARTS = "- - logits lg - - tok top1 top2 - gexp weights split - - - back spread".split()
MIX_PARTS = {
    1: "- -".split() + NORM_PARTS
    + "- - zvg zvg_copy zs conv_v0 - conv_v1 zs_copy conv_g0 - conv_g1 - conv_s0 - conv_s1 - clip".split()
    + "- gate pw - den - phi0 range0 -".split()
    + "sin0 re0 im0 square0 phi1 range1 - y0 q0 sin1 re1 im1 square1 phi2 range2 - y1 q1 sin2 re2 im2 square2".split()
    + "phi3 range3 - y2 q2 sin3 re3 im3 square3 - - y3 q3 inv t - - rs f - - out add".split(),
    2: "- -".split() + NORM_PARTS + "- - kv kv_copy - et et_copy - ew ew_copy - m m_copy - out add".split(),
}
FRONT = {
    0: NORM_PARTS + "xz xz_copy conv xs xd xd_copy split1 split2 soft dt".split(),
    3: NORM_PARTS + "center1 square1 var1 rstd1 shift1 mix1 kv kv_copy r r_copy".split(),
}
MIDDLE = {0: [], 3: "max ab S lnS pp eab aa w e12 num den o".split()}
BACK = {
    0: (["decay0", "decay1", "rows"] + [f"state{n}" for n in range(4)] + ["decay2"]
        + [f"state{n}" for n in range(4, 8)] + ["decay3"] + [f"state{n}" for n in range(8, NS)] + ["y", "out", "add"]),
    3: "center2 square2 var2 rstd2 shift2 mix2 kc01 q01 kc23 q23 rc rc_gate vc add".split(),
}
N_BANK, V_BANK, P_BANK, Q_BANK, R_BANK, S_BANK, S_BANKS = 0, 1, 2, 3, 4, 5, 3


G_BANK, U_BANK, GATE_BANK, Y_BANK, A_BANK, B_BANK = 0, 2, 4, 5, 6, 7
PITCH = T + 4
MT_TILES = 13


def merged(*orders):
    places = [((i + 0.5) / len(x), k, part) for k, x in enumerate(orders) for i, part in enumerate(x)]
    return [part for _, _, part in sorted(places, key=lambda place: place[:2])]


def side_parts(layer, pro, mix):
    slots = 3 * JOBS[layer]
    parts = [("pro", k) for k in pro_parts(STAGES[pro[0]][1])] if pro is not None else []
    if mix is not None:
        parts += [("mix", k) for k in MIX_PARTS[layer]]
    over = max(slots - SPARE[layer], 1)
    return [parts[min(i, over) * len(parts) // over:min(i + 1, over) * len(parts) // over] for i in range(slots)]


def pro_parts(layer):
    return NORM_PARTS + (["halves"] if layer == 2 else []) + (ROUTE_PARTS if layer in EXPERTS else [])


PREP = (["weff0", "weff1"], ["ealog", "sl_a", "sl_e", "sl_l", "tw", "de"],
        ["naexp", "sl_n", "sl_s", "sl_neg", "dm", "dd", "dsum", "drec", "dw", "ndw2", "blk",
         "idxf", "oh0", "oh1", "ba0", "ba1", "wi0", "wi1"])


def build(nc, x_in, small_in, w0_in, w1_in, w2_in, w3_in, sel_in, idx_in, out, stop_after=len(STAGES)):
    ctx = ExitStack()
    with ctx:
        def sb(name, shape, dt=F32):
            return ctx.enter_context(nc.sbuf_tensor(name, shape, dt))

        def sem(name):
            return ctx.enter_context(nc.semaphore(name))

        X = sb("X", [P, N])
        H = sb("H", [P, 2 * T])
        GF = sb("GF", [P, 2 * T])
        GB = sb("GB", [P, 2 * T], BF16)
        wa_at = nc.sbuf_base
        WA = sb("WA", [P, 3 * JOBS[1] * P])
        WB = sb("WB", [P, 3 * JOBS[2] * P])
        SM = sb("SM", [P, SMALL_COLS])
        SEL = sb("SEL", [P, (GATED[0] + E1 + GATED[2] + NS) * P], BF16)
        PS = ctx.enter_context(nc.psum_tensor("PS", [P, 8, T], F32))

        sq = sb("sq", [P, T])
        rstd = sq
        actb = sb("actb", [P, 2, T])
        vb2 = sb("vb2", [P, 2, T])
        hid = sb("hid", [P, HID, T])
        fin = sb("fin", [P, T])
        AA = sb("AA", [P, T + 4])
        lgs = AA[:, 0:T]
        tk = sb("tk", [P, 16, TILES, E0])
        LT = sb("LT", [P, TILES, 2 * E0])
        tcol = sb("tcol", [P, 8, TILES])
        ws = sb("ws", [P, TILES, P])
        wbf = sb("wbf", [P, 2, TILES, E0], BF16)
        epsc = sb("epsc", [P, 4])
        sv = sb("sv", [P, 64])
        idxi = sb("idxi", [P, K3], I32)
        ones = sb("ones", [P, T])
        hs = sb("hs", [P, T])
        mt_at = nc.sbuf_base
        MT = sb("MT", [P, MT_TILES * PITCH])
        W2H = nc.alloc_sbuf_tensor_at("W2H", [P, W2_COLS], F32R, offset=wa_at)
        W2L = nc.alloc_sbuf_tensor_at("W2L", [P, W2_COLS], F32R, offset=wa_at + 4 * W2_COLS)
        HH = nc.alloc_sbuf_tensor_at("HH", [P, 2 * T], F32R, offset=mt_at + 16 * PITCH)
        HL = nc.alloc_sbuf_tensor_at("HL", [P, 2 * T], F32R, offset=mt_at + 16 * PITCH + 8 * T)
        bparts = sb("bparts", [P, 3, T], BF16)

        def small(name, rows=P):
            at, n = OFF[name]
            return SM[0:rows, at:at + n]

        def smallc(name, i=0, rows=P):
            at, _ = OFF[name]
            return SM[0:rows, at + i:at + i + 1]

        def ltok_view(layer):
            return LT[:, :, 0:EXPERTS[layer] * (2 if layer == 0 else 1)]

        def tile(layer, i, n=T):
            over, first, cols = {0: (WB, W0_COLS, 3 * JOBS[2] * P), 1: (WB, 0, 3 * JOBS[2] * P), 2: (WB, 0, 0),
                                 3: (WA, 0, 3 * JOBS[1] * P)}[layer]
            here = (cols - first) // PITCH
            if i < here:
                return over[:, first + i * PITCH:first + i * PITCH + n]
            return MT[:, (i - here) * PITCH:(i - here) * PITCH + n]

        def tiles(layer, names):
            return {k: tile(layer, i, PITCH if k.isupper() else T) for i, k in enumerate(names.split())}

        M0 = tiles(0, "dt dt_ dx dx_ xs xs_ sz sz_ cs cs_ XC xd v av total s0 s1 s2 s3 e0 e1 e2 e3 b0")
        BX = [M0["b0"], AA[:, 0:T]]
        STATES = [M0[f"s{n}"] for n in range(4)]
        TF, TB, Y0 = fin[:, :], actb[:, 0, :], actb[:, 1, :]
        EXPS = [M0[f"e{n}"] for n in range(4)] + [hid[:, 0, :], hid[:, 1, :], hid[:, 2, :], vb2[:, 0, :]]

        def pair(layer, i, odd):
            return tile(layer, i + odd)

        M1T = tiles(1, "ZV ZG ZS xv sg p pw pwp phi k abs r sin cos re im nre nim sqre sqim den t inv inv2 f")
        GATES = [tile(1, 26), tile(1, 27)]
        M2 = tiles(2, "kv et ew m")
        M3 = tiles(3, "H MX PP d0 db x1 x1_ ks ks_ vs vs_ rs rs_ hs hs_ r kc rc S ls al be bv aw nw t1")

        AB = WA[:, 3 * PITCH:5 * PITCH].rearrange("p (a t) -> p a t", a=2)[:, :, 0:T]

        M3 |= {"t": fin[:, :], "t2": vb2[:, 0, :], "q0": actb[:, 0, :], "q1": actb[:, 1, :],
               "q2": H[:, 0:T], "q3": H[:, T:2 * T], "k": GF[:, 0:T], "v": GF[:, T:2 * T],
               "r0": hid[:, 0, :], "r1": hid[:, 1, :], "rcs": hid[:, 2, :],
               "sq2": vb2[:, 1, :]}
        H2 = MT[:, (MT_TILES - 1) * PITCH:MT_TILES * PITCH]

        def w3(name, n=P):
            return WB[:, L3_AT[name]:L3_AT[name] + n]

        s_x, s_small, s_w0, s_w1, s_w2, s_w3 = (sem(n) for n in ("s_x", "s_small", "s_w0", "s_w1", "s_w2", "s_w3"))
        s_out = sem("s_out")
        x_ready = sem("x_ready")
        w2_high = sem("w2_high")
        w2_low = sem("w2_low")
        consts = sem("consts")
        gate_copied = sem("gate_copied")
        g_ready = sem("g_ready")
        u_ready = sem("u_ready")
        gate_ready = sem("gate_ready")
        act_done = sem("act_done")
        v_ready = sem("v_ready")
        hid_ready = sem("hid_ready")
        y_added = sem("y_added")
        y_final = sem("y_final")
        fin_ready = sem("fin_ready")
        sems = {k: (sem(f"{k}_pe"), sem(f"{k}_act"), sem(f"{k}_dve")) 
                for k in ("pro", "a0", "a0b", "a1", "a2", "a3", "a3m", "a3b", "prep")}

        MIX_NAMES = {0: a0_names()[0], 1: a1_names(), 2: a2_names(), 3: a3_names()[0]}
        middles = [Steps(s, n, 0) for s, n in zip(sems["a3m"], a3_names()[1])]
        backs = {0: [Steps(s, n, 1) for s, n in zip(sems["a0b"], a0_names()[1])],
                 3: [Steps(s, n, 1) for s, n in zip(sems["a3b"], a3_names()[2])]}
        prep = [Steps(s, n, 0) for s, n in zip(sems["prep"], PREP)]
        prologues, base = [], [0, 0, 0]
        for kind, layer in STAGES:
            names = pro_names(layer) if kind == "ffn" else ([], [], [])
            prologues.append([Steps(s, n, b) for s, n, b in zip(sems["pro"], names, base)])
            base = [b + B * len(n) for b, n in zip(base, names)]
        mixes = {l: [Steps(s, n, 0) for s, n in zip(sems[f"a{l}"], MIX_NAMES[l])] for l in range(4)}
        sums = Steps(sem("a0_pool"), [f"sum{n}" for n in range(1, NS)], 1)
        job0, gate0, ffn_i, jb, gb = {}, {}, {}, 0, 0
        vjob0, vb0, fi = {}, 0, 0
        for s, (kind, layer) in enumerate(STAGES):
            if kind == "ffn":
                job0[s], gate0[s], vjob0[s], ffn_i[s] = jb, gb, vb0, fi
                jb += B * JOBS[layer]
                vb0 += B * (GATED[layer] if layer < 3 else JOBS[layer])
                if layer < 3:
                    gb += B * (GATED[layer] // GATE_EVERY[layer])
                fi += 1

        def copied(s, c, expert):
            return c * E1 + (gate0[s] - gate0[3] + expert + 2)

        def chunk(c):
            return bass.ds(c * T, T)

        def half(c):
            return bass.ds((c % 2) * T, T)

        def x_of(s, c):
            return s * B + X0 if STAGES[s - 1][0] == "mix" else c + ((s - 1) * B + 1 + X0)

        def x_ffn(s, c):
            return 2 * c + (s * B + 1 + X0)

        def stage_loop(eng, s, layer, body):
            if mixed(s):
                body(0, (s, 1), None)
                with eng.Fori(1, B - 1) as c:
                    body(c, (s, c + 1), (s, c - 1))
                body(B - 1, (s + 2, 0), (s, B - 2))
            else:
                if after_mixed(s):
                    body(0, (s, 1), (s - 2, B - 1))
                with eng.Fori(1 if after_mixed(s) else 0, B - 1) as c:
                    body(c, (s, c + 1), None)
                nxt = s + 1 < stop_after and STAGES[s + 1][0] == "ffn"
                body(B - 1, (s + 1, 0) if nxt else None, None)

        def after_mixed(s):
            return s >= 2 and mixed(s - 2)

        def mixed(s):
            return STAGES[s][0] == "ffn" and STAGES[s][1] in MIX_PARTS and STAGES[min(s + 1, 11)][0] == "mix"

        def mix_stage(eng, layer, front, back, middle=None):
            runs = [(back, BACK[layer])] + ([(middle, MIDDLE[layer])] if middle else []) + [(front, FRONT[layer])]
            last = len(runs) - 1

            def step(c, odd):
                at = [(k, part) for k, (_, parts) in enumerate(runs) for part in parts
                      if not isinstance(c, int) or 0 <= c + k < B]
                orders = [[(k, part) for n, part in at if n == k] for k in range(last + 1)]
                for k, part in merged(*reversed(orders)):
                    runs[k][0](c + k, part, (odd + k) % 2)

            for c in range(-last, 0):
                step(c, c % 2)
            pairs = (B - last) // 2
            with eng.Fori(0, pairs) as two:
                step(two * 2, 0)
                step(two * 2 + 1, 1)
            for c in range(2 * pairs, B):
                step(c, c % 2)

        def ahead(s, c):
            return (s + 2, c + 2 - B) if isinstance(c, int) and c + 2 >= B else (s, c + 2)

        def ffn_weights(layer):
            if layer == 3:
                return w3("weff0", F3), w3("weff1", F3), w3("wo", F3)
            w, j = (WB, JOBS[layer]) if layer in (0, 2) else (WA, JOBS[layer])
            return w[:, 0:j * P], w[:, j * P:2 * j * P], w[:, 2 * j * P:3 * j * P]

        sel_at = {0: 0, 1: GATED[0], 2: GATED[0] + E1}
        sel_b = GATED[0] + E1 + GATED[2]

        block = ctx.enter_context(nc.Block())

        @block.sync
        def _(sp):
            sp.dma_start(SM[:, :], small_in).then_inc(s_small, 16)
            sp.dma_start(idxi[:, :], idx_in).then_inc(s_small, 16)
            sp.dma_start(SEL[:, :], sel_in).then_inc(s_small, 16)
            for c in range(B):
                sp.dma_start(X[:, c * T:(c + 1) * T], x_in[:, c * T:(c + 1) * T]).then_inc(s_x, 16)
            sp.dma_start(WB[:, 0:W0_COLS], w0_in).then_inc(s_w0, 16)
            sp.dma_start(WA[:, :], w1_in).then_inc(s_w1, 16)
            if stop_after > 6:
                sp.wait_ge(x_ready, 5 * B + X0)
                sp.dma_start(WB[:, :], w2_in).then_inc(s_w2, 16)
            if stop_after > 6:
                sp.wait_ge(w2_low, W2_PIECES)
                sp.dma_start(WB[:, 0:W3_COLS], w3_in).then_inc(s_w3, 16)
            for c in range(B):
                sp.wait_ge(x_ready, x_of(stop_after, c))
                sp.dma_start(out[:, c * T:(c + 1) * T], X[:, c * T:(c + 1) * T]).then_inc(s_out, 16)
            sp.wait_ge(s_out, 16 * B)

        @block.tensor
        def _(pe):
            mm = nc.tensor.matmul

            def route_part(s, c, layer, part, steps):
                p, a, d = steps
                e = EXPERTS[layer]
                nl = 2 * e if layer == 0 else e
                if part == "logits":
                    pe.wait_ge(d.sem, d.value(c, "h"))
                    mm(PS[0:nl, B_BANK, :], small(f"gate{layer}"), H[:, half(c)], start=True, stop=True)\
                        .then_inc(p.mark("logits"), 1)
                if part == "tok":
                    pe.wait_ge(d.sem, d.value(c, "lg"))
                    for t in range(TILES):
                        last = nc.tensor.transpose(PS[:, B_BANK, t * P:(t + 1) * P], lgs[:, t * P:(t + 1) * P],
                                                   small("ident"))
                    last.then_inc(p.mark("tok"), 1)
                if part == "back":
                    pe.wait_ge(d.sem, d.value(c, "wl"))
                    for t in range(TILES):
                        last = nc.tensor.transpose(PS[:, B_BANK, t * P:(t + 1) * P], ws[:, t, :], small("ident"))
                    last.then_inc(p.mark("back"), 1)

            def prologue(s, c, part):
                kind, layer = STAGES[s]
                p, a, d = prologues[s]
                if part == "center":
                    if mixed(s) and not isinstance(c, int):
                        pe.wait_ge(x_ready, x_ffn(s, c - 3) + 1)
                    elif after_mixed(s) and isinstance(c, int) and c < 2:
                        pe.wait_ge(x_ready, x_ffn(s - 2, B - 3 + c) + 1)
                    elif s > 0:
                        pe.wait_ge(x_ready, x_of(s, c))
                    if not (s == 0 and isinstance(c, int) and c == 0):
                        pe.wait_ge(d.sem, d.before(c))
                    mm(PS[:, A_BANK, :], small("center"), X[:, chunk(c)], start=True, stop=True)\
                        .then_inc(p.mark("center"), 1)
                if part == "var":
                    pe.wait_ge(a.sem, a.value(c, "sq"))
                    mm(PS[:, B_BANK, :], small("avg"), sq[:, :], start=True, stop=True).then_inc(p.mark("var"), 1)
                if layer in EXPERTS:
                    route_part(s, c, layer, part, prologues[s])

            def ffn(s, layer):
                J, NV = JOBS[layer], GATED[layer] if layer < 3 else JOBS[layer]
                wg, wu, wd = ffn_weights(layer)

                def hd(n):
                    return n + (1 + CREDIT)

                if s == 0 or STAGES[s - 1][0] == "mix" and not after_mixed(s):
                    for part in pro_parts(layer):
                        prologue(s, 0, part)
                if s > 0:
                    pe.wait_ge(x_ready, x_ffn(s - 2, B - 1) if after_mixed(s) else s * B + X0)
                pe.wait_ge({0: s_w0, 1: s_w1, 2: s_w2, 3: s_w3}[layer], 16)
                if layer == 2:
                    pe.wait_ge(w2_low, W2_PIECES)

                def spread_copied(c, expert):
                    pe.wait_ge(gate_copied, copied(s, c, expert - 1))
                    at = (sel_at[1] + expert) * P
                    mm(PS[:, GATE_BANK, :], SEL[:, at:at + P], GB[:, half(c)], start=True, stop=True)\
                        .then_inc(gate_ready, 1)

                def product(bank, w, j, h, c):
                    out = PS[:, bank, :]
                    if layer != 2:
                        return mm(out, w[:, j * P:(j + 1) * P], h, start=True, stop=True)
                    at = (j + (0 if w is wg else J)) * P
                    high, low = W2H[:, at:at + P], W2L[:, at:at + P]
                    mm(out, high, HH[:, half(c)], start=True, stop=False)
                    mm(out, high, HL[:, half(c)], start=False, stop=False)
                    return mm(out, low, HH[:, half(c)], start=False, stop=True)

                def body(c, pro, mix):
                    n0 = c * J + job0[s]
                    h = H[:, half(c)]
                    slots = side_parts(layer, pro, mix)

                    def side(i):
                        for what, part in slots[i]:
                            if what == "mix":
                                mixer(*mix, part)
                            elif pro is not None:
                                prologue(*pro, part)

                    p, a, d = prologues[s]
                    pe.wait_ge(d.sem, d.value(c, d.names[-1]))
                    gi = 0
                    if layer == 1:
                        spread_copied(c, 0)
                    for j in range(J + LAG):
                        if j < J:
                            pe.wait_ge(act_done, hd(n0 + (j - behind(j, J, 2))))
                            product(G_BANK + j % 2, wg, j, h, c).then_inc(g_ready, 1)
                            side(3 * j)
                            if j >= 2 and (j - 2 < GATED[layer] or layer == 3):
                                pe.wait_ge(v_ready, c * NV + (vjob0[s] + j - 1))
                            else:
                                pe.wait_ge(hid_ready, hd(n0 + (j - behind(j, J, 2))))
                            product(U_BANK + j % 2, wu, j, h, c).then_inc(u_ready, 1)
                            side(3 * j + 1)
                        if j >= LAG:
                            jj = j - LAG
                            if jj == 0:
                                pe.wait_ge(fin_ready, c + (ffn_i[s] * B + 1))
                            pe.wait_ge(hid_ready, hd(n0 + jj))
                            mm(PS[:, Y_BANK, :], wd[:, jj * P:(jj + 1) * P], hid[:, jj % HID, :], start=jj == 0,
                               stop=jj == J - 1 and layer > 1).then_inc(y_added, 1)
                        if layer == 1 and j + 1 < GATED[1] and (j + 1) % GATE_EVERY[1] == 0:
                            spread_copied(c, (j + 1) // GATE_EVERY[1])
                        if layer != 1 and j < GATED[layer]:
                            pe.wait_ge(hid_ready, hd(n0 + (j - 1)))
                            at = (sel_at[layer] + gi) * P
                            mm(PS[:, GATE_BANK, :], SEL[:, at:at + P], GB[:, half(c)], start=True, stop=True)\
                                .then_inc(gate_ready, 1)
                            gi += 1
                        if j < J:
                            side(3 * j + 2)
                    if layer in (0, 1):
                        k = 3 * EXPERTS[layer]
                        mm(PS[:, Y_BANK, :], small(f"b2_{layer}", k), GF[0:k, half(c)], start=False, stop=True)\
                            .then_inc(y_final, 1)

                stage_loop(pe, s, layer, body)

            def norm0_parts(layer, c, part):
                p, a, d = mixes[layer]
                if part == "center":
                    if not (isinstance(c, int) and c == 0):
                        pe.wait_ge(d.sem, d.before(c))
                        pe.wait_ge(a.sem, a.before(c))
                    mm(PS[:, N_BANK, :], small("center"), X[:, chunk(c)], start=True, stop=True)\
                        .then_inc(p.mark("center0"), 1)
                if part == "var":
                    pe.wait_ge(a.sem, a.value(c, "sq0"))
                    mm(PS[:, V_BANK, :], small("avg"), sq[:, :], start=True, stop=True).then_inc(p.mark("var0"), 1)

            def front0(c, part, odd):
                p, a, d = mixes[0]
                norm0_parts(0, c, part)
                if part == "xz":
                    pe.wait_ge(d.sem, d.value(c, "h0"))
                    mm(PS[:, P_BANK, :], small("a0_xc"), hs[:, :], start=True, stop=True).then_inc(p.mark("xc"), 1)
                    mm(PS[:, Q_BANK, :], small("a0_z"), hs[:, :], start=True, stop=True).then_inc(p.mark("z"), 1)
                if part == "xd":
                    pe.wait_ge(a.sem, a.value(c, "xs"))
                    mm(PS[:, N_BANK, :], small("a0_xd"), pair(0, 4, odd), start=True, stop=True).then_inc(p.mark("xd"), 1)
                if part == "split1":
                    pe.wait_ge(a.sem, a.value(c, "xds"))
                    mm(PS[:, V_BANK, :], small("a0_dt"), M0["xd"], start=True, stop=True).then_inc(p.mark("dtpre"), 1)
                    mm(PS[:, P_BANK, :], small("a0_c"), M0["xd"], start=True, stop=True).then_inc(p.mark("C"), 1)

            def back0(c, part, odd):
                p, a, d = backs[0]
                fd = mixes[0][2]

                def row_of_b(n):
                    at = (sel_b + n) * P
                    mm(PS[:, S_BANK + n % S_BANKS, :], SEL[:, at:at + P], bparts[:, odd, :],
                       start=True, stop=True).then_inc(p.mark(f"bp{n}"), 1)

                if part == "rows":
                    pe.wait_ge(fd.sem, fd.value(c, "bl"))
                    pe.wait_ge(x_ready, c + (B + X0))
                    for n in range(S_BANKS):
                        row_of_b(n)
                if part.startswith("state") and int(part[5:]) + S_BANKS < NS:
                    n = int(part[5:]) + S_BANKS
                    pe.wait_ge(d.sem, d.value(c, f"bx{n - S_BANKS}"))
                    row_of_b(n)
                if part == "out":
                    pe.wait_ge(d.sem, d.value(c, "y"))
                    mm(PS[:, R_BANK, :], small("a0_out"), Y0, start=True, stop=True).then_inc(p.mark("out"), 1)

            def mix1(c, part):
                p, a, d = mixes[1]
                if part == "zvg":
                    pe.wait_ge(d.sem, d.value(c, "h0"))
                    mm(PS[:, A_BANK, :], small("a1_v"), hs[:, :], start=True, stop=True).then_inc(p.mark("zv"), 1)
                    mm(PS[:, B_BANK, :], small("a1_g"), hs[:, :], start=True, stop=True).then_inc(p.mark("zg"), 1)
                if part == "zs":
                    pe.wait_ge(a.sem, a.value(c, "zvp"))
                    mm(PS[:, A_BANK, :], small("a1_s"), hs[:, :], start=True, stop=True).then_inc(p.mark("zs"), 1)
                if part[:-1] in ("y", "q"):
                    m = int(part[-1])
                if part[:-1] == "y":
                    for z in ("re", "im"):
                        pe.wait_ge(d.sem, d.value(c, f"n{z}{m}"))
                        mm(PS[:, A_BANK, :], small(f"a1_{z}")[:, m * P:(m + 1) * P], M1T[f"n{z}"],
                           start=m == 0 and z == "re", stop=m == M1 - 1 and z == "im").then_inc(p.mark(f"y{z}{m}"), 1)
                if part[:-1] == "q":
                    for z in ("re", "im"):
                        pe.wait_ge(a.sem, a.value(c, f"sq{z}{m}"))
                        mm(PS[:, B_BANK, :], small("a1_sum"), M1T[f"sq{z}"], start=m == 0 and z == "re",
                           stop=m == M1 - 1 and z == "im").then_inc(p.mark(f"q{z}{m}"), 1)
                if part == "out":
                    pe.wait_ge(d.sem, d.value(c, "yy"))
                    mm(PS[:, A_BANK, :], small("a1_out"), M1T["t"], start=True, stop=True).then_inc(p.mark("out"), 1)

            def mix2(c, part):
                p, a, d = mixes[2]
                kv = M2["kv"].rearrange("p (t n) -> p t n", t=TILES)
                if part == "kv":
                    pe.wait_ge(d.sem, d.value(c, "h0"))
                    for t in range(TILES):
                        last = mm(PS[:, A_BANK, t * P:(t + 1) * P], hs[:, t * P:(t + 1) * P], small("a2_kv"),
                                  start=True, stop=True)
                    last.then_inc(p.mark("kv"), 1)
                if part == "et":
                    pe.wait_ge(a.sem, a.value(c, "kvs"))
                    for t in range(TILES):
                        last = mm(PS[0:D2, B_BANK, 0:P], kv[:, t, 0:D2], kv[:, t, :], start=t == 0, stop=t == TILES - 1)
                    last.then_inc(p.mark("et"), 1)
                if part == "ew":
                    pe.wait_ge(a.sem, a.value(c, "ets"))
                    mm(PS[:, A_BANK, 0:P], M2["et"][0:D2, 0:P], small("a2_o", D2), start=True, stop=True)\
                        .then_inc(p.mark("ew"), 1)
                if part == "m":
                    pe.wait_ge(a.sem, a.value(c, "ews"))
                    mm(PS[:, B_BANK, 0:P], small("a2_q"), M2["ew"][:, 0:P], start=True, stop=True)\
                        .then_inc(p.mark("m"), 1)
                if part == "out":
                    pe.wait_ge(a.sem, a.value(c, "ms"))
                    mm(PS[:, A_BANK, :], M2["m"][:, 0:P], hs[:, :], start=True, stop=True).then_inc(p.mark("out"), 1)

            def after(steps, c, name):
                pe.wait_ge(steps.sem, steps.value(c, name))

            def front3(c, part, odd):
                p, a, d = mixes[3]
                norm0_parts(3, c, part)
                if part == "center1":
                    after(d, c, "h0")
                    mm(PS[:, N_BANK, :], small("center"), pair(3, 13, odd), start=True, stop=True)\
                        .then_inc(p.mark("center1"), 1)
                if part == "var1":
                    after(a, c, "sq1")
                    mm(PS[:, V_BANK, :], small("avg"), sq[:, :], start=True, stop=True).then_inc(p.mark("var1"), 1)
                if part == "kv":
                    after(d, c, "xk")
                    mm(PS[:, P_BANK, :], w3("k"), M3["k"], start=True, stop=True).then_inc(p.mark("k"), 1)
                    after(d, c, "xv")
                    mm(PS[:, Q_BANK, :], w3("v"), M3["v"], start=True, stop=True).then_inc(p.mark("v"), 1)
                if part == "r":
                    after(d, c, "xr")
                    mm(PS[:, R_BANK, :], w3("r"), M3["r"], start=True, stop=True).then_inc(p.mark("r"), 1)

            def middle3(c, part, odd):
                pass

            def back3(c, part, odd):
                p, a, d = backs[3]

                def kc(f, bank):
                    mm(PS[:, bank, :], w3("kc", F3)[:, f * P:(f + 1) * P], M3["kc"], start=True, stop=True)\
                        .then_inc(p.mark(f"kc{f}"), 1)

                if part == "center2":
                    after(middles[2], c, "x1")
                    pe.wait_ge(x_ready, c + (10 * B + X0))
                    mm(PS[:, S_BANK, :], small("center"), pair(3, 5, odd), start=True, stop=True)\
                        .then_inc(p.mark("center2"), 1)
                if part == "var2":
                    after(a, c, "sq2")
                    mm(PS[:, S_BANK + 1, :], small("avg"), M3["sq2"], start=True, stop=True).then_inc(p.mark("var2"), 1)
                if part == "kc01":
                    after(d, c, "xkc")
                    kc(0, S_BANK + 2)
                    kc(1, S_BANK + 1)
                if part == "kc23":
                    kc(2, S_BANK)
                    after(a, c, "r0")
                    kc(3, S_BANK + 2)
                if part == "rc":
                    after(d, c, "xrc")
                    after(a, c, "r1")
                    mm(PS[:, S_BANK + 1, :], w3("rc"), M3["rc"], start=True, stop=True).then_inc(p.mark("rc"), 1)
                if part == "vc":
                    after(a, c, "q3")
                    for f in range(4):
                        last = mm(PS[:, S_BANK, :], w3("vc", F3)[:, f * P:(f + 1) * P], M3[f"q{f}"],
                                  start=f == 0, stop=f == 3)
                    last.then_inc(p.mark("vc"), 1)

            def mixer(s, c, part):
                layer = STAGES[s][1]
                p, a, d = mixes[layer]
                if part == "center":
                    ps, pc = ahead(s, c)
                    pd = prologues[ps][2]
                    pe.wait_ge(pd.sem, pd.value(pc, pd.names[-1]))
                    pe.wait_ge(x_ready, x_ffn(s, c))
                    mm(PS[:, A_BANK, :], small("center"), X[:, chunk(c)], start=True, stop=True)\
                        .then_inc(p.mark("center0"), 1)
                if part == "var":
                    pe.wait_ge(a.sem, a.value(c, "sq0"))
                    mm(PS[:, B_BANK, :], small("avg"), sq[:, :], start=True, stop=True).then_inc(p.mark("var0"), 1)
                (mix1 if layer == 1 else mix2)(c, part)

            pe.sem_inc(backs[0][0].sem, 1)
            pe.sem_inc(backs[3][0].sem, 1)
            pe.wait_ge(s_small, 48)
            pe.wait_ge(s_x, 16 * B)
            pe.wait_ge(consts, 6)

            def prep_pe():
                p, a, d = prep
                pe.wait_ge(s_w3, 16)
                for k in range(K3):
                    pe.wait_ge(d.sem, d.value(0, f"ba{k}"))
                    mm(PS[:, A_BANK + k, :], w3("A"), w3(f"weff{k}", F3),
                       start=True, stop=True).then_inc(p.mark(f"weff{k}"), 1)

            for s, (kind, layer) in enumerate(STAGES[:stop_after]):
                if s == 9:
                    pe.wait_ge(x_ready, 9 * B + X0)
                    prep_pe()
                    pe.wait_ge(prep[2].sem, prep[2].value(0, "wi1"))
                if s == 3:
                    pe.wait_ge(prep[2].sem, prep[2].value(0, "blk"))
                if kind == "ffn":
                    ffn(s, layer)
                elif layer in FRONT:
                    pe.wait_ge(x_ready, s * B + X0)
                    mix_stage(pe, layer, *((front0, back0) if layer == 0 else (front3, back3, middle3)))

        @block.scalar
        def _(act):
            run = nc.scalar.activation
            eps = epsc[:, 0:1]

            def norm_square(steps, c, n="", bank=A_BANK, dst=sq[:, :]):
                p, a, d = steps
                act.wait_ge(p.sem, p.value(c, f"center{n}"))
                run(dst, PS[:, bank, :], ACT.Square).then_inc(a.mark(f"sq{n}"), 1)

            def norm_rstd(steps, c, n="", bank=B_BANK, dst=sq[:, :]):
                p, a, d = steps
                nc.scalar.preload_act_table_set(NORM_SET)
                act.wait_ge(p.sem, p.value(c, f"var{n}"))
                run(dst, PS[:, bank, :], ACT.Ln, bias=eps).then_inc(a.mark(f"lnv{n}"), 1)
                act.wait_ge(a.sem, a.value(c, f"lnv{n}"))
                run(dst, dst, ACT.Exp, scale=-0.5).then_inc(a.mark(f"rstd{n}"), 1)

            def prologue(s, c, part):
                kind, layer = STAGES[s]
                steps = prologues[s]
                p, a, d = steps
                if part == "square":
                    norm_square(steps, c)
                if part == "rstd":
                    norm_rstd(steps, c)
                if part == "gexp" and layer in EXPERTS:
                    nc.scalar.preload_act_table_set(NORM_SET)
                    e = EXPERTS[layer]
                    if layer == 0:
                        act.wait_ge(d.sem, d.value(c, "ltok"))
                        run(tk[:, 12, :, 0:e], ltok_view(layer)[:, :, e:2 * e], ACT.Exp, scale=-1.0)\
                            .then_inc(a.mark("gexp"), 1)
                    else:
                        act.wait_ge(d.sem, d.value(c, "arg"))
                        run(tk[:, 12, :, 0:e], tk[:, 11, :, 0:e], ACT.Exp).then_inc(a.mark("gexp"), 1)

            def ffn(s, layer):
                J = JOBS[layer]
                func = {0: ACT.Silu, 1: ACT.Gelu, 2: ACT.Silu, 3: ACT.Relu}[layer]
                if s == 0 or STAGES[s - 1][0] == "mix" and not after_mixed(s):
                    for part in pro_parts(layer):
                        prologue(s, 0, part)

                def body(c, pro, mix):
                    n0 = c * J + job0[s]
                    slots = side_parts(layer, pro, mix)
                    for j in range(J):
                        act.wait_ge(hid_ready, n0 + (j - behind(j, J, 2) + 1 + CREDIT))
                        act.wait_ge(g_ready, n0 + (j + 1))
                        if layer == 1 and j < GATED[1] and j % GATE_EVERY[1] == 0:
                            expert = j // GATE_EVERY[1]
                            act.wait_ge(gate_ready, c * E1 + (gate0[s] + expert + 1))
                            run(GATES[expert % 2], PS[:, GATE_BANK, :], ACT.Copy).then_inc(gate_copied, 1)
                        kw = {"bias": smallc(f"bg{layer}", j)} if layer < 2 else {}
                        run(actb[:, j % 2, :], PS[:, G_BANK + j % 2, :], func, **kw).then_inc(act_done, 1)
                        for what, part in slots[3 * j] + slots[3 * j + 1] + slots[3 * j + 2]:
                            if what == "mix":
                                mixer(*mix, part)
                            elif pro is not None:
                                prologue(*pro, part)

                stage_loop(act, s, layer, body)

            def copy_of(c, steps, product, bank, dst, name, func=ACT.Copy, src=None, **kw):
                p, a, d = steps
                act.wait_ge(p.sem, p.value(c, product))
                run(dst, PS[:, bank, :] if src is None else src, func, **kw).then_inc(a.mark(name), 1)

            def norm0_parts(layer, c, part):
                if part == "square":
                    norm_square(mixes[layer], c, 0, N_BANK)
                if part == "rstd":
                    norm_rstd(mixes[layer], c, 0, V_BANK)

            def front0(c, part, odd):
                p, a, d = mixes[0]
                norm0_parts(0, c, part)
                if part == "xz_copy":
                    copy_of(c, mixes[0], "xc", P_BANK, M0["XC"][:, 1:T + 1], "xcp")
                    nc.scalar.preload_act_table_set(SILU_SET)
                    copy_of(c, mixes[0], "z", Q_BANK, pair(0, 6, odd), "sz", ACT.Silu)
                if part == "xs":
                    act.wait_ge(d.sem, d.value(c, "c2"))
                    run(pair(0, 4, odd), TF, ACT.Silu).then_inc(a.mark("xs"), 1)
                if part == "xd_copy":
                    copy_of(c, mixes[0], "xd", N_BANK, M0["xd"], "xds")
                if part == "soft":
                    nc.scalar.preload_act_table_set(NORM_SET)
                    copy_of(c, mixes[0], "dtpre", V_BANK, M0["v"], "v", ACT.Identity, bias=smallc("a0_bdt"))
                    act.wait_ge(a.sem, a.value(c, "v"))
                    run(M0["av"], M0["v"], ACT.Abs).then_inc(a.mark("av"), 1)
                    act.wait_ge(a.sem, a.value(c, "av"))
                    run(TF, M0["av"], ACT.Exp, scale=-1.0).then_inc(a.mark("ev"), 1)
                    act.wait_ge(a.sem, a.value(c, "ev"))
                    run(M0["av"], TF, ACT.Ln, bias=epsc[:, 3:4]).then_inc(a.mark("lv"), 1)
                    copy_of(c, mixes[0], "C", P_BANK, pair(0, 8, odd), "Cs")

            def back0(c, part, odd):
                p, a, d = backs[0]
                fd = mixes[0][2]
                if part.startswith("decay"):
                    nc.scalar.preload_act_table_set(NORM_SET)
                    if part == "decay0":
                        act.wait_ge(fd.sem, fd.value(c, "dt"))
                        act.wait_ge(d.sem, d.before(c))
                    for n in range(4 * int(part[-1]), 4 * int(part[-1]) + 4):
                        if n >= 8:
                            act.wait_ge(d.sem, d.value(c, f"s{n - 8}"))
                        run(EXPS[n % 8], pair(0, 0, odd), ACT.Exp, scale=sv[:, n:n + 1]).then_inc(a.mark(f"Ad{n}"), 1)

            def mix1(c, part):
                p, a, d = mixes[1]
                if part == "zvg_copy":
                    copy_of(c, mixes[1], "zv", A_BANK, M1T["ZV"][:, 3:T + 3], "zvp")
                    copy_of(c, mixes[1], "zg", B_BANK, M1T["ZG"][:, 3:T + 3], "zgp")
                if part == "zs_copy":
                    copy_of(c, mixes[1], "zs", A_BANK, M1T["ZS"][:, 3:T + 3], "zsp")
                if part == "gate":
                    act.wait_ge(d.sem, d.value(c, "g3"))
                    run(M1T["sg"], M1T["sg"], ACT.Silu).then_inc(a.mark("sg"), 1)
                    act.wait_ge(d.sem, d.value(c, "cl1"))
                    run(M1T["p"], M1T["p"], ACT.Exp).then_inc(a.mark("p"), 1)
                if part[:-1] in ("sin", "square"):
                    m = int(part[-1])
                    if part[:-1] == "sin":
                        act.wait_ge(d.sem, d.value(c, f"r{m}"))
                        run(M1T["abs"], M1T["r"], ACT.Abs).then_inc(a.mark(f"abs{m}"), 1)
                        run(M1T["sin"], M1T["r"], ACT.Sin).then_inc(a.mark(f"sin{m}"), 1)
                        act.wait_ge(a.sem, a.value(c, f"abs{m}"))
                        run(M1T["cos"], M1T["abs"], ACT.Sin, scale=-1.0, bias=epsc[:, 2:3])\
                            .then_inc(a.mark(f"cos{m}"), 1)
                    if part[:-1] == "square":
                        for z in ("re", "im"):
                            act.wait_ge(d.sem, d.value(c, f"n{z}{m}"))
                            if m:
                                act.wait_ge(p.sem, p.value(c, f"q{z}{m - 1}"))
                            run(M1T[f"sq{z}"], M1T[f"n{z}"], ACT.Square).then_inc(a.mark(f"sq{z}{m}"), 1)
                if part == "rs":
                    nc.scalar.preload_act_table_set(NORM_SET)
                    act.wait_ge(d.sem, d.value(c, "t"))
                    run(M1T["t"], M1T["t"], ACT.Ln, scale=1.0 / (2 * H1 * M1), bias=eps).then_inc(a.mark("lnq"), 1)
                    act.wait_ge(a.sem, a.value(c, "lnq"))
                    run(M1T["t"], M1T["t"], ACT.Exp, scale=-0.5).then_inc(a.mark("rs"), 1)

            def mix2(c, part):
                if part == "kv_copy":
                    copy_of(c, mixes[2], "kv", A_BANK, M2["kv"], "kvs")
                if part == "et_copy":
                    copy_of(c, mixes[2], "et", B_BANK, M2["et"][0:D2, 0:P], "ets", src=PS[0:D2, B_BANK, 0:P],
                            scale=(3.0 / D2) ** 0.5)
                if part == "ew_copy":
                    copy_of(c, mixes[2], "ew", A_BANK, M2["ew"][:, 0:P], "ews", src=PS[:, A_BANK, 0:P])
                if part == "m_copy":
                    copy_of(c, mixes[2], "m", B_BANK, M2["m"][:, 0:P], "ms", src=PS[:, B_BANK, 0:P])

            def front3(c, part, odd):
                p, a, d = mixes[3]
                norm0_parts(3, c, part)

                if part == "square1":
                    norm_square(mixes[3], c, 1, N_BANK)
                if part == "rstd1":
                    norm_rstd(mixes[3], c, 1, V_BANK)
                if part == "kv_copy":
                    copy_of(c, mixes[3], "k", P_BANK, pair(3, 7, odd), "ks")
                    copy_of(c, mixes[3], "v", Q_BANK, pair(3, 9, odd), "vs")
                if part == "r_copy":
                    copy_of(c, mixes[3], "r", R_BANK, pair(3, 11, odd), "sr", ACT.Sigmoid)

            def middle3(c, part, odd):
                p, a, d = middles

                def exps(*which):
                    nc.scalar.preload_act_table_set(NORM_SET)
                    for name, made, t in which:
                        act.wait_ge(d.sem, d.value(c, made))
                        run(M3[t], M3[t], ACT.Exp).then_inc(a.mark(name), 1)

                if part == "ab":
                    nc.scalar.preload_act_table_set(NORM_SET)
                    act.wait_ge(d.sem, d.value(c, "db"))
                    run(AB, AB, ACT.Exp).then_inc(a.mark("ab"), 1)
                if part == "lnS":
                    act.wait_ge(d.sem, d.value(c, "S"))
                    run(M3["ls"], M3["S"][:, 0:T], ACT.Ln, bias=epsc[:, 1:2]).then_inc(a.mark("lnS"), 1)
                if part == "eab":
                    exps(("ea", "al", "al"), ("eb", "nb", "be"))
                if part == "e12":
                    exps(("e1", "aw", "aw"), ("e2", "nw", "nw"))

            def back3(c, part, odd):
                p, a, d = backs[3]

                def squared_relu(f, bank):
                    copy_of(c, backs[3], f"kc{f}", bank, M3[f"r{f % 2}"], f"r{f}", ACT.Relu)
                    act.wait_ge(a.sem, a.value(c, f"r{f}"))
                    run(M3[f"q{f}"], M3[f"r{f % 2}"], ACT.Square).then_inc(a.mark(f"q{f}"), 1)

                if part == "square2":
                    norm_square(backs[3], c, 2, S_BANK, M3["sq2"])
                if part == "rstd2":
                    norm_rstd(backs[3], c, 2, S_BANK + 1, M3["sq2"])
                if part == "q01":
                    squared_relu(0, S_BANK + 2)
                    squared_relu(1, S_BANK + 1)
                if part == "q23":
                    squared_relu(2, S_BANK)
                    squared_relu(3, S_BANK + 2)
                if part == "rc_gate":
                    copy_of(c, backs[3], "rc", S_BANK + 1, M3["rcs"], "src", ACT.Sigmoid)

            def mixer(s, c, part):
                layer = STAGES[s][1]
                if part == "square":
                    norm_square(mixes[layer], c, 0)
                if part == "rstd":
                    norm_rstd(mixes[layer], c, 0)
                (mix1 if layer == 1 else mix2)(c, part)

            act.wait_ge(s_small, 48)
            act.wait_ge(consts, 6)
            act.sem_inc(act_done, CREDIT)
            act.sem_inc(gate_copied, 1)
            act.sem_inc(backs[0][1].sem, 1)
            act.sem_inc(backs[3][1].sem, 1)
            p, a, d = prep
            nc.scalar.preload_act_table_set(NORM_SET)
            run(sv[:, 0:NS], small("a0_alog"), ACT.Exp).then_inc(a.mark("ealog"), 1)
            run(sv[:, 20:21], smallc("a1_slope"), ACT.Abs).then_inc(a.mark("sl_a"), 1)
            act.wait_ge(a.sem, a.value(0, "sl_a"))
            run(sv[:, 21:22], sv[:, 20:21], ACT.Exp, scale=-1.0).then_inc(a.mark("sl_e"), 1)
            act.wait_ge(a.sem, a.value(0, "sl_e"))
            run(sv[:, 22:23], sv[:, 21:22], ACT.Ln, bias=epsc[:, 3:4]).then_inc(a.mark("sl_l"), 1)
            act.wait_ge(d.sem, d.value(0, "sl_neg"))
            run(small("time"), small("time"), ACT.Exp, scale=sv[:, 24:25]).then_inc(a.mark("tw"), 1)
            act.wait_ge(d.sem, d.value(0, "dd"))
            run(sv[:, 31:34], sv[:, 28:31], ACT.Exp).then_inc(a.mark("de"), 1)
            for s, (kind, layer) in enumerate(STAGES[:stop_after]):
                if s == 6:
                    act.wait_ge(s_w2, 16)
                    act.wait_ge(x_ready, 6 * B + X0)
                    for i in range(W2_PIECES):
                        run(W2H[:, i * T:(i + 1) * T], WB[:, i * T:(i + 1) * T], ACT.Copy).then_inc(w2_high, 1)
                if kind == "ffn":
                    ffn(s, layer)
                elif layer in FRONT:
                    act.wait_ge(x_ready, s * B + X0)
                    mix_stage(act, layer, *((front0, back0) if layer == 0 else (front3, back3, middle3)))

        @block.gpsimd
        def _(pool):
            d = backs[0][2]
            total = M0["total"]
            pool.sem_inc(sums.sem, 1)
            with pool.Fori(0, B) as c:
                for n in range(1, NS):
                    pool.wait_ge(d.sem, d.value(c, f"s{n}"))
                    if n > 1:
                        pool.wait_ge(sums.sem, sums.value(c, f"sum{n - 1}"))
                    nc.gpsimd.tensor_tensor(total, STATES[0] if n == 1 else total, STATES[n % 4], ALU.add)\
                        .then_inc(sums.mark(f"sum{n}"), 1)

        @block.vector
        def _(dve):
            v = nc.vector

            def normed(steps, c, dst, n="", bank=A_BANK):
                p, a, d = steps
                dve.wait_ge(a.sem, a.value(c, f"rstd{n}"))
                v.tensor_tensor(dst, PS[:, bank, :], rstd[:, :], ALU.mult).then_inc(d.mark(f"h{n}"), 1)

            def prologue(s, c, part):
                kind, layer = STAGES[s]
                p, a, d = prologues[s]
                if part == "norm":
                    normed(prologues[s], c, H[:, half(c)])
                if part == "halves":
                    dve.wait_ge(d.sem, d.value(c, "h"))
                    v.tensor_copy(HH[:, half(c)], H[:, half(c)]).then_inc(d.mark("hh"), 1)
                    dve.wait_ge(d.sem, d.value(c, "hh"))
                    v.tensor_tensor(HL[:, half(c)], H[:, half(c)], HH[:, half(c)].bitcast(F32), ALU.subtract)\
                        .then_inc(d.mark("hl"), 1)
                if layer not in EXPERTS:
                    return
                e = EXPERTS[layer]
                nl = 2 * e if layer == 0 else e

                def need(name):
                    dve.wait_ge(d.sem, d.value(c, name))

                def K(i):
                    return tk[:, i, :, 0:e]

                def col(i):
                    return tcol[:, i, :]

                def wide(i):
                    return tcol[:, i, :].unsqueeze(2).to_broadcast([P, TILES, e])

                rank = small("rank")[:, E0 - e:E0].unsqueeze(1).to_broadcast([P, TILES, e])
                tt, red = v.tensor_tensor, v.tensor_reduce
                if part == "lg":
                    dve.wait_ge(p.sem, p.value(c, "logits"))
                    gb = {0: smallc("gb0", 0, nl), 1: smallc("gb1", 0, nl), 2: 0.0}[layer]
                    v.tensor_scalar(lgs[0:nl, :], PS[0:nl, B_BANK, :], gb, 1.0 / TAU if layer == 1 else 1.0,
                                    ALU.add, ALU.mult).then_inc(d.mark("lg"), 1)
                if part == "top1":
                    dve.wait_ge(p.sem, p.value(c, "tok"))
                    lt = ltok_view(layer)
                    v.tensor_copy(lt, PS[:, B_BANK, :].rearrange("p (t e) -> p t e", t=TILES)[:, :, 0:nl])\
                        .then_inc(d.mark("ltok"), 1)
                    need("ltok")
                    lb = lt[:, :, 0:e]
                    red(col(0), lb, AX, ALU.max).then_inc(d.mark("m1"), 1)
                    need("m1")
                    tt(K(2), lb, wide(0), ALU.is_equal).then_inc(d.mark("eq1"), 1)
                    need("eq1")
                    tt(K(3), K(2), rank, ALU.mult).then_inc(d.mark("rk1"), 1)
                    need("rk1")
                    red(col(1), K(3), AX, ALU.max).then_inc(d.mark("t1"), 1)
                    need("t1")
                    tt(K(4), K(3), wide(1), ALU.is_equal).then_inc(d.mark("oh1"), 1)
                if part == "top2":
                    lb = ltok_view(layer)[:, :, 0:e]
                    need("oh1")
                    v.scalar_tensor_tensor(out=K(5), in0=K(4), scalar=NEG_HUGE, in1=lb, op0=ALU.mult, op1=ALU.add)\
                        .then_inc(d.mark("l2"), 1)
                    need("l2")
                    red(col(2), K(5), AX, ALU.max).then_inc(d.mark("m2"), 1)
                    need("m2")
                    tt(K(6), K(5), wide(2), ALU.is_equal).then_inc(d.mark("eq2"), 1)
                    need("eq2")
                    tt(K(7), K(6), rank, ALU.mult).then_inc(d.mark("rk2"), 1)
                    need("rk2")
                    red(col(3), K(7), AX, ALU.max).then_inc(d.mark("t2"), 1)
                    need("t2")
                    tt(K(8), K(7), wide(3), ALU.is_equal).then_inc(d.mark("oh2"), 1)
                    need("oh2")
                    tt(K(9), K(4), K(8), ALU.add).then_inc(d.mark("mask"), 1)
                    if layer != 0:
                        tt(K(11), lb, wide(0), ALU.subtract).then_inc(d.mark("arg"), 1)
                if part == "weights":
                    if layer == 0:
                        dve.wait_ge(a.sem, a.value(c, "gexp"))
                        v.tensor_scalar(K(11), K(12), 1.0, None, ALU.add).then_inc(d.mark("s1p"), 1)
                        need("s1p")
                        v.reciprocal(K(10), K(11)).then_inc(d.mark("srec"), 1)
                        need("srec")
                        score = K(10)
                    else:
                        need("arg")
                        dve.wait_ge(a.sem, a.value(c, "gexp"))
                        score = K(12)
                    tt(K(13), score, K(9), ALU.mult).then_inc(d.mark("ms"), 1)
                    need("ms")
                    red(col(4), K(13), AX, ALU.add).then_inc(d.mark("sum"), 1)
                    need("sum")
                    v.tensor_scalar(col(5), col(4), 1e-10 if layer == 0 else 0.0, None, ALU.add)\
                        .then_inc(d.mark("sume"), 1)
                    need("sume")
                    v.reciprocal(col(6), col(5)).then_inc(d.mark("rec"), 1)
                    need("rec")
                    tt(K(14), K(13), wide(6), ALU.mult).then_inc(d.mark("w"), 1)
                if part == "split":
                    need("w")
                    v.tensor_copy(wbf[:, 0, :, 0:e], K(14)).then_inc(d.mark("wh"), 1)
                    need("wh")
                    v.tensor_copy(ws[:, :, 0:e], wbf[:, 0, :, 0:e]).then_inc(d.mark("whf"), 1)
                    need("whf")
                    tt(K(15), K(14), ws[:, :, 0:e], ALU.subtract).then_inc(d.mark("wr"), 1)
                    need("wr")
                    v.tensor_copy(wbf[:, 1, :, 0:e], K(15)).then_inc(d.mark("wm"), 1)
                    need("wm")
                    v.tensor_copy(ws[:, :, e:2 * e], wbf[:, 1, :, 0:e]).then_inc(d.mark("wmf"), 1)
                    need("wmf")
                    tt(ws[:, :, 2 * e:3 * e], K(15), ws[:, :, e:2 * e], ALU.subtract).then_inc(d.mark("wl"), 1)
                if part == "spread":
                    dve.wait_ge(p.sem, p.value(c, "back"))
                    v.tensor_copy(GF[0:3 * e, half(c)], PS[0:3 * e, B_BANK, :]).then_inc(d.mark("gf"), 1)
                    v.tensor_copy(GB[0:3 * e, half(c)], PS[0:3 * e, B_BANK, :]).then_inc(d.mark("gb"), 1)

            def ffn(s, layer):
                J, NG = JOBS[layer], GATED[layer]
                NV = NG if layer < 3 else J
                if s == 0 or STAGES[s - 1][0] == "mix" and not after_mixed(s):
                    for part in pro_parts(layer):
                        prologue(s, 0, part)

                def body(c, pro, mix):
                    slots = side_parts(layer, pro, mix)

                    def side(i):
                        for what, part in slots[i]:
                            if what == "mix":
                                mixer(*mix, part)
                            elif pro is not None:
                                prologue(*pro, part)

                    n0 = c * J + job0[s]
                    v0 = c * NV + vjob0[s]
                    ge = GATE_EVERY.get(layer, 1)
                    gate_n = c * (NG // ge) + gate0[s]
                    for j in range(J):
                        dst = hid[:, j % HID, :]
                        hid_free = n0 + (j - behind(j, J, HID) + 1 + CREDIT)
                        u, g = PS[:, U_BANK + j % 2, :], actb[:, j % 2, :]
                        side(3 * j)
                        dve.wait_ge(act_done, n0 + (j + 1 + CREDIT))
                        dve.wait_ge(u_ready, n0 + (j + 1))
                        vj = vb2[:, j % 2, :]
                        dve.wait_ge(hid_ready, n0 + (j - behind(j, J, 2) + 1 + CREDIT))
                        if layer == 3:
                            v.tensor_scalar(vj, u, 0.0, smallc("f3_val", 1), ALU.max, ALU.mult).then_inc(v_ready, 1)
                            side(3 * j + 1)
                            dve.wait_ge(v_ready, v0 + (j + 1))
                            dve.wait_ge(y_added, hid_free)
                            v.scalar_tensor_tensor(out=dst, in0=g, scalar=smallc("f3_val", 0), in1=vj,
                                                   op0=ALU.mult, op1=ALU.add).then_inc(hid_ready, 1)
                        else:
                            gated = j < NG
                            if not gated:
                                dve.wait_ge(y_added, hid_free)
                            res = vj if gated else dst
                            if layer < 2:
                                ins = v.scalar_tensor_tensor(out=res, in0=u, scalar=smallc(f"bu{layer}", j), in1=g,
                                                             op0=ALU.add, op1=ALU.mult)
                            else:
                                ins = v.tensor_tensor(res, u, g, ALU.mult)
                            ins.then_inc(v_ready if gated else hid_ready, 1)
                            side(3 * j + 1)
                            if gated:
                                dve.wait_ge(v_ready, v0 + (j + 1))
                                if layer == 1:
                                    dve.wait_ge(gate_copied, copied(s, c, j // ge))
                                else:
                                    dve.wait_ge(gate_ready, gate_n + (j // ge + 1))
                                dve.wait_ge(y_added, hid_free)
                                gate = GATES[j // ge % 2] if layer == 1 else PS[:, GATE_BANK, :]
                                v.tensor_tensor(dst, gate, vj, ALU.mult).then_inc(hid_ready, 1)
                        side(3 * j + 2)
                    if layer < 2:
                        dve.wait_ge(y_final, c + (ffn_i[s] * B + 1))
                    else:
                        dve.wait_ge(y_added, n0 + (J + CREDIT))
                    bias = sv[:, 50 + layer:51 + layer] if layer < 2 else 0.0
                    v.tensor_scalar(fin[:, :], PS[:, Y_BANK, :], 0.5, bias, ALU.mult, ALU.add).then_inc(fin_ready, 1)
                    dve.wait_ge(fin_ready, c + (ffn_i[s] * B + 2))
                    v.tensor_tensor(X[:, chunk(c)], X[:, chunk(c)], fin[:, :], ALU.add).then_inc(x_ready, 1)

                stage_loop(dve, s, layer, body)

            def tools(c, steps):
                p, a, d = steps

                def need(name):
                    dve.wait_ge(d.sem, d.value(c, name))

                def tt(name, out, i0, i1, op):
                    v.tensor_tensor(out, i0, i1, op).then_inc(d.mark(name), 1)

                def ts(name, out, i0, s1, s2, o0, o1=None):
                    if o1 is None:
                        v.tensor_scalar(out, i0, s1, None, o0).then_inc(d.mark(name), 1)
                    else:
                        v.tensor_scalar(out, i0, s1, s2, o0, o1).then_inc(d.mark(name), 1)

                def stt(name, out, i0, sc, i1, o0, o1):
                    v.scalar_tensor_tensor(out=out, in0=i0, scalar=sc, in1=i1, op0=o0, op1=o1).then_inc(d.mark(name), 1)

                return need, tt, ts, stt

            def add_to_x(c, term):
                v.tensor_tensor(X[:, chunk(c)], term, X[:, chunk(c)], ALU.add).then_inc(x_ready, 1)

            def front0(c, part, odd):
                p, a, d = mixes[0]
                need, tt, ts, stt = tools(c, mixes[0])
                conv, xs, dt, dx = TF, pair(0, 4, odd), pair(0, 0, odd), pair(0, 2, odd)
                bp = bparts[:, odd, :]
                cw = [smallc("a0_cw", i) for i in range(3)]
                if part == "norm":
                    normed(mixes[0], c, hs[:, :], 0, N_BANK)
                if part == "conv":
                    dve.wait_ge(a.sem, a.value(c, "xcp"))
                    ts("c0", conv, M0["XC"][:, 0:T], cw[0], None, ALU.mult)
                    for i in (1, 2):
                        need(f"c{i - 1}")
                        stt(f"c{i}", conv, M0["XC"][:, i:T + i], cw[i], conv, ALU.mult, ALU.add)
                if part == "split1":
                    dve.wait_ge(a.sem, a.value(c, "xds"))
                    v.tensor_copy(bp, M0["xd"]).then_inc(d.mark("bh"), 1)
                    need("bh")
                    tt("br", dx, M0["xd"], bp, ALU.subtract)
                    need("br")
                    v.tensor_copy(bparts[:, 2, :], dx).then_inc(d.mark("bm"), 1)
                if part == "split2":
                    need("bm")
                    v.tensor_copy(bp[32:64, :], bparts[32:64, 2, :]).then_inc(d.mark("bt"), 1)
                    tt("bl", bp[64:96, :], dx[64:96, :], bparts[64:96, 2, :], ALU.subtract)
                if part == "dt":
                    dve.wait_ge(a.sem, a.value(c, "lv"))
                    stt("dt0", conv, M0["v"], 0.0, M0["av"], ALU.max, ALU.add)
                    need("dt0")
                    ts("dt", dt, conv, 1e-5, None, ALU.add)
                    need("dt")
                    tt("dx", dx, dt, xs, ALU.mult)

            def back0(c, part, odd):
                p, a, d = backs[0]
                fd = mixes[0][2]
                need, tt, ts, stt = tools(c, backs[0])
                if part.startswith("state"):
                    n = int(part[5:])
                    dve.wait_ge(p.sem, p.value(c, f"bp{n}"))
                    if n == 0:
                        dve.wait_ge(fd.sem, fd.value(c, "dx"))
                    tt(f"bx{n}", BX[n % 2], PS[:, S_BANK + n % S_BANKS, :], pair(0, 2, odd), ALU.mult)
                    dve.wait_ge(a.sem, a.value(c, f"Ad{n}"))
                    need(f"bx{n}")
                    if n >= 4:
                        dve.wait_ge(sums.sem, sums.value(c, f"sum{max(n - 4, 1)}"))
                    v.tensor_tensor_scan(STATES[n % 4], EXPS[n % 8], BX[n % 2], 0.0, ALU.mult, ALU.add)\
                        .then_inc(d.mark(f"s{n}"), 1)
                if part == "y":
                    dve.wait_ge(sums.sem, sums.value(c, f"sum{NS - 1}"))
                    tt("cs", TB, M0["total"], pair(0, 8, odd), ALU.mult)
                    need("cs")
                    stt("y", Y0, pair(0, 4, odd), smallc("a0_d"), TB, ALU.mult, ALU.add)
                if part == "add":
                    dve.wait_ge(p.sem, p.value(c, "out"))
                    tt("o", TB, PS[:, R_BANK, :], pair(0, 6, odd), ALU.mult)
                    need("o")
                    add_to_x(c, TB)

            def mix1(c, part):
                p, a, d = mixes[1]
                need, tt, ts, stt = tools(c, mixes[1])
                xv, sg, pt, pwp, t = M1T["xv"], M1T["sg"], M1T["p"], M1T["pwp"], M1T["t"]
                phi, k = M1T["phi"], M1T["k"]

                def conv(z, dst, taps):
                    zp = M1T["Z" + z.upper()]
                    if taps == 0:
                        dve.wait_ge(a.sem, a.value(c, f"z{z}p"))
                        ts(f"{z}0", dst, zp[:, 0:T], smallc(f"a1_cw{z}", 0), smallc(f"a1_cb{z}"), ALU.mult, ALU.add)
                    for i in ((1,), (2, 3))[taps]:
                        need(f"{z}{i - 1}")
                        stt(f"{z}{i}", dst, zp[:, i:T + i], smallc(f"a1_cw{z}", i), dst, ALU.mult, ALU.add)

                if part.startswith("conv"):
                    conv(part[-2], {"v": xv, "g": sg, "s": pt}[part[-2]], int(part[-1]))
                if part == "clip":
                    need("s3")
                    ts("cl0", pt, pt, smallc("a1_score"), 20.0, ALU.mult, ALU.min)
                    need("cl0")
                    ts("cl1", pt, pt, -20.0, None, ALU.max)
                if part == "pw":
                    dve.wait_ge(a.sem, a.value(c, "p"))
                    tt("pw", M1T["pw"], pt, small("time"), ALU.mult)
                    ts("a", t, xv, sv[:, 40:41], sv[:, 37:38], ALU.mult, ALU.add)
                    need("a")
                    tt("m", t, t, xv, ALU.mult)
                if part == "den":
                    need("m")
                    stt("pwp", pwp, t, sv[:, 36:37], M1T["pw"], ALU.add, ALU.mult)
                    v.tensor_tensor_scan(M1T["den"], ones[:, :], M1T["pw"], 0.0, ALU.mult, ALU.add)\
                        .then_inc(d.mark("den"), 1)
                if part[:-1] in ("phi", "range", "re", "im"):
                    m = int(part[-1])
                    if part[:-1] == "phi":
                        ts(f"phi{m}", phi, xv, smallc("a1_theta", m), None, ALU.mult)
                        need(f"phi{m}")
                        ts(f"q{m}", k, phi, INV_2PI, ROUND, ALU.mult, ALU.add)
                        need(f"q{m}")
                        ts(f"k{m}", k, k, ROUND, None, ALU.subtract)
                    if part[:-1] == "range":
                        need(f"k{m}")
                        stt(f"r1_{m}", phi, k, -TWO_PI_HI, phi, ALU.mult, ALU.add)
                        need(f"r1_{m}")
                        stt(f"r2_{m}", phi, k, -TWO_PI_LO, phi, ALU.mult, ALU.add)
                        need(f"r2_{m}")
                        ts(f"r{m}", M1T["r"], phi, PI_IN, -PI_IN, ALU.min, ALU.max)
                    for z, turn in (("re", "cos"), ("im", "sin")):
                        if part[:-1] == z:
                            dve.wait_ge(a.sem, a.value(c, f"cos{m}"))
                            tt(f"{z}{m}", M1T[z], pwp, M1T[turn], ALU.mult)
                            need(f"{z}{m}")
                            if m:
                                dve.wait_ge(p.sem, p.value(c, f"y{z}{m - 1}"))
                            v.tensor_tensor_scan(M1T[f"n{z}"], ones[:, :], M1T[z], 0.0, ALU.mult, ALU.add)\
                                .then_inc(d.mark(f"n{z}{m}"), 1)
                if part == "inv":
                    ts("dmax", M1T["inv2"], M1T["den"], 1e-4, None, ALU.max)
                    need("dmax")
                    v.reciprocal(M1T["inv"], M1T["inv2"]).then_inc(d.mark("inv"), 1)
                    need("inv")
                    tt("i2", M1T["inv2"], M1T["inv"], M1T["inv"], ALU.mult)
                if part == "t":
                    need("i2")
                    dve.wait_ge(p.sem, p.value(c, f"qim{M1 - 1}"))
                    tt("t", t, PS[:, B_BANK, :], M1T["inv2"], ALU.mult)
                if part == "f":
                    dve.wait_ge(a.sem, a.value(c, "rs"))
                    tt("f", M1T["f"], t, M1T["inv"], ALU.mult)
                    need("f")
                    tt("f2", M1T["f"], M1T["f"], sg, ALU.mult)
                    need("f2")
                    tt("yy", t, PS[:, A_BANK, :], M1T["f"], ALU.mult)
                if part == "add":
                    dve.wait_ge(p.sem, p.value(c, "out"))
                    add_to_x(c, PS[:, A_BANK, :])

            def mix2(c, part):
                p, a, d = mixes[2]
                if part == "add":
                    dve.wait_ge(p.sem, p.value(c, "out"))
                    add_to_x(c, PS[:, A_BANK, :])

            def shifted(steps, c, n, h, t, bank, rs):
                p, a, d = steps
                need, tt, ts, stt = tools(c, steps)
                dve.wait_ge(a.sem, a.value(c, f"rstd{n}"))
                tt(f"n{n}", t, PS[:, bank, :], rs, ALU.mult)
                need(f"n{n}")
                ts(f"h{n}", h[:, 1:T + 1], t, smallc(f"a3_g{n}"), smallc(f"a3_b{n}"), ALU.mult, ALU.add)
                need(f"h{n}")
                tt(f"d{n}", t, h[:, 1:T + 1], h[:, 0:T], ALU.subtract)

            def front3(c, part, odd):
                p, a, d = mixes[3]
                need, tt, ts, stt = tools(c, mixes[3])
                h, t = M3["H"], M3["t"]
                if part == "norm":
                    normed(mixes[3], c, pair(3, 13, odd), 0, N_BANK)
                if part == "shift1":
                    shifted(mixes[3], c, 1, h, t, N_BANK, sq[:, :])
                if part == "mix1":
                    need("d1")
                    for z in "kvr":
                        stt(f"x{z}", M3[z], t, smallc(f"a3_m{z}"), h[:, 0:T], ALU.mult, ALU.add)

            def middle3(c, part, odd):
                p, a, d = middles
                fa = mixes[3][1]
                need, tt, ts, stt = tools(c, middles)
                mx, pp, t, S = M3["MX"], M3["PP"], M3["t1"], M3["S"][:, 0:T]
                K, V = pair(3, 7, odd), pair(3, 9, odd)
                al, be, bv, aw, nw = (M3[n] for n in ("al", "be", "bv", "aw", "nw"))

                if part == "max":
                    dve.wait_ge(fa.sem, fa.value(c, "ks"))
                    v.tensor_tensor_scan(mx[:, 1:T + 1], ones[:, :], K, NEG_HUGE, ALU.mult, ALU.max)\
                        .then_inc(d.mark("cm"), 1)
                    need("cm")
                    tt("da", AB[:, 0, :], mx[:, 0:T], mx[:, 1:T + 1], ALU.subtract)
                    tt("db", AB[:, 1, :], K, mx[:, 1:T + 1], ALU.subtract)
                if part == "S":
                    dve.wait_ge(a.sem, a.value(c, "ab"))
                    v.tensor_tensor_scan(S, AB[:, 0, :], AB[:, 1, :], 0.0, ALU.mult, ALU.add).then_inc(d.mark("S"), 1)
                if part == "pp":
                    dve.wait_ge(a.sem, a.value(c, "lnS"))
                    tt("pp", pp[:, 1:T + 1], mx[:, 1:T + 1], M3["ls"], ALU.add)
                    need("pp")
                    tt("dl", t, pp[:, 0:T], K, ALU.subtract)
                    need("dl")
                    ts("al", al, t, 0.0, None, ALU.min)
                    ts("nb", be, t, -1.0, 0.0, ALU.mult, ALU.min)
                if part == "aa":
                    dve.wait_ge(a.sem, a.value(c, "eb"))
                    tt("bv", bv, be, V, ALU.mult)
                    need("bv")
                    v.tensor_tensor_scan(AA[:, 1:T + 1], al, bv, 0.0, ALU.mult, ALU.add).then_inc(d.mark("aa"), 1)
                if part == "w":
                    stt("dw", t, K, smallc("a3_first"), pp[:, 0:T], ALU.add, ALU.subtract)
                    need("dw")
                    ts("aw", aw, t, -1.0, 0.0, ALU.mult, ALU.min)
                    ts("nw", nw, t, 0.0, None, ALU.min)
                if part == "num":
                    dve.wait_ge(a.sem, a.value(c, "e2"))
                    need("aa")
                    tt("n0", bv, aw, AA[:, 0:T], ALU.mult)
                    tt("n1b", be, nw, V, ALU.mult)
                    need("n1b")
                    tt("num", bv, bv, be, ALU.add)
                if part == "den":
                    tt("den", aw, aw, nw, ALU.add)
                    need("den")
                    ts("deni", aw, aw, 1e-8, None, ALU.add)
                    need("deni")
                    v.reciprocal(nw, aw).then_inc(d.mark("rden"), 1)
                if part == "o":
                    need("rden")
                    tt("o", bv, bv, nw, ALU.mult)
                    need("o")
                    dve.wait_ge(fa.sem, fa.value(c, "sr"))
                    tt("ro", bv, bv, pair(3, 11, odd), ALU.mult)
                    need("ro")
                    tt("x1", pair(3, 5, odd), bv, pair(3, 13, odd), ALU.add)

            def back3(c, part, odd):
                p, a, d = backs[3]
                need, tt, ts, stt = tools(c, backs[3])
                h, t = H2, M3["t2"]
                if part == "shift2":
                    shifted(backs[3], c, 2, h, t, S_BANK, M3["sq2"])
                if part == "mix2":
                    need("d2")
                    for z in ("kc", "rc"):
                        stt(f"x{z}", M3[z], t, smallc(f"a3_cm{z[0]}"), h[:, 0:T], ALU.mult, ALU.add)
                if part == "add":
                    dve.wait_ge(p.sem, p.value(c, "vc"))
                    dve.wait_ge(a.sem, a.value(c, "src"))
                    tt("res", t, PS[:, S_BANK, :], M3["rcs"], ALU.mult)
                    need("res")
                    tt("acc", t, t, pair(3, 5, odd), ALU.add)
                    need("acc")
                    add_to_x(c, t)

            def mixer(s, c, part):
                layer = STAGES[s][1]
                if part == "norm":
                    normed(mixes[layer], c, hs[:, :], 0)
                (mix1 if layer == 1 else mix2)(c, part)

            for i, val in enumerate((LN_EPS, 1e-8, HALF_PI, 1.0)):
                v.memset(epsc[:, i:i + 1], val).then_inc(consts, 1)
            v.memset(ones[:, :], 1.0).then_inc(consts, 1)
            v.memset(AA[:, :], 0.0)
            v.memset(GB[:, :], 0.0)
            v.memset(ws[:, :, :], 0.0).then_inc(consts, 1)
            dve.sem_inc(hid_ready, CREDIT)
            dve.sem_inc(y_added, CREDIT)
            dve.sem_inc(fin_ready, 1)
            dve.sem_inc(x_ready, X0)
            dve.sem_inc(backs[0][2].sem, 1)
            dve.sem_inc(backs[3][2].sem, 1)
            dve.wait_ge(consts, 6)
            dve.wait_ge(s_small, 48)
            p, a, d = prep

            def need(name):
                dve.wait_ge(d.sem, d.value(0, name))

            dve.wait_ge(a.sem, a.value(0, "sl_l"))
            v.tensor_scalar(sv[:, 0:NS], sv[:, 0:NS], -1.0, None, ALU.mult).then_inc(d.mark("naexp"), 1)
            v.tensor_scalar(sv[:, 23:24], smallc("a1_slope"), 0.0, None, ALU.max).then_inc(d.mark("sl_n"), 1)
            need("sl_n")
            v.tensor_tensor(sv[:, 25:26], sv[:, 23:24], sv[:, 22:23], ALU.add).then_inc(d.mark("sl_s"), 1)
            need("sl_s")
            v.tensor_scalar(sv[:, 24:25], sv[:, 25:26], -1.0, None, ALU.mult).then_inc(d.mark("sl_neg"), 1)
            v.tensor_reduce(sv[:, 26:27], small("a1_deriv"), AX, ALU.max).then_inc(d.mark("dm"), 1)
            need("dm")
            v.tensor_scalar(sv[:, 28:31], small("a1_deriv"), sv[:, 26:27], None, ALU.subtract).then_inc(d.mark("dd"), 1)
            dve.wait_ge(a.sem, a.value(0, "de"))
            v.tensor_reduce(sv[:, 34:35], sv[:, 31:34], AX, ALU.add).then_inc(d.mark("dsum"), 1)
            need("dsum")
            v.reciprocal(sv[:, 35:36], sv[:, 34:35]).then_inc(d.mark("drec"), 1)
            need("drec")
            v.tensor_scalar(sv[:, 36:39], sv[:, 31:34], sv[:, 35:36], None, ALU.mult).then_inc(d.mark("dw"), 1)
            need("dw")
            v.tensor_scalar(sv[:, 40:41], sv[:, 38:39], -1.0, None, ALU.mult).then_inc(d.mark("ndw2"), 1)
            for part, gain in (("re", "a1_nre"), ("im", "a1_nim")):
                for m in range(M1):
                    w = small(f"a1_{part}")[:, m * P:(m + 1) * P]
                    last = v.tensor_scalar(w, w, smallc(gain, m), None, ALU.mult)
            last.then_inc(d.mark("blk"), 1)
            v.tensor_copy(sv[:, 42:44], idxi[:, :]).then_inc(d.mark("idxf"), 1)
            need("idxf")
            for k in range(K3):
                v.tensor_tensor(sv[:, 44 + k:45 + k], sv[:, 42 + k:43 + k], smallc("f3_expert"), ALU.is_equal)\
                    .then_inc(d.mark(f"oh{k}"), 1)

            def prep_l3():
                dve.wait_ge(s_w3, 16)
                need("oh1")
                for k in range(K3):
                    v.tensor_scalar(w3(f"weff{k}", F3), w3("B", F3), sv[:, 44 + k:45 + k], None, ALU.mult)\
                        .then_inc(d.mark(f"ba{k}"), 1)
                for k in range(K3):
                    dve.wait_ge(prep[0].sem, prep[0].value(0, f"weff{k}"))
                    v.tensor_tensor(w3(f"weff{k}", F3), PS[:, A_BANK + k, :], w3("wi", F3), ALU.add)\
                        .then_inc(d.mark(f"wi{k}"), 1)

            for i in range(2):
                v.tensor_scalar(sv[:, 50 + i:51 + i], smallc(f"by{i}"), 0.5, None, ALU.mult).then_inc(consts, 1)
            dve.wait_ge(consts, 8)
            for s, (kind, layer) in enumerate(STAGES[:stop_after]):
                if s == 9:
                    prep_l3()
                if s == 0:
                    v.memset(M0["XC"][:, 0:1], 0.0)
                    v.memset(M0["XC"][:, T + 1:T + 2], 0.0).then_inc(consts, 1)
                    dve.wait_ge(consts, 9)
                if s == 3:
                    for z in ("ZV", "ZG", "ZS"):
                        last = v.memset(M1T[z][:, 0:3], 0.0)
                    last.then_inc(consts, 1)
                    dve.wait_ge(consts, 10)
                if s == 9:
                    v.memset(M3["H"][:, 0:1], 0.0)
                    v.memset(H2[:, 0:1], 0.0)
                    v.memset(M3["MX"][:, 0:1], NEG_HUGE)
                    v.memset(M3["PP"][:, 0:1], NEG_HUGE)
                    v.memset(AA[:, 0:1], 0.0).then_inc(consts, 1)
                    dve.wait_ge(consts, 11)
                if s == 6:
                    for i in range(W2_PIECES):
                        dve.wait_ge(w2_high, i + 1)
                        v.tensor_tensor(W2L[:, i * T:(i + 1) * T], WB[:, i * T:(i + 1) * T],
                                        W2H[:, i * T:(i + 1) * T].bitcast(F32), ALU.subtract).then_inc(w2_low, 1)
                if kind == "ffn":
                    ffn(s, layer)
                elif layer in FRONT:
                    mix_stage(dve, layer, *((front0, back0) if layer == 0 else (front3, back3, middle3)))


_OUTS = [((8, 512, 128), "float32")]


def kernel(**inputs):
    import numpy as np
    import concourse.bacc as _bacc
    from concourse import mybir as _mybir
    from concourse.bass_utils import run_bass_kernel_spmd as _run

    f32 = np.float32
    get = {k: np.asarray(v) for k, v in inputs.items()}

    def T_(a):
        return np.ascontiguousarray(a.T)

    def wide(a, cols=P):
        out = np.zeros((P, cols), f32)
        out[:a.shape[0], :a.shape[1]] = a
        return out

    sm = {}
    eye = np.eye(P, dtype=f32)
    sm["center"] = eye - f32(1.0 / P)
    sm["avg"] = np.full((P, P), 1.0 / P, f32)
    sm["ident"] = eye
    w_in, w_x = get["L0_attn_W_in"], get["L0_attn_W_x"]
    sm["a0_xc"], sm["a0_z"] = w_in[:P].T, w_in[P:].T
    dt_rows = (np.arange(R0) // NS) * 32 + NS + np.arange(R0) % NS
    sm["a0_xd"], sm["a0_dt"], sm["a0_c"] = (np.zeros((P, P), f32) for _ in range(3))
    sm["a0_xd"][:, dt_rows] = w_x[:R0].T
    for at in (0, 32, 64):
        sm["a0_xd"][:, at:at + NS] = w_x[R0:R0 + NS].T
    sm["a0_xd"][:, 96:96 + NS] = w_x[R0 + NS:].T
    sm["a0_dt"][dt_rows] = get["L0_attn_W_dt"].T
    sm["a0_c"][96:96 + NS] = get["L0_attn_W_C"].T
    sm["a0_out"] = get["L0_attn_W_out"].T
    w_p = get["L1_attn_in_proj_w"]
    sm["a1_v"], sm["a1_g"] = w_p[:, :P], w_p[:, P:2 * P]
    sm["a1_s"] = np.repeat(w_p[:, 2 * P:], H1, axis=1)
    for name, src in (("a1_re", "L1_attn_W_re"), ("a1_im", "L1_attn_W_im")):
        w = get[src].reshape(H1, M1, H1)
        blocks = np.zeros((M1, P, P), f32)
        for m in range(M1):
            for k in range(K1):
                blocks[m, H1 * k:H1 * k + H1, H1 * k:H1 * k + H1] = w[:, m, :]
        sm[name] = blocks.transpose(1, 0, 2).reshape(P, M1 * P)
    sm["a1_sum"] = np.kron(np.eye(K1, dtype=f32), np.ones((H1, H1), f32))
    sm["a1_out"] = get["L1_attn_out_proj_w"]
    t = np.arange(T, dtype=f32)
    sm["time"] = np.where(np.arange(P)[:, None] < (K1 - A1) * H1, (T - 1 - t)[None, :], t[None, :]).astype(f32)
    sm["a2_kv"] = np.concatenate([get["L2_attn_wv"].T, get["L2_attn_wk"].T], axis=1)
    sm["a2_q"] = np.concatenate([np.zeros((P - D2, P), f32), get["L2_attn_wq"]])
    sm["a2_o"] = wide(get["L2_attn_wo"].T)
    g0 = get["L0_ffn_gate_w"].T
    sm["gate0"] = np.concatenate([g0, g0], axis=1)
    sm["gate1"], sm["gate2"] = get["L1_ffn_Wr"], get["L2_ffn_gate_w"]
    sm["b2_0"] = wide(np.concatenate([get["L0_ffn_b2"]] * 3))
    sm["b2_1"] = wide(np.concatenate([get["L1_ffn_be2"]] * 3))
    sm["rank"] = np.broadcast_to(np.arange(E0, 0, -1, dtype=f32), (P, E0))

    def col(a):
        a = a.reshape(-1, 1)
        return wide(a, 1)

    be1, bs1 = get["L1_ffn_be1"], get["L1_ffn_bs1"]
    sm["bg0"] = np.concatenate([get["L0_ffn_b1"].reshape(-1), get["L0_ffn_sb1"]]).reshape(-1, P).T
    sm["bu0"] = np.concatenate([get["L0_ffn_b3"].reshape(-1), get["L0_ffn_sb3"]]).reshape(-1, P).T
    sm["bg1"] = np.concatenate([be1[:, F1:].reshape(-1), bs1[SH1:]]).reshape(-1, P).T
    sm["bu1"] = np.concatenate([be1[:, :F1].reshape(-1), bs1[:SH1]]).reshape(-1, P).T
    sm["by0"], sm["by1"] = col(get["L0_ffn_sb2"]), col(get["L1_ffn_bs2"])
    sm["gb0"] = col(np.concatenate([get["L0_ffn_expert_bias"], np.zeros(E0, f32)]))
    sm["gb1"] = col(get["L1_ffn_br"])
    sm["a0_cw"] = get["L0_attn_conv_w"]
    sm["a0_bdt"], sm["a0_alog"], sm["a0_d"] = col(get["L0_attn_b_dt"]), get["L0_attn_A_log"], col(get["L0_attn_D_param"])
    cw, cb = get["L1_attn_conv_w"][:, 0, :].T, get["L1_attn_conv_b"]
    sm["a1_cwv"], sm["a1_cwg"], sm["a1_cws"] = cw[:P], cw[P:2 * P], np.repeat(cw[2 * P:], H1, axis=0)
    sm["a1_cbv"], sm["a1_cbg"], sm["a1_cbs"] = col(cb[:P]), col(cb[P:2 * P]), col(np.repeat(cb[2 * P:], H1))
    sm["a1_theta"] = get["L1_attn_theta"].reshape(P, M1)
    sm["a1_slope"] = col(np.repeat(np.concatenate([get["L1_attn_decay_slopes"], get["L1_attn_anchor_slopes"]]), H1))
    sm["a1_score"] = col(np.repeat(get["L1_attn_score_scale"], H1))
    sm["a1_deriv"] = np.broadcast_to(get["L1_attn_deriv_logits"], (P, 3))
    ns = get["L1_attn_norm_scale"].reshape(2, H1, M1)
    sm["a1_nre"], sm["a1_nim"] = np.tile(ns[0], (K1, 1)), np.tile(ns[1], (K1, 1))
    for name, src in (("first", "time_first"), ("g1", "ln1_g"), ("b1", "ln1_b"), ("g2", "ln2_g"), ("b2", "ln2_b"),
                      ("mk", "mix_k"), ("mv", "mix_v"), ("mr", "mix_r"), ("cmk", "cmix_k"), ("cmr", "cmix_r")):
        sm[f"a3_{name}"] = col(get[f"L3_attn_{src}"])
    sm["f3_val"] = np.broadcast_to(get["L3_ffn_top_k_values"], (P, K3))
    sm["f3_expert"] = col(np.repeat(np.arange(E3, dtype=f32), R3))
    small = np.concatenate([sm[name].reshape(P, n) for name, n in SMALL], axis=1)

    def rows(a):
        return a.reshape(-1, P, D).transpose(1, 0, 2).reshape(P, -1)

    def pad(a, n):
        return np.concatenate([a, np.zeros((n - a.shape[0],) + a.shape[1:], f32)])

    w0 = np.concatenate([
        np.concatenate([get["L0_ffn_w1"].reshape(-1, D), get["L0_ffn_sw1"]]).T,
        np.concatenate([get["L0_ffn_w3"].reshape(-1, D), get["L0_ffn_sw3"]]).T,
        rows(np.concatenate([get["L0_ffn_w2"].transpose(0, 2, 1).reshape(-1, D), get["L0_ffn_sw2"].T]))], axis=1)
    we1, ws1 = get["L1_ffn_We1"], get["L1_ffn_Ws1"]
    w1 = np.concatenate([
        we1[:, :, F1:].transpose(1, 0, 2).reshape(D, -1), ws1[:, SH1:],
        we1[:, :, :F1].transpose(1, 0, 2).reshape(D, -1), ws1[:, :SH1],
        rows(np.concatenate([get["L1_ffn_We2"].reshape(-1, D), get["L1_ffn_Ws2"]]))], axis=1)
    w2 = np.concatenate([
        get["L2_ffn_Wg"].transpose(1, 0, 2).reshape(D, -1), wide(get["L2_ffn_Sg"], 2 * P),
        get["L2_ffn_Wu"].transpose(1, 0, 2).reshape(D, -1), wide(get["L2_ffn_Su"], 2 * P),
        rows(np.concatenate([get["L2_ffn_Wd"].reshape(-1, D), pad(get["L2_ffn_Sd"], 2 * P)]))], axis=1)
    w3 = np.concatenate([
        get["L3_ffn_wi_w"].T, rows(get["L3_ffn_wo_w"].T), wide(get["L3_ffn_lora_As"].reshape(-1, D), F3),
        get["L3_ffn_lora_Bs"].transpose(0, 2, 1).reshape(P, F3),
        get["L3_attn_Wk_t"].T, get["L3_attn_Wv_t"].T, get["L3_attn_Wr_t"].T, get["L3_attn_Wr_c"].T,
        get["L3_attn_Wk_c"].T, rows(get["L3_attn_Wv_c"].T)], axis=1)

    def spread(experts, owner):
        one = (np.arange(experts)[:, None] == owner[None, :]).astype(f32)
        return np.concatenate([one, one, one, np.zeros((P - 3 * experts, owner.size), f32)])

    rows_of_b = np.zeros((P, NS, P), f32)
    for at in (0, 32, 64):
        rows_of_b[at + np.arange(NS), np.arange(NS)] = 1.0
    rows_of_b = rows_of_b.reshape(P, NS * P)
    sel = np.concatenate([
        spread(E0, np.arange(E0 * F0) // F0),
        spread(E1, np.repeat(np.arange(E1), P)),
        spread(E2, np.arange(E2 * F2) // F2), rows_of_b], axis=1).astype(np.dtype("bfloat16"))
    idx = np.ascontiguousarray(np.broadcast_to(get["L3_ffn_top_k_indices"], (P, K3)))
    x = np.ascontiguousarray(get["L0_attn_x"].reshape(N, D).T)

    arrays = {"in_x": x, "in_small": small, "in_w0": w0, "in_w1": w1, "in_w2": w2, "in_w3": w3, "in_sel": sel,
              "in_idx": idx}
    arrays = {k: np.ascontiguousarray(v) for k, v in arrays.items()}
    nc = _bacc.Bacc("TRN2", target_bir_lowering=False, num_devices=1, dynamic_dma_scratch_size=1024)
    args = [nc.dram_tensor(k, a.shape, _mybir.dt.from_np(a.dtype), kind="ExternalInput").ap()
            for k, a in arrays.items()]
    res = nc.dram_tensor("out_0_dram", (P, N), _mybir.dt.float32, kind="ExternalOutput").ap()
    build(nc, *args, res)
    r = _run(nc, [arrays], core_ids=[0])
    return np.ascontiguousarray(r.results[0]["out_0_dram"].T).reshape(B, T, D)
```
